# Optimizing a Trainium2 kernel written in Bass

```python
import numpy as np
import jax
import jax.numpy as jnp

def _softmax(x, axis=-1):
    return jax.nn.softmax(x, axis=axis)

def _gelu(x):
    return jax.nn.gelu(x, approximate=True)

def _silu(x):
    return jax.nn.silu(x)

def _sigmoid(x):
    return jax.nn.sigmoid(x)

def _layernorm(x, axis=-1, eps=1e-05):
    m = jnp.mean(x, axis=axis, keepdims=True)
    v = jnp.var(x, axis=axis, keepdims=True)
    return (x - m) / jnp.sqrt(v + eps)

def _scatter_add(tgt, idx, src, axis=0):
    return tgt.at[idx].add(src)

def _segment_sum(src, seg, n):
    return jax.ops.segment_sum(src, seg, n)
kernel_name = 'mk_adaln_attn_ffn_d2_seqx_r8_344e35'

def setup_inputs(seed: int=0):
    np.random.seed(seed)
    _w = jnp.asarray

    def _rec_inputs():
        import jax
        import jax.numpy as jnp
        _rk = jax.random.key(seed)
        x = -0.0002928 + 1 * jax.random.normal(jax.random.fold_in(_rk, 1), (8, 128, 128), jnp.float32)
        _lenS = 128 - jax.random.randint(jax.random.fold_in(_rk, 7), (8,), 0, max(1, 128 // 4) + 1, jnp.int32)
        _lenS2 = 128 - jax.random.randint(jax.random.fold_in(_rk, 8), (8,), 0, max(1, 128 // 4) + 1, jnp.int32)
        cond_1024 = 0.0061147 + 1.02565 * jax.random.normal(jax.random.fold_in(_rk, 11), (8, 128), jnp.float32)
        return (x, cond_1024)
    x, cond_1024 = _rec_inputs()

    def _L0_cond_setup():
        import jax, jax.numpy as jnp
        import numpy as np
        D, HS, HE, E, K = (128, 256, 128, 8, 2)
        B, T = (4, 128)
        N_SHARED = 1
        key = jax.random.key(seed)
        ks = jax.random.split(key, 9)
        g = lambda k, shape, s: jax.random.normal(k, shape, jnp.float32) * s
        return {'x': g(ks[0], (B, T, D), 1.0), 't_emb': g(ks[1], (B, D), 1.0), 'router_W': g(ks[2], (2 * D, E), 0.01), 'router_bias': jnp.zeros((E,), jnp.float32), 'w1': g(ks[3], (D, HS), 0.02), 'w3': g(ks[4], (D, HS), 0.02), 'w2': g(ks[5], (HS, D), 0.02), 'W1e': g(ks[6], (E, D, HE), 0.02), 'W2e': g(ks[7], (E, HE, D), 0.02)}
    _L0_cond_all = _L0_cond_setup()
    _L0_cond_in = {k: v for k, v in _L0_cond_all.items() if k in ('router_W', 'router_bias', 'w1', 'w3', 'w2', 'W1e', 'W2e')}
    del _L0_cond_all

    def _L0_attn_setup():
        import jax, jax.numpy as jnp
        import numpy as np
        D_MODEL = 128
        D_STATE = 32
        D_CONV = 4
        EXPAND = 2
        D_INNER = EXPAND * D_MODEL
        DT_RANK = D_MODEL // 16
        BATCH = 8
        SEQ = 128

        def _silu(x):
            return x * jax.nn.sigmoid(x)

        def _layernorm(x, g, b, eps=1e-05):
            m = x.mean(-1, keepdims=True)
            v = x.var(-1, keepdims=True)
            return (x - m) / jnp.sqrt(v + eps) * g + b

        def _mamba(x, Win, convw, convb, Wx, Wdt, bdt, Alog, Dp, Wout):
            Bn, Ln, _ = x.shape
            xz = jnp.einsum('bld,ed->ble', x, Win)
            u, z = jnp.split(xz, 2, axis=-1)
            up = jnp.pad(u, ((0, 0), (D_CONV - 1, 0), (0, 0)))
            uc = convb
            for k in range(D_CONV):
                uc = uc + up[:, k:k + Ln, :] * convw[:, k]
            uc = _silu(uc)
            x_dbl = jnp.einsum('bld,ed->ble', uc, Wx)
            dt = jax.nn.softplus(jnp.einsum('blr,dr->bld', x_dbl[..., :DT_RANK], Wdt) + bdt)
            Bv = x_dbl[..., DT_RANK:DT_RANK + D_STATE]
            Cv = x_dbl[..., DT_RANK + D_STATE:]
            A = -jnp.exp(Alog)

            def step(h, ins):
                dt_t, B_t, C_t, u_t = ins
                dA = jnp.exp(dt_t[..., None] * A)
                h = dA * h + (dt_t * u_t)[..., None] * B_t[:, None, :]
                y = jnp.einsum('bdn,bn->bd', h, C_t)
                return (h, y)
            h0 = jnp.zeros((Bn, D_INNER, D_STATE), x.dtype)
            xs = (dt.transpose(1, 0, 2), Bv.transpose(1, 0, 2), Cv.transpose(1, 0, 2), uc.transpose(1, 0, 2))
            _, ys = jax.lax.scan(step, h0, xs)
            y = ys.transpose(1, 0, 2) + uc * Dp
            y = y * _silu(z)
            return jnp.einsum('bld,ed->ble', y, Wout)
        key = jax.random.key(seed)
        ks = iter(jax.random.split(key, 64))

        def rn(shape, scale):
            return jax.random.normal(next(ks), shape, jnp.float32) * scale

        def direction_params():
            return dict(Win=rn((2 * D_INNER, D_MODEL), 0.02), convw=rn((D_INNER, D_CONV), 0.1), convb=jnp.zeros((D_INNER,), jnp.float32), Wx=rn((DT_RANK + 2 * D_STATE, D_INNER), 0.02), Wdt=rn((D_INNER, DT_RANK), 0.02), bdt=rn((D_INNER,), 0.5), Alog=jnp.log(jnp.broadcast_to(jnp.arange(1, D_STATE + 1, dtype=jnp.float32), (D_INNER, D_STATE))), Dp=jnp.ones((D_INNER,), jnp.float32), Wout=rn((D_MODEL, D_INNER), 0.02), ln_g=jnp.ones((D_MODEL,), jnp.float32), ln_b=jnp.zeros((D_MODEL,), jnp.float32))
        f = direction_params()
        b = direction_params()
        inp = {'x': rn((BATCH, SEQ, D_MODEL), 1.0)}
        for k, v in f.items():
            inp[k + '_f'] = v
        for k, v in b.items():
            inp[k + '_b'] = v
        inp['Wfuse'] = rn((D_MODEL, 2 * D_MODEL), 0.02)
        inp['bfuse'] = jnp.zeros((D_MODEL,), jnp.float32)
        return inp
    _L0_attn_all = _L0_attn_setup()
    _L0_attn_in = {k: v for k, v in _L0_attn_all.items() if k in ('Win_f', 'convw_f', 'convb_f', 'Wx_f', 'Wdt_f', 'bdt_f', 'Alog_f', 'Dp_f', 'Wout_f', 'ln_g_f', 'ln_b_f', 'Win_b', 'convw_b', 'convb_b', 'Wx_b', 'Wdt_b', 'bdt_b', 'Alog_b', 'Dp_b', 'Wout_b', 'ln_g_b', 'ln_b_b', 'Wfuse', 'bfuse')}
    del _L0_attn_all

    def _L0_cond2_setup():
        import jax, jax.numpy as jnp
        import numpy as np
        N, T, D, H = (128, 64, 128, 128)
        key = jax.random.key(seed)
        k1, k2, k3, k4 = jax.random.split(key, 4)
        x = jax.random.normal(k1, (N, T, D), dtype=jnp.float32)
        h0 = jax.random.normal(k2, (N, H), dtype=jnp.float32)
        Wx = jax.random.normal(k3, (D, H), dtype=jnp.float32) / np.sqrt(D)
        Wh = jax.random.normal(k4, (H, H), dtype=jnp.float32) / np.sqrt(H)
        b = jnp.zeros((H,), dtype=jnp.float32)
        return {'x': x, 'h0': h0, 'Wx': Wx, 'Wh': Wh, 'b': b}
    _L0_cond2_all = _L0_cond2_setup()
    _L0_cond2_in = {k: v for k, v in _L0_cond2_all.items() if k in ('Wx', 'Wh', 'b')}
    del _L0_cond2_all

    def _L0_ffn_setup():
        import jax, jax.numpy as jnp
        import numpy as np
        EPS = 1e-05

        @jax.custom_vjp
        def ste_quantize(w):
            scale = jnp.maximum(jnp.mean(jnp.abs(w)), EPS)
            return jnp.clip(jnp.round(w / scale), -1.0, 1.0)

        def _ste_fwd(w):
            return (ste_quantize(w), None)

        def _ste_bwd(_, g):
            return (g,)
        ste_quantize.defvjp(_ste_fwd, _ste_bwd)
        key = jax.random.key(seed)
        k1, k2 = jax.random.split(key)
        x = jax.random.normal(k1, (8, 1024, 128), dtype=jnp.float32)
        weight = jax.random.normal(k2, (128, 128), dtype=jnp.float32) * 0.02
        return {'x': x, 'weight': weight}
    _L0_ffn_all = _L0_ffn_setup()
    _L0_ffn_in = {k: v for k, v in _L0_ffn_all.items() if k in ('weight',)}
    del _L0_ffn_all

    def _L1_cond_setup():
        import jax, jax.numpy as jnp
        import numpy as np
        import math
        N, T, D, H = (64, 64, 128, 128)

        def lstm_forward(x, h0, Wx, Wh, b):
            Hd = h0.shape[1]
            xW = jnp.einsum('ntd,dg->ntg', x, Wx) + b
            c0 = jnp.zeros_like(h0)

            def step(carry, xw_t):
                prev_h, prev_c = carry
                a = xw_t + prev_h @ Wh
                i = jax.nn.sigmoid(a[:, :Hd])
                f = jax.nn.sigmoid(a[:, Hd:2 * Hd])
                o = jax.nn.sigmoid(a[:, 2 * Hd:3 * Hd])
                g = jnp.tanh(a[:, 3 * Hd:])
                next_c = f * prev_c + i * g
                next_h = o * jnp.tanh(next_c)
                return ((next_h, next_c), next_h)
            (_, _), hs = jax.lax.scan(step, (h0, c0), jnp.swapaxes(xW, 0, 1))
            return jnp.swapaxes(hs, 0, 1)
        key = jax.random.key(seed)
        k1, k2, k3, k4 = jax.random.split(key, 4)
        x = jax.random.normal(k1, (N, T, D), dtype=jnp.float32)
        h0 = jax.random.normal(k2, (N, H), dtype=jnp.float32)
        Wx = jax.random.normal(k3, (D, 4 * H), dtype=jnp.float32) / math.sqrt(D)
        Wh = jax.random.normal(k4, (H, 4 * H), dtype=jnp.float32) / math.sqrt(H)
        b = jnp.zeros((4 * H,), dtype=jnp.float32)
        return {'x': x, 'h0': h0, 'Wx': Wx, 'Wh': Wh, 'b': b}
    _L1_cond_all = _L1_cond_setup()
    _L1_cond_in = {k: v for k, v in _L1_cond_all.items() if k in ('Wx', 'Wh', 'b')}
    del _L1_cond_all

    def _L1_attn_setup():
        import jax, jax.numpy as jnp
        import numpy as np
        B, T, D = (4, 512, 128)

        def _rmsnorm(y, w):
            return y * jax.lax.rsqrt(jnp.mean(y * y, axis=-1, keepdims=True) + 1e-06) * w
        key = jax.random.key(seed)
        ks = jax.random.split(key, 6)
        std = np.sqrt(2.0 / D).astype(np.float32)
        return {'x': jax.random.normal(ks[0], (B, T, D), dtype=jnp.float32), 'Wr': jax.random.normal(ks[1], (D, D), dtype=jnp.float32) * std, 'Wk': jax.random.normal(ks[2], (D, D), dtype=jnp.float32) * std, 'Wv': jax.random.normal(ks[3], (D, D), dtype=jnp.float32) * std, 'Wo': jax.random.normal(ks[4], (D, D), dtype=jnp.float32) * std, 'decay': jnp.ones((D,), dtype=jnp.float32) * 0.99, 'ln_w': jnp.ones((D,), dtype=jnp.float32)}
    _L1_attn_all = _L1_attn_setup()
    _L1_attn_in = {k: v for k, v in _L1_attn_all.items() if k in ('Wr', 'Wk', 'Wv', 'Wo', 'decay', 'ln_w')}
    del _L1_attn_all

    def _L1_cond2_setup():
        import jax, jax.numpy as jnp
        import numpy as np
        INV_SQRT2 = 0.7071067811865476
        key = jax.random.key(seed)
        k1, k2, k3, k4 = jax.random.split(key, 4)
        B, N, d = (8, 512, 128)
        scale = 1.0 / np.sqrt(d)
        return {'v': jax.random.normal(k1, (B, N, d), dtype=jnp.float32), 'q_pool': jax.random.normal(k2, (B, d), dtype=jnp.float32), 'W1': jax.random.normal(k3, (d, d), dtype=jnp.float32) * scale, 'b1': jnp.zeros((d,), dtype=jnp.float32), 'W2': jax.random.normal(k4, (d, d), dtype=jnp.float32) * scale, 'b2': jnp.zeros((d,), dtype=jnp.float32)}
    _L1_cond2_all = _L1_cond2_setup()
    _L1_cond2_in = {k: v for k, v in _L1_cond2_all.items() if k in ('W1', 'b1', 'W2', 'b2')}
    del _L1_cond2_all

    def _L1_ffn_setup():
        import jax, jax.numpy as jnp
        import numpy as np
        from jax import lax
        H = 128
        E = 8
        E_MLP = E - 4
        TOP_K = 2
        I = 64
        KC = 4
        SHARED_SCALE = 1.0
        key = jax.random.key(seed)
        ks = jax.random.split(key, 8)
        B, S = (4, 512)
        s_h = 1.0 / np.sqrt(H)
        s_i = 1.0 / np.sqrt(I)
        return {'hidden_states': jax.random.normal(ks[0], (B, S, H), dtype=jnp.float32), 'Wr': jax.random.normal(ks[1], (H, E), dtype=jnp.float32) * s_h, 'router_bias': jnp.zeros((E,), dtype=jnp.float32), 'Wg': jax.random.normal(ks[2], (E_MLP, H, I), dtype=jnp.float32) * s_h, 'Wu': jax.random.normal(ks[3], (E_MLP, H, I), dtype=jnp.float32) * s_h, 'Wd': jax.random.normal(ks[4], (E_MLP, I, H), dtype=jnp.float32) * s_i, 'conv_w': jax.random.normal(ks[5], (KC, 1, H), dtype=jnp.float32) * (1.0 / np.sqrt(KC)), 'conv_b': jnp.zeros((H,), dtype=jnp.float32)}
    _L1_ffn_all = _L1_ffn_setup()
    _L1_ffn_in = {k: v for k, v in _L1_ffn_all.items() if k in ('Wr', 'router_bias', 'Wg', 'Wu', 'Wd', 'conv_w', 'conv_b')}
    del _L1_ffn_all
    return {'x': x, 'cond_1024': cond_1024, 'L0_cond_router_W': _L0_cond_in['router_W'], 'L0_cond_router_bias': _L0_cond_in['router_bias'], 'L0_cond_w1': _L0_cond_in['w1'], 'L0_cond_w3': _L0_cond_in['w3'], 'L0_cond_w2': _L0_cond_in['w2'], 'L0_cond_W1e': _L0_cond_in['W1e'], 'L0_cond_W2e': _L0_cond_in['W2e'], 'L0_attn_Win_f': _L0_attn_in['Win_f'], 'L0_attn_convw_f': _L0_attn_in['convw_f'], 'L0_attn_convb_f': _L0_attn_in['convb_f'], 'L0_attn_Wx_f': _L0_attn_in['Wx_f'], 'L0_attn_Wdt_f': _L0_attn_in['Wdt_f'], 'L0_attn_bdt_f': _L0_attn_in['bdt_f'], 'L0_attn_Alog_f': _L0_attn_in['Alog_f'], 'L0_attn_Dp_f': _L0_attn_in['Dp_f'], 'L0_attn_Wout_f': _L0_attn_in['Wout_f'], 'L0_attn_ln_g_f': _L0_attn_in['ln_g_f'], 'L0_attn_ln_b_f': _L0_attn_in['ln_b_f'], 'L0_attn_Win_b': _L0_attn_in['Win_b'], 'L0_attn_convw_b': _L0_attn_in['convw_b'], 'L0_attn_convb_b': _L0_attn_in['convb_b'], 'L0_attn_Wx_b': _L0_attn_in['Wx_b'], 'L0_attn_Wdt_b': _L0_attn_in['Wdt_b'], 'L0_attn_bdt_b': _L0_attn_in['bdt_b'], 'L0_attn_Alog_b': _L0_attn_in['Alog_b'], 'L0_attn_Dp_b': _L0_attn_in['Dp_b'], 'L0_attn_Wout_b': _L0_attn_in['Wout_b'], 'L0_attn_ln_g_b': _L0_attn_in['ln_g_b'], 'L0_attn_ln_b_b': _L0_attn_in['ln_b_b'], 'L0_attn_Wfuse': _L0_attn_in['Wfuse'], 'L0_attn_bfuse': _L0_attn_in['bfuse'], 'L0_cond2_Wx': _L0_cond2_in['Wx'], 'L0_cond2_Wh': _L0_cond2_in['Wh'], 'L0_cond2_b': _L0_cond2_in['b'], 'L0_ffn_weight': _L0_ffn_in['weight'], 'L1_cond_Wx': _L1_cond_in['Wx'], 'L1_cond_Wh': _L1_cond_in['Wh'], 'L1_cond_b': _L1_cond_in['b'], 'L1_attn_Wr': _L1_attn_in['Wr'], 'L1_attn_Wk': _L1_attn_in['Wk'], 'L1_attn_Wv': _L1_attn_in['Wv'], 'L1_attn_Wo': _L1_attn_in['Wo'], 'L1_attn_decay': _L1_attn_in['decay'], 'L1_attn_ln_w': _L1_attn_in['ln_w'], 'L1_cond2_W1': _L1_cond2_in['W1'], 'L1_cond2_b1': _L1_cond2_in['b1'], 'L1_cond2_W2': _L1_cond2_in['W2'], 'L1_cond2_b2': _L1_cond2_in['b2'], 'L1_ffn_Wr': _L1_ffn_in['Wr'], 'L1_ffn_router_bias': _L1_ffn_in['router_bias'], 'L1_ffn_Wg': _L1_ffn_in['Wg'], 'L1_ffn_Wu': _L1_ffn_in['Wu'], 'L1_ffn_Wd': _L1_ffn_in['Wd'], 'L1_ffn_conv_w': _L1_ffn_in['conv_w'], 'L1_ffn_conv_b': _L1_ffn_in['conv_b']}

def reference(x, cond_1024, L0_cond_router_W, L0_cond_router_bias, L0_cond_w1, L0_cond_w3, L0_cond_w2, L0_cond_W1e, L0_cond_W2e, L0_attn_Win_f, L0_attn_convw_f, L0_attn_convb_f, L0_attn_Wx_f, L0_attn_Wdt_f, L0_attn_bdt_f, L0_attn_Alog_f, L0_attn_Dp_f, L0_attn_Wout_f, L0_attn_ln_g_f, L0_attn_ln_b_f, L0_attn_Win_b, L0_attn_convw_b, L0_attn_convb_b, L0_attn_Wx_b, L0_attn_Wdt_b, L0_attn_bdt_b, L0_attn_Alog_b, L0_attn_Dp_b, L0_attn_Wout_b, L0_attn_ln_g_b, L0_attn_ln_b_b, L0_attn_Wfuse, L0_attn_bfuse, L0_cond2_Wx, L0_cond2_Wh, L0_cond2_b, L0_ffn_weight, L1_cond_Wx, L1_cond_Wh, L1_cond_b, L1_attn_Wr, L1_attn_Wk, L1_attn_Wv, L1_attn_Wo, L1_attn_decay, L1_attn_ln_w, L1_cond2_W1, L1_cond2_b1, L1_cond2_W2, L1_cond2_b2, L1_ffn_Wr, L1_ffn_router_bias, L1_ffn_Wg, L1_ffn_Wu, L1_ffn_Wd, L1_ffn_conv_w, L1_ffn_conv_b):
    import jax
    import jax.numpy as jnp

    def _L0_cond_ref(x, t_emb, router_W, router_bias, w1, w3, w2, W1e, W2e):
        import jax, jax.numpy as jnp
        import numpy as np
        D, HS, HE, E, K = (128, 256, 128, 8, 2)
        B, T = (4, 128)
        N_SHARED = 1
        Bb, Tt, C = x.shape
        xf = x.reshape(-1, C)
        tf = jnp.broadcast_to(t_emb[:, None, :], (Bb, Tt, C)).reshape(-1, C)
        N = xf.shape[0]
        shared = jax.nn.silu(xf @ w1) * (xf @ w3) @ w2
        s = jax.nn.sigmoid((jnp.concatenate([xf, tf], axis=-1) @ router_W).astype(jnp.float32))
        sel_scores = s + router_bias
        _, topk_idx = jax.lax.top_k(sel_scores, K)
        s_sel = jnp.take_along_axis(s, topk_idx, axis=1)
        denom = s_sel.sum(axis=1, keepdims=True)
        gates = jnp.where(denom > 1e-09, s_sel / (denom + 1e-09), 1.0 / K).astype(x.dtype)
        combine = jnp.zeros((N, E), x.dtype).at[jnp.arange(N)[:, None], topk_idx].add(gates)
        h = jax.nn.gelu(jnp.einsum('nc,ech->enh', xf, W1e), approximate=False)
        y = jnp.einsum('enh,ehc->enc', h, W2e)
        routed = jnp.einsum('ne,enc->nc', combine, y)
        return ((shared + routed) / (N_SHARED + K)).reshape(Bb, Tt, C)

    def _L0_attn_ref(x, Win_f, convw_f, convb_f, Wx_f, Wdt_f, bdt_f, Alog_f, Dp_f, Wout_f, ln_g_f, ln_b_f, Win_b, convw_b, convb_b, Wx_b, Wdt_b, bdt_b, Alog_b, Dp_b, Wout_b, ln_g_b, ln_b_b, Wfuse, bfuse):
        import jax, jax.numpy as jnp
        import numpy as np
        D_MODEL = 128
        D_STATE = 32
        D_CONV = 4
        EXPAND = 2
        D_INNER = EXPAND * D_MODEL
        DT_RANK = D_MODEL // 16
        BATCH = 8
        SEQ = 128

        def _silu(x):
            return x * jax.nn.sigmoid(x)

        def _layernorm(x, g, b, eps=1e-05):
            m = x.mean(-1, keepdims=True)
            v = x.var(-1, keepdims=True)
            return (x - m) / jnp.sqrt(v + eps) * g + b

        def _mamba(x, Win, convw, convb, Wx, Wdt, bdt, Alog, Dp, Wout):
            Bn, Ln, _ = x.shape
            xz = jnp.einsum('bld,ed->ble', x, Win)
            u, z = jnp.split(xz, 2, axis=-1)
            up = jnp.pad(u, ((0, 0), (D_CONV - 1, 0), (0, 0)))
            uc = convb
            for k in range(D_CONV):
                uc = uc + up[:, k:k + Ln, :] * convw[:, k]
            uc = _silu(uc)
            x_dbl = jnp.einsum('bld,ed->ble', uc, Wx)
            dt = jax.nn.softplus(jnp.einsum('blr,dr->bld', x_dbl[..., :DT_RANK], Wdt) + bdt)
            Bv = x_dbl[..., DT_RANK:DT_RANK + D_STATE]
            Cv = x_dbl[..., DT_RANK + D_STATE:]
            A = -jnp.exp(Alog)

            def step(h, ins):
                dt_t, B_t, C_t, u_t = ins
                dA = jnp.exp(dt_t[..., None] * A)
                h = dA * h + (dt_t * u_t)[..., None] * B_t[:, None, :]
                y = jnp.einsum('bdn,bn->bd', h, C_t)
                return (h, y)
            h0 = jnp.zeros((Bn, D_INNER, D_STATE), x.dtype)
            xs = (dt.transpose(1, 0, 2), Bv.transpose(1, 0, 2), Cv.transpose(1, 0, 2), uc.transpose(1, 0, 2))
            _, ys = jax.lax.scan(step, h0, xs)
            y = ys.transpose(1, 0, 2) + uc * Dp
            y = y * _silu(z)
            return jnp.einsum('bld,ed->ble', y, Wout)
        fo = _mamba(x, Win_f, convw_f, convb_f, Wx_f, Wdt_f, bdt_f, Alog_f, Dp_f, Wout_f)
        fo = _layernorm(fo, ln_g_f, ln_b_f)
        xr = x[:, ::-1, :]
        bo = _mamba(xr, Win_b, convw_b, convb_b, Wx_b, Wdt_b, bdt_b, Alog_b, Dp_b, Wout_b)
        bo = _layernorm(bo[:, ::-1, :], ln_g_b, ln_b_b)
        combined = jnp.concatenate([fo, bo], axis=-1)
        return jnp.einsum('ble,de->bld', combined, Wfuse) + bfuse

    def _L0_cond2_ref(x, h0, Wx, Wh, b):
        import jax, jax.numpy as jnp
        import numpy as np
        N, T, D, H = (128, 64, 128, 128)
        xW = jnp.einsum('ntd,dh->tnh', x, Wx) + b

        def step(h, xw_t):
            h_next = jnp.tanh(h @ Wh + xw_t)
            return (h_next, h_next)
        _, hs = jax.lax.scan(step, h0, xW)
        return jnp.swapaxes(hs, 0, 1)

    def _L0_ffn_ref(x, weight):
        import jax, jax.numpy as jnp
        import numpy as np
        EPS = 1e-05

        @jax.custom_vjp
        def ste_quantize(w):
            scale = jnp.maximum(jnp.mean(jnp.abs(w)), EPS)
            return jnp.clip(jnp.round(w / scale), -1.0, 1.0)

        def _ste_fwd(w):
            return (ste_quantize(w), None)

        def _ste_bwd(_, g):
            return (g,)
        ste_quantize.defvjp(_ste_fwd, _ste_bwd)
        w_ternary = ste_quantize(weight)
        scale = jnp.maximum(jnp.mean(jnp.abs(weight)), EPS)
        return jnp.einsum('bsi,oi->bso', x, w_ternary * scale)

    def _L1_cond_ref(x, h0, Wx, Wh, b):
        import jax, jax.numpy as jnp
        import numpy as np
        import math
        N, T, D, H = (64, 64, 128, 128)

        def lstm_forward(x, h0, Wx, Wh, b):
            Hd = h0.shape[1]
            xW = jnp.einsum('ntd,dg->ntg', x, Wx) + b
            c0 = jnp.zeros_like(h0)

            def step(carry, xw_t):
                prev_h, prev_c = carry
                a = xw_t + prev_h @ Wh
                i = jax.nn.sigmoid(a[:, :Hd])
                f = jax.nn.sigmoid(a[:, Hd:2 * Hd])
                o = jax.nn.sigmoid(a[:, 2 * Hd:3 * Hd])
                g = jnp.tanh(a[:, 3 * Hd:])
                next_c = f * prev_c + i * g
                next_h = o * jnp.tanh(next_c)
                return ((next_h, next_c), next_h)
            (_, _), hs = jax.lax.scan(step, (h0, c0), jnp.swapaxes(xW, 0, 1))
            return jnp.swapaxes(hs, 0, 1)
        return lstm_forward(x, h0, Wx, Wh, b)

    def _L1_attn_ref(x, Wr, Wk, Wv, Wo, decay, ln_w):
        import jax, jax.numpy as jnp
        import numpy as np
        B, T, D = (4, 512, 128)

        def _rmsnorm(y, w):
            return y * jax.lax.rsqrt(jnp.mean(y * y, axis=-1, keepdims=True) + 1e-06) * w
        Bsz, Tlen, Dm = x.shape
        r = jax.nn.sigmoid(jnp.einsum('btd,ed->bte', x, Wr))
        k = jnp.einsum('btd,ed->bte', x, Wk)
        v = jnp.einsum('btd,ed->bte', x, Wv)
        dec = jax.nn.sigmoid(decay)
        log_decay = jnp.log(jnp.clip(dec, 1e-07))
        t = jnp.arange(Tlen, dtype=x.dtype)[:, None]
        scale = jnp.exp(t * log_decay[None, :])
        kv = k * v
        cum = jnp.cumsum(kv / jnp.clip(scale, 1e-10)[None], axis=1)
        state = cum * scale[None]
        y = _rmsnorm(r * state, ln_w)
        return jnp.einsum('btd,ed->bte', y, Wo)

    def _L1_cond2_ref(v, q_pool, W1, b1, W2, b2):
        import jax, jax.numpy as jnp
        import numpy as np
        INV_SQRT2 = 0.7071067811865476
        B, N, d = v.shape
        h = jax.nn.silu(q_pool @ W1.T + b1)
        gate = jax.nn.sigmoid(h @ W2.T + b2)[:, None, :]
        levels = int(np.log2(N))
        a = v
        details = []
        for _ in range(levels):
            e, o = (a[:, 0::2], a[:, 1::2])
            details.append((e - o) * INV_SQRT2)
            a = (e + o) * INV_SQRT2
        a = a * gate
        for dc in reversed(details):
            dc = dc * gate
            e = (a + dc) * INV_SQRT2
            o = (a - dc) * INV_SQRT2
            n = e.shape[1]
            a = jnp.stack([e, o], axis=2).reshape(B, 2 * n, d)
        return v + a

    def _L1_ffn_ref(hidden_states, Wr, router_bias, Wg, Wu, Wd, conv_w, conv_b):
        import jax, jax.numpy as jnp
        import numpy as np
        from jax import lax
        H = 128
        E = 8
        E_MLP = E - 4
        TOP_K = 2
        I = 64
        KC = 4
        SHARED_SCALE = 1.0
        B, S, Hd = hidden_states.shape
        T = B * S
        x = hidden_states.reshape(T, Hd)
        scores = jax.nn.sigmoid(x @ Wr)
        _, idx = lax.top_k(scores + router_bias, TOP_K)
        w = jnp.take_along_axis(scores, idx, axis=-1)
        w = w / (jnp.sum(w, axis=-1, keepdims=True) + 1e-09)
        cw = jnp.zeros((T, E), dtype=x.dtype).at[jnp.arange(T)[:, None], idx].add(w)
        g = jnp.einsum('th,ehi->tei', x, Wg)
        u = jnp.einsum('th,ehi->tei', x, Wu)
        hid = jax.nn.silu(g) * u
        mlp_out = jnp.einsum('tei,eih->teh', hid, Wd)
        routed = jnp.einsum('te,teh->th', cw[:, :E_MLP], mlp_out)
        routed = routed + cw[:, E_MLP:E_MLP + 1] * x
        routed = routed + cw[:, E_MLP + 2:E_MLP + 3] * x
        routed = routed + cw[:, E_MLP + 3:E_MLP + 4] * jax.nn.relu(x)
        routed = routed.reshape(B, S, Hd)
        shared = lax.conv_general_dilated(hidden_states, conv_w, window_strides=(1,), padding=[(KC - 1, 0)], dimension_numbers=('NHC', 'HIO', 'NHC'), feature_group_count=Hd) + conv_b
        return routed + SHARED_SCALE * shared
    x = x + _L0_attn_ref(_L0_cond_ref(x, cond_1024, L0_cond_router_W, L0_cond_router_bias, L0_cond_w1, L0_cond_w3, L0_cond_w2, L0_cond_W1e, L0_cond_W2e), L0_attn_Win_f, L0_attn_convw_f, L0_attn_convb_f, L0_attn_Wx_f, L0_attn_Wdt_f, L0_attn_bdt_f, L0_attn_Alog_f, L0_attn_Dp_f, L0_attn_Wout_f, L0_attn_ln_g_f, L0_attn_ln_b_f, L0_attn_Win_b, L0_attn_convw_b, L0_attn_convb_b, L0_attn_Wx_b, L0_attn_Wdt_b, L0_attn_bdt_b, L0_attn_Alog_b, L0_attn_Dp_b, L0_attn_Wout_b, L0_attn_ln_g_b, L0_attn_ln_b_b, L0_attn_Wfuse, L0_attn_bfuse)
    x = x + _L0_ffn_ref(_L0_cond2_ref(x, cond_1024, L0_cond2_Wx, L0_cond2_Wh, L0_cond2_b), L0_ffn_weight)
    x = x + _L1_attn_ref(_L1_cond_ref(x, cond_1024, L1_cond_Wx, L1_cond_Wh, L1_cond_b), L1_attn_Wr, L1_attn_Wk, L1_attn_Wv, L1_attn_Wo, L1_attn_decay, L1_attn_ln_w)
    x = x + _L1_ffn_ref(_L1_cond2_ref(x, cond_1024, L1_cond2_W1, L1_cond2_b1, L1_cond2_W2, L1_cond2_b2), L1_ffn_Wr, L1_ffn_router_bias, L1_ffn_Wg, L1_ffn_Wu, L1_ffn_Wd, L1_ffn_conv_w, L1_ffn_conv_b)
    return x

_drawn_inputs = setup_inputs


def setup_inputs(seed=0):
    import zlib

    import numpy as np

    out = dict(_drawn_inputs(seed))
    spreads = {'L0_cond_router_bias': (0.0, 0.8),
     'L0_attn_convb_f': (0.0, 0.8),
     'L0_attn_Dp_f': (1.0, 0.6),
     'L0_attn_ln_g_f': (1.0, 0.6),
     'L0_attn_ln_b_f': (0.0, 0.1),
     'L0_attn_convb_b': (0.0, 0.55),
     'L0_attn_Dp_b': (1.0, 0.6),
     'L0_attn_ln_g_b': (1.0, 0.6),
     'L0_attn_ln_b_b': (0.0, 0.1),
     'L0_attn_bfuse': (0.0, 0.1),
     'L0_cond2_b': (0.0, 0.1),
     'L1_cond_b': (0.0, 0.1),
     'L1_attn_decay': (0.9900000095367432, 0.2),
     'L1_attn_ln_w': (1.0, 0.2),
     'L1_cond2_b1': (0.0, 0.1),
     'L1_cond2_b2': (0.0, 0.1),
     'L1_ffn_router_bias': (0.0, 0.1),
     'L1_ffn_conv_b': (0.0, 0.383)}
    factors = {'L0_cond_router_W': 8.0,
     'L0_cond_w1': 5.507,
     'L0_cond_w3': 5.504,
     'L0_cond_w2': 5.504,
     'L0_cond_W1e': 4.305,
     'L0_cond_W2e': 8.0,
     'L0_attn_Win_f': 4.624,
     'L0_attn_convw_f': 8.0,
     'L0_attn_Wx_f': 8.0,
     'L0_attn_Wdt_f': 8.0,
     'L0_attn_bdt_f': 8.0,
     'L0_attn_Alog_f': 8.0,
     'L0_attn_Wout_f': 3.411,
     'L0_attn_Win_b': 3.294,
     'L0_attn_convw_b': 8.0,
     'L0_attn_Wx_b': 8.0,
     'L0_attn_Wdt_b': 8.0,
     'L0_attn_bdt_b': 8.0,
     'L0_attn_Alog_b': 8.0,
     'L0_attn_Wout_b': 5.453}
    for name, (base, spread) in spreads.items():
        noise = np.random.default_rng([zlib.crc32(name.encode()), seed]).standard_normal(out[name].shape)
        drawn = base * np.exp(spread * noise) if base else spread * noise
        out[name] = jnp.asarray(drawn.astype(out[name].dtype))
    for name, factor in factors.items():
        out[name] = (out[name] * factor).astype(out[name].dtype)
    return out
```

```python
from contextlib import ExitStack

import concourse.bass as bass
from concourse import mybir

F32 = mybir.dt.float32
BF16 = mybir.dt.bfloat16
U32 = mybir.dt.uint32
ALU = mybir.AluOpType
ACT = mybir.ActivationFunctionType
AX_X = mybir.AxisListType.X

B, T, D = 8, 128, 128
N = B * T
HALF = N // 2
HB = B // 2
DI, NS, DC, DR = 256, 32, 4, 8
HS, E = 256, 8
G4 = 4
CH = 16
NCH = T // CH
CHB = CH * B
FAR = 1.0e24


def columns(parts):
    at, place = 0, {}
    for name, width in parts:
        place[name] = (at, at + width)
        at += width
    return place, at


MAMBA = [("WinT", 2 * DI), ("WxdT", 2 * DR), ("WxB", 2 * 96), ("WxC", 2 * 96), ("WdtT", DI),
         ("WoutT", 2 * D), ("Alog", 2 * NS), ("convw", 2 * DC), ("convb", 2), ("bdt", 2), ("Dp", 2),
         ("ln_g", 1), ("ln_b", 1)]
PACK0, W0 = columns([("xT", N), ("condT", B), ("RWx", E), ("RWt", E), ("rbias", E), ("w1", HS), ("w3", HS),
                     ("w2", HS), ("W1e", E * 128), ("W2e", E * 128)])
PACK1, W1 = columns([(f"{n}_{d}", w) for d in "fb" for n, w in MAMBA]
                    + [("WfT", 2 * D), ("bfuse", 1), ("WxR", D), ("WhR", D), ("bR", D), ("WqT", D),
                       ("WxL", 4 * D), ("WhL", 4 * D), ("bL", 4 * D), ("WrT", D), ("WkT", D), ("WvT", D),
                       ("WoT", D), ("decay", 1), ("ln_w", 1), ("C1T", D), ("C2T", D), ("cb1", 1), ("cb2", 1),
                       ("fWr", E), ("frb", E), ("Wg", 256), ("Wu", 256), ("Wd", 256), ("fcw", DC), ("fcb", 1)])
CONF, WF = columns([("ident", 128), ("mean", 128), ("ones", 128), ("iota8", E), ("iotat", T), ("keep", N)])
CONB, WB = columns([("identb", 128), ("pick32", NS * 128), ("pick8", E * 128), ("pick46", 128),
                    ("pickpair", 256)])


def build(nc, pack0, pack1, conf, conb, out):
    ctx = ExitStack()
    with ctx:
        scopes = [ctx]

        def sb(name, shape, dt=F32):
            return scopes[-1].enter_context(nc.sbuf_tensor(name, shape, dt))

        def sem(name):
            return ctx.enter_context(nc.semaphore(name))

        p0 = sb("p0", [128, W0])
        p1 = sb("p1", [128, W1])
        cf = sb("cf", [128, WF])
        cb = sb("cb", [128, WB], BF16)
        PS = ctx.enter_context(nc.psum_tensor("PS", [128, 8, 512], F32))

        def w(name):
            for src, place in ((p0, PACK0), (p1, PACK1), (cf, CONF), (cb, CONB)):
                if name in place:
                    a, b = place[name]
                    return src[:, a:b]
            raise KeyError(name)

        xT = w("xT")
        condT = w("condT")
        ident = w("ident")
        meanw = w("mean")
        pick32 = w("pick32")

        uin = [sb("uin_f", [128, N]), sb("uin_r", [128, N])]
        lnout = [sb("ln_fwd", [128, HALF]), sb("ln_bwd", [128, HALF])]
        x1 = sb("x1", [128, N])
        Aneg = sb("Aneg", [128, 2, 2 * NS])
        diagD = sb("diagD", [128, 2, 2, 128])
        wq = sb("wq", [128, D])
        g1 = sb("g1", [128, B])
        WxLs = sb("WxLs", [128, 4 * D])
        WhLs = sb("WhLs", [128, 4 * D])
        bLs = sb("bLs", [128, 4 * D])
        H0 = sb("H0", [128, B])
        dscale = sb("dscale", [128, T])
        dinv = sb("dinv", [128, T])
        up = sb("up", [128, 2, HB, DC - 1 + T])

        class Router:

            def __init__(self, name, guarded):
                self.guarded = guarded
                self.s = sb(name + "_s", [128, 8, E])
                self.sel = sb(name + "_sel", [128, 8, E])
                self.top = sb(name + "_top", [128, 8, 8])
                self.idx = sb(name + "_idx", [128, 8, 8], U32)
                self.idf = sb(name + "_idf", [128, 8, 2])
                self.hot = sb(name + "_hot", [128, 8, 2, E])
                self.mask = sb(name + "_mask", [128, 8, E])
                self.ss = sb(name + "_ss", [128, 8, E])
                self.den = sb(name + "_den", [128, 8])
                self.rec = sb(name + "_rec", [128, 8])
                self.flag = sb(name + "_flag", [128, 8])
                self.comb = sb(name + "_comb", [128, 8, E])
                self.rest = sb(name + "_rest", [128, 8, E])
                self.parts = sb(name + "_parts", [128, 8, 3 * E], BF16)
                self.gT = sb(name + "_gT", [3 * E, N], BF16)
                self.logits = sem(name + "_logits")
                self.scored = sem(name + "_scored")
                self.step = sem(name + "_step")
                self.turned = sem(name + "_turned")
                self.gates = sem(name + "_gates")

            def act(self, eng, bank):
                eng.wait_ge(self.logits, 1)
                eng.activation(self.s[:, :, :], PS[:, bank, 0:8 * E].rearrange("p (t e) -> p t e", e=E),
                               ACT.Sigmoid).then_inc(self.scored, 1)

            def dve(self, eng, bias, bank):
                done = [0]

                def after(ins):
                    done[0] += 1
                    ins.then_inc(self.step, 1)
                    eng.wait_ge(self.step, done[0])

                eng.wait_ge(self.scored, 1)
                after(eng.tensor_tensor(self.sel[:, :, :], self.s[:, :, :],
                                        bias.unsqueeze(1).to_broadcast([128, 8, E]), ALU.add))
                for t in range(8):
                    done[0] += 1
                    eng.max(self.top[:, t, :], self.sel[:, t, :]).then_inc(self.step, 1)
                eng.wait_ge(self.step, done[0])
                for t in range(8):
                    done[0] += 1
                    eng.max_index(self.idx[:, t, :], self.top[:, t, :], self.sel[:, t, :]).then_inc(self.step, 1)
                eng.wait_ge(self.step, done[0])
                after(eng.tensor_copy(self.idf[:, :, :], self.idx[:, :, 0:2]))
                iota = w("iota8").unsqueeze(1).unsqueeze(1).to_broadcast([128, 8, 2, E])
                after(eng.tensor_tensor(self.hot[:, :, :, :], iota,
                                        self.idf[:, :, :].unsqueeze(3).to_broadcast([128, 8, 2, E]), ALU.is_equal))
                after(eng.tensor_tensor(self.mask[:, :, :], self.hot[:, :, 0, :], self.hot[:, :, 1, :], ALU.add))
                after(eng.tensor_tensor(self.ss[:, :, :], self.s[:, :, :], self.mask[:, :, :], ALU.mult))
                after(eng.tensor_reduce(self.den[:, :], self.ss[:, :, :], AX_X, ALU.add))
                after(eng.tensor_scalar(self.rec[:, :], self.den[:, :], 1e-9, None, ALU.add))
                after(eng.reciprocal(self.rec[:, :], self.rec[:, :]))
                if self.guarded:
                    after(eng.tensor_scalar(self.flag[:, :], self.den[:, :], 1e-9, None, ALU.is_gt))
                    after(eng.tensor_tensor(self.rec[:, :], self.rec[:, :], self.flag[:, :], ALU.mult))
                    after(eng.tensor_scalar(self.flag[:, :], self.flag[:, :], -0.5, 0.5, ALU.mult, ALU.add))
                after(eng.tensor_tensor(self.comb[:, :, :], self.ss[:, :, :],
                                        self.rec[:, :].unsqueeze(2).to_broadcast([128, 8, E]), ALU.mult))
                if self.guarded:
                    after(eng.tensor_tensor(self.mask[:, :, :], self.mask[:, :, :],
                                            self.flag[:, :].unsqueeze(2).to_broadcast([128, 8, E]), ALU.mult))
                    after(eng.tensor_tensor(self.comb[:, :, :], self.comb[:, :, :], self.mask[:, :, :], ALU.add))
                after(eng.tensor_copy(self.parts[:, :, 0:E], self.comb[:, :, :]))
                after(eng.tensor_tensor(self.rest[:, :, :], self.comb[:, :, :], self.parts[:, :, 0:E], ALU.subtract))
                after(eng.tensor_copy(self.parts[:, :, E:2 * E], self.rest[:, :, :]))
                after(eng.tensor_tensor(self.parts[:, :, 2 * E:3 * E], self.rest[:, :, :],
                                        self.parts[:, :, E:2 * E], ALU.subtract))
                self.n_steps = done[0]
                eng.wait_ge(self.turned, 1)
                eng.tensor_copy(self.gT[:, :], PS[0:3 * E, bank, :].bitcast(BF16)).then_inc(self.gates, 1)

            def pe_turn(self, eng, bank):
                n = 1 + 8 + 8 + 7 + (5 if self.guarded else 0) + 1 + 4
                eng.wait_ge(self.step, n)
                turned = PS[0:3 * E, bank, :].bitcast(BF16)
                for t in range(8):
                    mm = eng.transpose(turned[:, t * 128:(t + 1) * 128], self.parts[:, t, :], w("identb"))
                mm.then_inc(self.turned, 1)

        loaded = [sem(f"loaded{i}") for i in range(4)]
        prep_act = sem("prep_act")
        prep_dve = sem("prep_dve")
        prep_pe = sem("prep_pe")
        pads = sem("pads")
        absw = sb("absw", [128, D])
        asum = sb("asum", [128, 1])
        qscale = sb("qscale", [128, 1])
        qthr = sb("qthr", [128, 2])
        qneg = sb("qneg", [128, D])
        sgd = sb("sgd", [128, 1])
        ldec = sb("ldec", [128, 1])
        c2h = sb("c2h", [128, B])
        gate = sb("gate", [128, B])
        eps = sb("eps", [128, 3])

        with nc.Block() as block:
            @block.sync
            def _(eng):
                eng.dma_start(p0[:, 0:1024 + 32], pack0[:, 0:1024 + 32]).then_inc(loaded[0], 16)
                eng.dma_start(cb[:, :], conb).then_inc(loaded[3], 16)
                eng.dma_start(cf[:, :], conf).then_inc(loaded[2], 16)
                eng.dma_start(p0[:, 1024 + 32:], pack0[:, 1024 + 32:]).then_inc(loaded[0], 16)
                eng.dma_start(p1[:, :], pack1).then_inc(loaded[1], 16)
                for s, n in zip(loaded, (32, 16, 16, 16)):
                    eng.wait_ge(s, n)

            @block.gpsimd
            def _(eng):
                eng.memset(up[:, :, :, :], 0.0).then_inc(pads, 1)
                eng.memset(eps[:, 0:1], 1e-5).then_inc(pads, 1)
                eng.memset(eps[:, 1:2], 1e-6).then_inc(pads, 1)
                eng.memset(eps[:, 2:3], 1.0).then_inc(pads, 1)

            @block.scalar
            def _(eng):
                eng.wait_ge(loaded[1], 16)
                eng.wait_ge(loaded[2], 16)
                eng.wait_ge(pads, 4)
                eng.activation(absw[:, :], w("WqT"), ACT.Abs).then_inc(prep_act, 1)
                for d, tag in enumerate("fb"):
                    eng.activation(Aneg[:, d, :], w("Alog_" + tag), ACT.Exp).then_inc(prep_act, 1)
                eng.activation(sgd[:, :], w("decay"), ACT.Sigmoid).then_inc(prep_act, 1)
                eng.wait_ge(prep_dve, 1)
                eng.activation(ldec[:, :], sgd[:, :], ACT.Ln).then_inc(prep_act, 1)
                eng.wait_ge(prep_act, 5)
                eng.activation(dscale[:, :], w("iotat"), ACT.Exp, scale=ldec[:, 0:1]).then_inc(prep_act, 1)
                eng.wait_ge(prep_pe, 1)
                eng.activation(c2h[:, :], PS[:, 0, 0:B], ACT.Silu, bias=w("cb1")).then_inc(prep_act, 1)
                eng.wait_ge(prep_pe, 2)
                eng.activation(gate[:, :], PS[:, 1, 0:B], ACT.Sigmoid, bias=w("cb2")).then_inc(prep_act, 1)

            @block.tensor
            def _(eng):
                eng.wait_ge(loaded[1], 16)
                eng.wait_ge(loaded[2], 16)
                eng.wait_ge(loaded[0], 32)
                eng.matmul(PS[:, 0, 0:B], w("C1T"), condT, start=True, stop=True).then_inc(prep_pe, 1)
                eng.wait_ge(prep_act, 7)
                eng.matmul(PS[:, 1, 0:B], w("C2T"), c2h[:, :], start=True, stop=True).then_inc(prep_pe, 1)
                eng.wait_ge(prep_dve, 2)
                eng.matmul(PS[:, 2, 0:1], w("ones"), asum[:, :], start=True, stop=True).then_inc(prep_pe, 1)

            @block.vector
            def _(eng):
                eng.wait_ge(loaded[1], 16)
                eng.wait_ge(loaded[2], 16)
                eng.wait_ge(loaded[0], 32)
                eng.wait_ge(prep_act, 4)
                eng.tensor_scalar(sgd[:, :], sgd[:, :], 1e-7, None, ALU.max).then_inc(prep_dve, 1)
                eng.tensor_reduce(asum[:, :], absw[:, :], AX_X, ALU.add).then_inc(prep_dve, 1)
                eng.tensor_scalar(Aneg[:, :, :], Aneg[:, :, :], -1.0, None, ALU.mult).then_inc(prep_dve, 1)
                n = 3
                for d, tag in enumerate("fb"):
                    for h in range(2):
                        a = PACK1["Dp_" + tag][0] + h
                        eng.tensor_scalar(diagD[:, d, h, :], ident, p1[:, a:a + 1], None, ALU.mult)\
                           .then_inc(prep_dve, 1)
                        n += 1
                L = 3 * D
                eng.tensor_scalar(WxLs[:, 0:L], w("WxL")[:, 0:L], 0.5, None, ALU.mult).then_inc(prep_dve, 1)
                eng.tensor_copy(WxLs[:, L:], w("WxL")[:, L:]).then_inc(prep_dve, 1)
                eng.tensor_scalar(WhLs[:, 0:L], w("WhL")[:, 0:L], 0.25, None, ALU.mult).then_inc(prep_dve, 1)
                eng.tensor_scalar(WhLs[:, L:], w("WhL")[:, L:], 0.5, None, ALU.mult).then_inc(prep_dve, 1)
                eng.tensor_scalar(bLs[0:1, 0:L], w("bL")[0:1, 0:L], 0.5, None, ALU.mult).then_inc(prep_dve, 1)
                eng.tensor_copy(bLs[0:1, L:], w("bL")[0:1, L:]).then_inc(prep_dve, 1)
                eng.tensor_scalar(H0[:, :], condT, 2.0, None, ALU.mult).then_inc(prep_dve, 1)
                n += 7
                eng.wait_ge(prep_act, 6)
                eng.tensor_scalar(dinv[:, :], dscale[:, :], 1e-10, None, ALU.max).then_inc(prep_dve, 1)
                n += 1
                eng.wait_ge(prep_dve, n)
                eng.reciprocal(dinv[:, :], dinv[:, :]).then_inc(prep_dve, 1)
                n += 1
                eng.wait_ge(prep_pe, 3)
                eng.tensor_scalar(qscale[:, :], PS[:, 2, 0:1], 1.0 / (D * D), 1e-5, ALU.mult, ALU.max)\
                   .then_inc(prep_dve, 1)
                n += 1
                eng.wait_ge(prep_dve, n)
                eng.tensor_scalar(qthr[:, 0:1], qscale[:, :], 0.5, None, ALU.mult).then_inc(prep_dve, 1)
                eng.tensor_scalar(qthr[:, 1:2], qscale[:, :], -0.5, None, ALU.mult).then_inc(prep_dve, 1)
                n += 2
                eng.wait_ge(prep_dve, n)
                eng.tensor_scalar(wq[:, :], w("WqT"), qthr[:, 0:1], qscale[:, 0:1], ALU.is_gt, ALU.mult)\
                   .then_inc(prep_dve, 1)
                eng.tensor_scalar(qneg[:, :], w("WqT"), qthr[:, 1:2], qscale[:, 0:1], ALU.is_lt, ALU.mult)\
                   .then_inc(prep_dve, 1)
                n += 2
                eng.wait_ge(prep_dve, n)
                eng.tensor_tensor(wq[:, :], wq[:, :], qneg[:, :], ALU.subtract).then_inc(prep_dve, 1)
                eng.wait_ge(prep_act, 8)
                eng.tensor_scalar(g1[:, :], gate[:, :], 1.0, None, ALU.add).then_inc(prep_dve, 1)

        units = [(th, "shared", m) for th in range(2) for m in range(2)]
        units += [(th, "expert", e) for th in range(2) for e in range(E)]
        scopes.append(ExitStack())
        r0 = Router("r0", guarded=True)
        m_a, m_b, m_act, m_mul, m_acc, m_in, m_rev = (sem("moe_" + n)
                                                  for n in ("a", "b", "act", "mul", "acc", "in", "rev"))
        mG = sb("mG", [128, 2, 512])
        mS = sb("mS", [128, 2, 512])
        first = {th: min(j for j, u in enumerate(units) if u[0] == th) for th in range(2)}
        last = {th: max(j for j, u in enumerate(units) if u[0] == th) for th in range(2)}

        with nc.Block() as block:
            @block.tensor
            def _(eng):
                for t in range(8):
                    eng.matmul(PS[:, 0, t * E:(t + 1) * E], xT[:, t * 128:(t + 1) * 128], w("RWx"),
                               start=(t == 0), stop=False, skip_group_check=True)
                    mm = eng.matmul(PS[:, 0, t * E:(t + 1) * E], condT[:, t:t + 1].to_broadcast([128, 128]),
                                    w("RWt"), start=False, stop=True, skip_group_check=True)
                mm.then_inc(r0.logits, 1)

                def accumulate(j):
                    th, kind, i = units[j]
                    wt = w("w2" if kind == "shared" else "W2e")[:, i * 128:(i + 1) * 128]
                    eng.wait_ge(m_mul, j + 1)
                    eng.matmul(PS[:, 6 + th, :], wt, mS[:, j % 2, :], start=(j == first[th]),
                               stop=(j == last[th]), skip_group_check=True).then_inc(m_acc, 1)

                for j, (th, kind, i) in enumerate(units):
                    cols = xT[:, th * HALF:(th + 1) * HALF]
                    if j >= 2:
                        eng.wait_ge(m_act, j - 1)
                    wt = w("w1" if kind == "shared" else "W1e")[:, i * 128:(i + 1) * 128]
                    eng.matmul(PS[:, 2 + j % 2, :], wt, cols, start=True, stop=True).then_inc(m_a, 1)
                    if (kind, th, i) == ("expert", 0, 0):
                        r0.pe_turn(eng, 1)
                        eng.wait_ge(r0.gates, 1)
                    if j >= 2:
                        eng.wait_ge(m_mul, j - 1)
                    if kind == "shared":
                        eng.matmul(PS[:, 4 + j % 2, :], w("w3")[:, i * 128:(i + 1) * 128], cols,
                                   start=True, stop=True).then_inc(m_b, 1)
                    else:
                        eng.matmul(PS[:, 4 + j % 2, :], w("pick8")[0:3 * E, i * 128:(i + 1) * 128],
                                   r0.gT[:, th * HALF:(th + 1) * HALF], start=True, stop=True).then_inc(m_b, 1)
                    if j:
                        accumulate(j - 1)
                accumulate(len(units) - 1)

            @block.scalar
            def _(eng):
                r0.act(eng, 0)
                for j, (th, kind, i) in enumerate(units):
                    eng.wait_ge(m_a, j + 1)
                    if j >= 2:
                        eng.wait_ge(m_mul, j - 1)
                    eng.activation(mG[:, j % 2, :], PS[:, 2 + j % 2, :],
                                   ACT.Silu if kind == "shared" else ACT.Gelu).then_inc(m_act, 1)
                for th in range(2):
                    eng.wait_ge(m_in, th + 1)
                    a, b = th * HALF, (th + 1) * HALF
                    eng.activation(uin[1][:, a:b].rearrange("p (b t) -> p b t", t=T),
                                   uin[0][:, a:b].rearrange("p (b t) -> p b t", t=T)[:, :, ::-1], ACT.Copy)\
                       .then_inc(m_rev, 1)

            @block.vector
            def _(eng):
                def multiply(j):
                    eng.wait_ge(m_act, j + 1)
                    eng.wait_ge(m_b, j + 1)
                    if j >= 2:
                        eng.wait_ge(m_acc, j - 1)
                    eng.tensor_tensor(mS[:, j % 2, :], mG[:, j % 2, :], PS[:, 4 + j % 2, :], ALU.mult)\
                       .then_inc(m_mul, 1)

                for j in range(3):
                    multiply(j)
                r0.dve(eng, w("rbias"), 1)
                for j in range(3, len(units)):
                    multiply(j)
                for th in range(2):
                    eng.wait_ge(m_acc, last[th] + 1)
                    eng.tensor_scalar(uin[0][:, th * HALF:(th + 1) * HALF], PS[:, 6 + th, :], 1.0 / 3.0, None,
                                      ALU.mult).then_inc(m_in, 1)

        uc = sb("uc", [128, 2, HALF])
        cv = sb("cv", [128, 2, HALF])
        sz = sb("sz", [128, 2, HALF])
        dtr = sb("dtr", [DR, HALF])
        dt_ = sb("dt", [128, 2, HALF])
        dtu = sb("dtu", [128, 2, HALF])
        spv = sb("spv", [128, 2, HALF])
        spe = sb("spe", [128, 2, HALF])
        spl = sb("spl", [128, 2, HALF])
        spq = sb("spq", [128, 2, HALF])
        bc3 = [sb("b3", [96, HALF], BF16), sb("c3", [96, HALF], BF16)]
        rest = sb("rest", [96, HALF])
        mid = sb("mid", [96, HALF], BF16)
        Bsb = sb("Bsb", [128, 2, HALF])
        dBu = sb("dBu", [128, 4, HALF])
        hst = sb("hst", [128, 4, HALF])
        hC = sb("hC", [128, 4, HALF])
        yz = sb("yz", [128, 2, HALF])
        fo = sb("fo", [128, HALF])
        cen = sb("cen", [128, HALF])
        sq = sb("sq", [128, HALF])
        sd = sb("sd", [128, HALF])

        f_xz, f_u, f_z, f_conv, f_uc, f_dbl, f_dtr, f_dtp, f_sp, f_hi, f_v = (
            sem("front_" + n) for n in ("xz", "u", "z", "conv", "uc", "dbl", "dtr", "dtp", "sp", "hi", "v"))
        s_b, s_c, s_bc, s_da, s_dbu, s_h, s_hc, s_y = (
            sem("scan_" + n) for n in ("b", "c", "bcopy", "dA", "dBu", "h", "hC", "y"))
        k_yz, k_o, k_fo, k_mean, k_cen, k_sq, k_var, k_sd, k_n, k_fuse, k_x1 = (
            sem("back_" + n) for n in ("yz", "o", "fo", "mean", "cen", "sq", "var", "sd", "n", "fuse", "x1"))
        YB, CB, BB, AB = (0, 1), (2, 3), (4, 7), (5, 6)

        for c, (th, d) in enumerate((th, d) for th in range(2) for d in range(2)):
            tag = "fb"[d]
            cols = uin[d][:, th * HALF:(th + 1) * HALF]

            def col(name, i, tag=tag):
                a = PACK1[name + "_" + tag][0] + i
                return p1[:, a:a + 1]

            with nc.Block() as block:
                @block.tensor
                def _(eng):
                    for q in range(4):
                        eng.matmul(PS[:, q, :], w("WinT_" + tag)[:, q * 128:(q + 1) * 128], cols,
                                   start=True, stop=True).then_inc(f_xz, 1)
                    eng.wait_ge(f_uc, 2 * c + 2)
                    for bank, name, m in ((4, "WxdT_", DR), (5, "WxB_", 96), (6, "WxC_", 96)):
                        for h in range(2):
                            mm = eng.matmul(PS[0:m, bank, :], w(name + tag)[:, h * m:(h + 1) * m], uc[:, h, :],
                                            start=(h == 0), stop=(h == 1))
                        mm.then_inc(f_dbl, 1)
                    eng.wait_ge(f_dtr, c + 1)
                    eng.wait_ge(f_u, 2 * c + 2)
                    for h in range(2):
                        eng.matmul(PS[:, h, :], w("WdtT_" + tag)[0:DR, h * 128:(h + 1) * 128], dtr[:, :],
                                   start=True, stop=True).then_inc(f_dtp, 1)

                @block.scalar
                def _(eng):
                    for h in range(2):
                        eng.wait_ge(f_xz, 4 * c + h + 1)
                        eng.activation(up[:, h, :, DC - 1:], PS[:, h, :].rearrange("p (b t) -> p b t", t=T),
                                       ACT.Copy).then_inc(f_u, 1)
                    for h in range(2):
                        eng.wait_ge(f_xz, 4 * c + h + 3)
                        eng.activation(sz[:, h, :], PS[:, 2 + h, :], ACT.Silu).then_inc(f_z, 1)
                    for h in range(2):
                        eng.wait_ge(f_conv, 8 * c + 4 * h + 4)
                        eng.activation(uc[:, h, :], cv[:, h, :], ACT.Silu).then_inc(f_uc, 1)
                    eng.wait_ge(f_dbl, 3 * c + 1)
                    eng.activation(dtr[:, :], PS[0:DR, 4, :], ACT.Copy).then_inc(f_dtr, 1)
                    for i in range(2):
                        eng.wait_ge(f_dbl, 3 * c + 2 + i)
                        eng.activation(bc3[i][:, :], PS[0:96, 5 + i, :], ACT.Copy).then_inc(f_hi, 1)
                    for h in range(2):
                        eng.wait_ge(f_dtp, 2 * c + h + 1)
                        eng.activation(spv[:, h, :], PS[:, h, :], ACT.Identity, bias=col("bdt", h)).then_inc(f_sp, 1)
                    eng.wait_ge(f_sp, 5 * c + 2)
                    eng.activation(spl[:, :, :], spv[:, :, :], ACT.Abs).then_inc(f_sp, 1)
                    eng.wait_ge(f_sp, 5 * c + 3)
                    eng.activation(spe[:, :, :], spl[:, :, :], ACT.Exp, scale=-1.0).then_inc(f_sp, 1)
                    eng.wait_ge(f_sp, 5 * c + 4)
                    eng.activation(spl[:, :, :], spe[:, :, :], ACT.Ln, bias=eps[:, 2:3]).then_inc(f_sp, 1)

                @block.vector
                def _(eng):
                    n = 8 * c
                    for h in range(2):
                        eng.wait_ge(f_u, 2 * c + h + 1)
                        acc = cv[:, h, :].rearrange("p (b t) -> p b t", t=T)
                        eng.tensor_scalar(acc, up[:, h, :, 0:T], col("convw", h * DC), col("convb", h),
                                          ALU.mult, ALU.add).then_inc(f_conv, 1)
                        n += 1
                        for k in range(1, DC):
                            eng.wait_ge(f_conv, n)
                            eng.scalar_tensor_tensor(acc, up[:, h, :, k:k + T], col("convw", h * DC + k), acc,
                                                     ALU.mult, ALU.add).then_inc(f_conv, 1)
                            n += 1
                    n = 16 * c

                    def after(ins):
                        nonlocal n
                        n += 1
                        ins.then_inc(f_v, 1)
                        eng.wait_ge(f_v, n)

                    for i in range(2):
                        eng.wait_ge(f_hi, 2 * c + i + 1)
                        after(eng.tensor_tensor(rest[:, :], PS[0:96, 5 + i, :], bc3[i][:, :], ALU.subtract))
                        after(eng.tensor_copy(mid[:, :], rest[:, :]))
                        after(eng.tensor_copy(bc3[i][32:64, :], mid[32:64, :]))
                        after(eng.tensor_tensor(bc3[i][64:96, :], rest[64:96, :], mid[64:96, :], ALU.subtract))
                    eng.wait_ge(f_sp, 5 * c + 5)
                    after(eng.tensor_scalar(spq[:, :, :], spe[:, :, :], 1.0, None, ALU.add))
                    after(eng.scalar_tensor_tensor(spq[:, :, :], spq[:, :, :], 1.0, spe[:, :, :],
                                                   ALU.subtract, ALU.subtract))
                    after(eng.scalar_tensor_tensor(spl[:, :, :], spv[:, :, :], 0.0, spl[:, :, :], ALU.max, ALU.add))
                    after(eng.tensor_tensor(dt_[:, :, :], spl[:, :, :], spq[:, :, :], ALU.subtract))
                    after(eng.tensor_tensor(dtu[:, :, :], dt_[:, :, :], uc[:, :, :], ALU.mult))
                    for h in range(2):
                        after(eng.memset(dt_[:, h, :].rearrange("p (b t) -> p b t", t=T)[:, :, 0:1], FAR))
                    after(eng.tensor_copy(cen[:, 0:1], dt_[:, 0, 0:1]))

            def schedule(eng, step, lead, c=c):
                for n in range(0, lead):
                    step(n, n % 2)
                pairs = (NS - lead) // 2
                with eng.Fori(0, pairs) as i:
                    step(i * 2 + lead, lead % 2)
                    step(i * 2 + (lead + 1), (lead + 1) % 2)
                for n in range(lead + 2 * pairs, NS + 1):
                    step(n, n % 2)

            def at_least(eng, s, base, rel, static):
                if static:
                    if base + rel > 0:
                        eng.wait_ge(s, base + rel)
                else:
                    eng.wait_ge(s, rel + base)

            LEAD = 3
            nb, kb = c * NS, c * 2 * NS

            with nc.Block() as block:
                @block.tensor
                def _(eng):
                    for h in range(2):
                        eng.matmul(PS[:, YB[h], :], diagD[:, d, h, :], uc[:, h, :], start=True, stop=False,
                                   skip_group_check=True)

                    def step(n, slot):
                        static = isinstance(n, int)
                        if not (static and n == NS):
                            at_least(eng, s_bc, nb, n - 1, static)
                            pick = pick32[0:96, bass.ds(n * 128, 128)]
                            eng.matmul(PS[:, BB[slot], :], pick, bc3[0][:, :], start=True, stop=True)\
                               .then_inc(s_b, 1)
                            at_least(eng, s_hc, kb, n * 2 - 2, static)
                            eng.matmul(PS[:, CB[slot], :], pick, bc3[1][:, :], start=True, stop=True)\
                               .then_inc(s_c, 1)
                        if not (static and n == 0):
                            for h in range(2):
                                at_least(eng, s_hc, kb, n * 2 - 1 + h, static)
                                eng.matmul(PS[:, YB[h], :], ident, hC[:, 2 * (1 - slot) + h, :], start=False,
                                           stop=(static and n == NS), skip_group_check=True).then_inc(s_y, 1)

                    schedule(eng, step, LEAD)

                @block.scalar
                def _(eng):
                    def step(n, slot):
                        static = isinstance(n, int)
                        if static and n == NS:
                            return
                        at_least(eng, s_b, nb, n + 1, static)
                        at_least(eng, s_dbu, kb, n * 2 - 2, static)
                        eng.activation(Bsb[:, slot, :], PS[:, BB[slot], :], ACT.Copy).then_inc(s_bc, 1)
                        for h in range(2):
                            at_least(eng, s_h, kb, n * 2 - 1 + h, static)
                            eng.activation(PS[:, AB[h], :], dt_[:, h, :], ACT.Exp,
                                           scale=Aneg[:, d, bass.ds(n + h * NS, 1)]).then_inc(s_da, 1)

                    schedule(eng, step, LEAD)

                @block.gpsimd
                def _(eng):
                    def step(n, slot):
                        static = isinstance(n, int)
                        if static and n == NS:
                            return
                        at_least(eng, s_bc, nb, n + 1, static)
                        for h in range(2):
                            at_least(eng, s_h, kb, n * 2 - 3 + h, static)
                            eng.tensor_tensor(dBu[:, 2 * slot + h, :], dtu[:, h, :], Bsb[:, slot, :], ALU.mult)\
                               .then_inc(s_dbu, 1)

                    schedule(eng, step, LEAD)

                @block.vector
                def _(eng):
                    def product(n, slot, h, static):
                        at_least(eng, s_h, kb, n * 2 + 1 + h, static)
                        at_least(eng, s_c, nb, n + 1, static)
                        at_least(eng, s_y, kb, n * 2 - 3 + h, static)
                        eng.tensor_tensor(hC[:, 2 * slot + h, :], hst[:, 2 * slot + h, :], PS[:, CB[slot], :],
                                          ALU.mult).then_inc(s_hc, 1)

                    def scan(n, slot, h, static):
                        at_least(eng, s_da, kb, n * 2 + 1 + h, static)
                        at_least(eng, s_dbu, kb, n * 2 + 1 + h, static)
                        at_least(eng, s_hc, kb, n * 2 - 3 + h, static)
                        eng.tensor_tensor_scan(hst[:, 2 * slot + h, :], PS[:, AB[h], :], dBu[:, 2 * slot + h, :],
                                               0.0, ALU.mult, ALU.add).then_inc(s_h, 1)

                    def step(n, slot):
                        static = isinstance(n, int)
                        if not (static and n == NS):
                            scan(n, slot, 0, static)
                        if not (static and n == 0):
                            product(n - 1, 1 - slot, 1, static)
                        if not (static and n == NS):
                            scan(n, slot, 1, static)
                            product(n, slot, 0, static)

                    schedule(eng, step, LEAD)

            with nc.Block() as block:
                @block.tensor
                def _(eng):
                    eng.wait_ge(k_yz, 2 * c + 2)
                    for h in range(2):
                        mm = eng.matmul(PS[:, 2, :], w("WoutT_" + tag)[:, h * 128:(h + 1) * 128], yz[:, h, :],
                                        start=(h == 0), stop=(h == 1))
                    mm.then_inc(k_o, 1)
                    eng.wait_ge(k_fo, c + 1)
                    eng.matmul(PS[:, 3, :], meanw, fo[:, :], start=True, stop=True).then_inc(k_mean, 1)
                    eng.wait_ge(k_sq, c + 1)
                    eng.matmul(PS[:, 4, :], meanw, sq[:, :], start=True, stop=True).then_inc(k_var, 1)
                    if d == 1:
                        eng.wait_ge(k_n, 3 * c + 3)
                        for i in range(2):
                            mm = eng.matmul(PS[:, 5, :], w("WfT")[:, i * 128:(i + 1) * 128], lnout[i][:, :],
                                            start=(i == 0), stop=(i == 1))
                        mm.then_inc(k_fuse, 1)

                @block.scalar
                def _(eng):
                    eng.wait_ge(k_o, c + 1)
                    eng.activation(fo[:, :], PS[:, 2, :], ACT.Copy).then_inc(k_fo, 1)
                    eng.wait_ge(k_cen, c + 1)
                    eng.activation(sq[:, :], cen[:, :], ACT.Square).then_inc(k_sq, 1)
                    eng.wait_ge(k_var, c + 1)
                    eng.activation(sd[:, :], PS[:, 4, :], ACT.Sqrt, bias=eps[:, 0:1]).then_inc(k_sd, 1)

                @block.vector
                def _(eng):
                    for h in range(2):
                        eng.tensor_tensor(yz[:, h, :], sz[:, h, :], PS[:, YB[h], :], ALU.mult).then_inc(k_yz, 1)
                    eng.wait_ge(k_mean, c + 1)
                    eng.tensor_tensor(cen[:, :], fo[:, :], PS[:, 3, :], ALU.subtract).then_inc(k_cen, 1)
                    eng.wait_ge(k_cen, c + 1)
                    eng.wait_ge(k_sd, c + 1)
                    eng.reciprocal(sd[:, :], sd[:, :]).then_inc(k_n, 1)
                    eng.wait_ge(k_n, 3 * c + 1)
                    eng.tensor_tensor(cen[:, :], cen[:, :], sd[:, :], ALU.mult).then_inc(k_n, 1)
                    eng.wait_ge(k_n, 3 * c + 2)
                    dst = lnout[d][:, :].rearrange("p (b t) -> p b t", t=T)
                    eng.tensor_scalar(dst[:, :, ::-1] if d else dst, cen[:, :].rearrange("p (b t) -> p b t", t=T),
                                      col("ln_g", 0), col("ln_b", 0), ALU.mult, ALU.add).then_inc(k_n, 1)
                    if d == 1:
                        eng.wait_ge(k_fuse, th + 1)
                        dst = x1[:, :].rearrange("p (t b) -> p b t", b=B)[:, th * HB:(th + 1) * HB, :]
                        eng.scalar_tensor_tensor(
                            dst, PS[:, 5, :].rearrange("p (b t) -> p b t", t=T), w("bfuse"),
                            xT[:, th * HALF:(th + 1) * HALF].rearrange("p (b t) -> p b t", t=T), ALU.add, ALU.add)\
                           .then_inc(k_x1, 1)

        scopes.pop().close()
        hr = sb("hr", [128, N])
        x2 = sb("x2", [128, N])
        Hs = sb("Hs", [128, N])
        gt = sb("gt", [128, 2, 5, B])
        vv = sb("vv", [128, 2, B])
        tc = sb("tc", [128, B])
        r_pre, r_mm, r_h, r_ffn, r_x2 = (sem("rnn_" + n) for n in ("pre", "mm", "h", "ffn", "x2"))
        l_mm, l_g, l_v, l_c, l_t, l_h = (sem("lstm_" + n) for n in ("mm", "g", "v", "c", "t", "h"))
        l_z = sem("lstm_zero")
        RB, LB, FB = (0, 1), (2, 3), 4

        with nc.Block() as block:
            @block.tensor
            def _(eng):
                ones_row = w("ones")[0:1, 0:CHB]
                for c in range(NCH + 1):
                    rnn, lstm = c < NCH, c >= 1
                    span = slice(c * CHB, (c + 1) * CHB)
                    if rnn:
                        bank = PS[:, RB[c % 2], 0:CHB]
                        if c >= 2:
                            eng.wait_ge(r_h, (c - 1) * CH)
                        eng.matmul(bank, w("WxR"), x1[:, span], start=True, stop=False, skip_group_check=True)
                        eng.matmul(bank, w("bR")[0:1, :], ones_row, start=False, stop=False, skip_group_check=True)
                    for s in range(CH):
                        if lstm:
                            t = (c - 1) * CH + s
                            prev = Hs[:, (t - 1) * B:t * B] if t else H0[:, :]
                            if t:
                                eng.wait_ge(l_h, t)
                            for g in range(G4):
                                mm = eng.matmul(PS[:, LB[(c - 1) % 2], (s * G4 + g) * B:(s * G4 + g + 1) * B],
                                                WhLs[:, g * 128:(g + 1) * 128], prev, start=False, stop=True,
                                                skip_group_check=True)
                            mm.then_inc(l_mm, 1)
                        if rnn:
                            t = c * CH + s
                            if t:
                                eng.wait_ge(r_h, t)
                            eng.matmul(PS[:, RB[c % 2], s * B:(s + 1) * B], w("WhR"),
                                       hr[:, (t - 1) * B:t * B] if t else condT, start=False, stop=True,
                                       skip_group_check=True).then_inc(r_mm, 1)
                    if rnn:
                        eng.wait_ge(r_h, (c + 1) * CH)
                        if c:
                            eng.wait_ge(r_x2, c)
                        eng.matmul(PS[:, FB, 0:CHB], wq[:, :], hr[:, span], start=True, stop=True).then_inc(r_ffn, 1)
                        eng.wait_ge(r_x2, c + 1)
                        if c >= 2:
                            eng.wait_ge(l_g, (c - 1) * CH)
                        gates = PS[:, LB[c % 2], :].rearrange("p (s g b) -> p s g b", g=G4, b=B)
                        for g in range(G4):
                            eng.matmul(gates[:, :, g, :], WxLs[:, g * 128:(g + 1) * 128],
                                       x2[:, span].rearrange("p (s b) -> p s b", b=B), start=(g == 0), stop=False,
                                       skip_group_check=True)
                            eng.matmul(gates[:, :, g, :], bLs[0:1, g * 128:(g + 1) * 128],
                                       ones_row.rearrange("p (s b) -> p s b", b=B), start=False, stop=False,
                                       skip_group_check=True)

            @block.scalar
            def _(eng):
                for c in range(NCH + 1):
                    for s in range(CH):
                        if c >= 1:
                            t = (c - 1) * CH + s
                            eng.wait_ge(l_mm, t + 1)
                            if t >= 2:
                                eng.wait_ge(l_h, t - 1)
                            eng.activation(gt[:, t % 2, 0:G4, :],
                                           PS[:, LB[(c - 1) % 2], s * G4 * B:(s + 1) * G4 * B]
                                           .rearrange("p (g b) -> p g b", b=B), ACT.Tanh).then_inc(l_g, 1)
                        if c < NCH:
                            t = c * CH + s
                            eng.wait_ge(r_mm, t + 1)
                            eng.activation(hr[:, t * B:(t + 1) * B], PS[:, RB[c % 2], s * B:(s + 1) * B], ACT.Tanh)\
                               .then_inc(r_h, 1)
                        if c >= 1:
                            t = (c - 1) * CH + s
                            eng.wait_ge(l_c, t + 1)
                            eng.activation(tc[:, :], gt[:, (t + 1) % 2, 4, :], ACT.Tanh, scale=0.5).then_inc(l_t, 1)

            @block.vector
            def _(eng):
                eng.memset(gt[:, 0, 4, :], 0.0).then_inc(l_z, 1)
                eng.wait_ge(l_z, 1)
                for c in range(NCH + 1):
                    if c >= 1:
                        for s in range(CH):
                            t = (c - 1) * CH + s
                            cur, nxt = gt[:, t % 2, :, :], gt[:, (t + 1) % 2, :, :]
                            eng.wait_ge(l_g, t + 1)
                            eng.scalar_tensor_tensor(vv[:, :, :], cur[:, 0:2, :], 1.0, cur[:, 3:5, :],
                                                     ALU.add, ALU.mult).then_inc(l_v, 1)
                            eng.wait_ge(l_v, t + 1)
                            eng.scalar_tensor_tensor(nxt[:, 4, :], vv[:, 1, :], 0.5, vv[:, 0, :],
                                                     ALU.mult, ALU.add).then_inc(l_c, 1)
                            eng.wait_ge(l_t, t + 1)
                            eng.scalar_tensor_tensor(Hs[:, t * B:(t + 1) * B], cur[:, 2, :], 1.0, tc[:, :],
                                                     ALU.add, ALU.mult).then_inc(l_h, 1)
                    if c < NCH:
                        span = slice(c * CHB, (c + 1) * CHB)
                        eng.wait_ge(r_ffn, c + 1)
                        eng.tensor_tensor(x2[:, span], x1[:, span], PS[:, FB, 0:CHB], ALU.add).then_inc(r_x2, 1)

        rr = sb("rr", [128, N])
        kvs = sb("kvs", [128, N])
        cum = sb("cum", [128, N])
        yy = sb("yy", [128, N])
        x3 = sb("x3", [128, N])
        PAD = (DC - 1) * B
        vp = sb("vp", [128, PAD + N])
        res = sb("res", [128, N])
        tG = sb("tG", [128, 2, 512])
        tM = sb("tM", [128, 2, 512])
        tS = sb("tS", [128, 2, 512])
        r1 = Router("r1", guarded=False)
        a_mm, a_act, a_dve, a_cum, a_ms, a_sd, a_y, a_o = (
            sem("attn_" + n) for n in ("mm", "act", "dve", "cum", "ms", "sd", "y", "o"))
        e_a, e_b, e_g, e_act, e_mul, e_acc, e_x, e_res = (
            sem("ffn_" + n) for n in ("a", "b", "g", "act", "mul", "acc", "x", "res"))
        v_pad = sem("v_pad")
        v_in = sem("v_in")
        stored = sem("stored")

        def bt(ap):
            return ap.rearrange("p (b t) -> p b t", t=T)

        def tb(ap):
            return ap.rearrange("p (t b) -> p b t", b=B)

        def half(ap, h):
            return ap[:, h * 512:(h + 1) * 512]

        with nc.Block() as block:
            @block.tensor
            def _(eng):
                for h in range(2):
                    if h:
                        eng.wait_ge(a_act, 2 * h)
                        eng.wait_ge(a_dve, 2 * h - 1)
                    for bank, name in ((0, "WrT"), (1, "WkT"), (2, "WvT")):
                        eng.matmul(PS[:, bank, :], w(name), half(Hs, h), start=True, stop=True).then_inc(a_mm, 1)
                for h in range(2):
                    eng.wait_ge(a_ms, h + 1)
                    eng.matmul(PS[:, 3 + h, :], meanw, half(kvs, h), start=True, stop=True).then_inc(a_mm, 1)
                for h in range(2):
                    eng.wait_ge(a_y, 3 * h + 3)
                    eng.matmul(PS[:, 5 + h, :], w("WoT"), half(yy, h), start=True, stop=True).then_inc(a_o, 1)
                eng.wait_ge(v_in, 2)
                for t in range(8):
                    mm = eng.matmul(PS[:, 0, t * E:(t + 1) * E], vp[:, PAD + t * 128:PAD + (t + 1) * 128], w("fWr"),
                                    start=(t == 0), stop=True, skip_group_check=True)
                mm.then_inc(r1.logits, 1)

                for j in range(4):
                    h, pair = j // 2, j % 2
                    cols = vp[:, PAD + h * 512:PAD + (h + 1) * 512]
                    if j >= 1:
                        eng.wait_ge(e_act, j)
                        eng.wait_ge(e_mul, 2 * j)
                    eng.matmul(PS[:, 2, :], w("Wg")[:, pair * 128:(pair + 1) * 128], cols, start=True, stop=True)\
                       .then_inc(e_a, 1)
                    eng.matmul(PS[:, 3, :], w("Wu")[:, pair * 128:(pair + 1) * 128], cols, start=True, stop=True)\
                       .then_inc(e_b, 1)
                    if j == 0:
                        r1.pe_turn(eng, 1)
                        eng.wait_ge(r1.gates, 1)
                    eng.matmul(PS[:, 4, :], w("pickpair")[0:3 * E, pair * 128:(pair + 1) * 128],
                               r1.gT[:, h * 512:(h + 1) * 512], start=True, stop=True).then_inc(e_g, 1)
                    eng.wait_ge(e_mul, 2 * j + 2)
                    eng.matmul(PS[:, 5, :] if h == 0 else PS[:, 6, :], w("Wd")[:, pair * 128:(pair + 1) * 128],
                               tS[:, j % 2, :], start=(pair == 0), stop=(pair == 1)).then_inc(e_acc, 1)
                for h in range(2):
                    if h:
                        eng.wait_ge(e_res, 9)
                    eng.matmul(PS[:, 7, :], w("pick46")[0:3 * E, :], r1.gT[:, h * 512:(h + 1) * 512],
                               start=True, stop=True).then_inc(e_x, 1)
                    eng.matmul(PS[:, 0, :], w("pick8")[0:3 * E, 7 * 128:8 * 128], r1.gT[:, h * 512:(h + 1) * 512],
                               start=True, stop=True).then_inc(e_x, 1)

            @block.scalar
            def _(eng):
                for h in range(2):
                    eng.wait_ge(a_mm, 3 * h + 1)
                    eng.activation(half(rr, h), PS[:, 0, :], ACT.Sigmoid, scale=0.5).then_inc(a_act, 1)
                    eng.wait_ge(a_mm, 3 * h + 2)
                    if h:
                        eng.wait_ge(a_dve, 1)
                    eng.activation(half(yy, h), PS[:, 1, :], ACT.Copy, scale=0.25).then_inc(a_act, 1)
                for h in range(2):
                    eng.wait_ge(a_cum, 3 + h)
                    eng.activation(half(kvs, h), half(yy, h), ACT.Square).then_inc(a_ms, 1)
                for h in range(2):
                    eng.wait_ge(a_mm, 6 + h + 1)
                    eng.activation(half(kvs, h), PS[:, 3 + h, :], ACT.Sqrt, bias=eps[:, 1:2]).then_inc(a_sd, 1)
                r1.act(eng, 0)
                for j in range(4):
                    eng.wait_ge(e_a, j + 1)
                    if j >= 2:
                        eng.wait_ge(e_mul, 2 * j - 3)
                    eng.activation(tG[:, j % 2, :], PS[:, 2, :], ACT.Silu).then_inc(e_act, 1)

            @block.vector
            def _(eng):
                eng.memset(vp[:, 0:PAD], 0.0).then_inc(v_pad, 1)
                for h in range(2):
                    eng.wait_ge(a_act, 2 * h + 2)
                    eng.wait_ge(a_mm, 3 * h + 3)
                    eng.tensor_tensor(half(yy, h), half(yy, h), PS[:, 2, :], ALU.mult).then_inc(a_dve, 1)
                    eng.wait_ge(a_dve, 2 * h + 1)
                    ts = slice(h * 64, (h + 1) * 64)
                    eng.tensor_tensor(bt(kvs[:, :])[:, :, ts], tb(half(yy, h)),
                                      dinv[:, ts].unsqueeze(1).to_broadcast([128, B, 64]), ALU.mult)\
                       .then_inc(a_dve, 1)
                eng.wait_ge(a_dve, 4)
                eng.tensor_tensor_scan(cum[:, :], w("keep"), kvs[:, :], 0.0, ALU.mult, ALU.add).then_inc(a_cum, 1)
                eng.wait_ge(a_cum, 1)
                eng.tensor_tensor(bt(cum[:, :]), bt(cum[:, :]), dscale[:, :].unsqueeze(1).to_broadcast([128, B, T]),
                                  ALU.mult).then_inc(a_cum, 1)
                eng.wait_ge(a_cum, 2)
                for h in range(2):
                    eng.tensor_tensor(tb(half(yy, h)), tb(half(rr, h)), bt(cum[:, :])[:, :, h * 64:(h + 1) * 64],
                                      ALU.mult).then_inc(a_cum, 1)
                for h in range(2):
                    eng.wait_ge(a_sd, h + 1)
                    eng.reciprocal(half(kvs, h), half(kvs, h)).then_inc(a_y, 1)
                    eng.wait_ge(a_y, 3 * h + 1)
                    eng.tensor_scalar(half(yy, h), half(yy, h), w("ln_w"), None, ALU.mult).then_inc(a_y, 1)
                    eng.wait_ge(a_y, 3 * h + 2)
                    eng.tensor_tensor(half(yy, h), half(yy, h), half(kvs, h), ALU.mult).then_inc(a_y, 1)
                for h in range(2):
                    eng.wait_ge(a_o, h + 1)
                    eng.tensor_tensor(half(x3, h), half(x2, h), PS[:, 5 + h, :], ALU.add).then_inc(v_pad, 1)
                    eng.wait_ge(v_pad, h + 2)
                    eng.tensor_tensor(vp[:, PAD + h * 512:PAD + (h + 1) * 512].rearrange("p (t b) -> p t b", b=B),
                                      half(x3, h).rearrange("p (t b) -> p t b", b=B),
                                      g1[:, :].unsqueeze(1).to_broadcast([128, 64, B]), ALU.mult).then_inc(v_in, 1)
                r1.dve(eng, w("frb"), 1)
                for j in range(4):
                    eng.wait_ge(e_act, j + 1)
                    eng.wait_ge(e_b, j + 1)
                    eng.tensor_tensor(tM[:, j % 2, :], tG[:, j % 2, :], PS[:, 3, :], ALU.mult).then_inc(e_mul, 1)
                    eng.wait_ge(e_mul, 2 * j + 1)
                    eng.wait_ge(e_g, j + 1)
                    if j >= 2:
                        eng.wait_ge(e_acc, j - 1)
                    eng.tensor_tensor(tS[:, j % 2, :], tM[:, j % 2, :], PS[:, 4, :], ALU.mult).then_inc(e_mul, 1)
                n = 0

                def after(ins):
                    nonlocal n
                    n += 1
                    ins.then_inc(e_res, 1)
                    eng.wait_ge(e_res, n)

                a0 = PACK1["fcw"][0]
                for h in range(2):
                    o = half(res, h)
                    v = vp[:, PAD + h * 512:PAD + (h + 1) * 512]

                    def tap(k):
                        return vp[:, h * 512 + k * B:(h + 1) * 512 + k * B], p1[:, a0 + k:a0 + k + 1]

                    after(eng.tensor_scalar(o, tap(0)[0], tap(0)[1], w("fcb"), ALU.mult, ALU.add))
                    for k in range(1, DC):
                        after(eng.scalar_tensor_tensor(o, tap(k)[0], tap(k)[1], o, ALU.mult, ALU.add))
                    after(eng.tensor_tensor(o, o, half(x3, h), ALU.add))
                    eng.wait_ge(e_acc, 2 * h + 2)
                    after(eng.tensor_tensor(o, o, PS[:, 5 + h, :], ALU.add))
                    eng.wait_ge(e_x, 2 * h + 2)
                    after(eng.tensor_tensor(tM[:, 0, :], v, PS[:, 7, :], ALU.mult))
                    after(eng.scalar_tensor_tensor(tM[:, 1, :], v, 0.0, PS[:, 0, :], ALU.max, ALU.mult))
                    after(eng.tensor_tensor(o, o, tM[:, 0, :], ALU.add))
                    after(eng.tensor_tensor(o, o, tM[:, 1, :], ALU.add))

            @block.sync
            def _(eng):
                for h in range(2):
                    eng.wait_ge(e_res, 10 * (h + 1))
                    eng.dma_start(half(out, h), half(res, h)).then_inc(stored, 16)
                eng.wait_ge(stored, 32)


def kernel(**inputs):
    import numpy as np
    import ml_dtypes
    import concourse.bacc as bacc
    from concourse.bass_utils import run_bass_kernel_spmd

    x = {k: np.asarray(v) for k, v in inputs.items()}

    def packed(place, width, parts):
        a = np.zeros((128, width), np.float32)
        for name, v in parts.items():
            lo, hi = place[name]
            v = np.asarray(v)
            v = v.reshape(v.shape[0], -1)
            a[:v.shape[0], lo:lo + v.shape[1]] = v
        return a

    def blocks(m, rows=128):
        return m.reshape(-1, rows, m.shape[1]).transpose(1, 0, 2)

    def row128(v):
        return np.broadcast_to(v[None, :], (128, v.shape[0]))

    m0 = {
        "xT": x["x"].reshape(N, D).T, "condT": x["cond_1024"].T,
        "RWx": x["L0_cond_router_W"][0:D], "RWt": x["L0_cond_router_W"][D:], "rbias": row128(x["L0_cond_router_bias"]),
        "w1": x["L0_cond_w1"], "w3": x["L0_cond_w3"], "w2": blocks(x["L0_cond_w2"]),
        "W1e": x["L0_cond_W1e"].transpose(1, 0, 2), "W2e": x["L0_cond_W2e"].transpose(1, 0, 2),
    }
    m1 = {}
    for t in "fb":
        g = {k[len("L0_attn_"):-2]: v for k, v in x.items() if k.startswith("L0_attn_") and k.endswith("_" + t)}
        wx = g["Wx"].T
        three = lambda m: np.concatenate([m, m, m], axis=1)
        m1.update({k + "_" + t: v for k, v in {
            "WinT": g["Win"].T, "WxdT": blocks(wx[:, 0:DR]), "WxB": blocks(three(wx[:, DR:DR + NS])),
            "WxC": blocks(three(wx[:, DR + NS:])), "WdtT": g["Wdt"].T, "WoutT": blocks(g["Wout"].T),
            "Alog": blocks(g["Alog"]), "convw": blocks(g["convw"]), "convb": blocks(g["convb"][:, None]),
            "bdt": blocks(g["bdt"][:, None]), "Dp": blocks(g["Dp"][:, None]),
            "ln_g": g["ln_g"][:, None], "ln_b": g["ln_b"][:, None]}.items()})
    pairs = lambda m: m.transpose(1, 0, 2)
    m1.update({
        "WfT": blocks(x["L0_attn_Wfuse"].T), "bfuse": x["L0_attn_bfuse"][:, None],
        "WxR": x["L0_cond2_Wx"], "WhR": x["L0_cond2_Wh"], "bR": x["L0_cond2_b"][None, :],
        "WqT": x["L0_ffn_weight"].T, "WxL": x["L1_cond_Wx"], "WhL": x["L1_cond_Wh"], "bL": x["L1_cond_b"][None, :],
        "WrT": x["L1_attn_Wr"].T, "WkT": x["L1_attn_Wk"].T, "WvT": x["L1_attn_Wv"].T, "WoT": x["L1_attn_Wo"].T,
        "decay": x["L1_attn_decay"][:, None], "ln_w": x["L1_attn_ln_w"][:, None],
        "C1T": x["L1_cond2_W1"].T, "C2T": x["L1_cond2_W2"].T, "cb1": x["L1_cond2_b1"][:, None],
        "cb2": x["L1_cond2_b2"][:, None], "fWr": x["L1_ffn_Wr"], "frb": row128(x["L1_ffn_router_bias"]),
        "Wg": pairs(x["L1_ffn_Wg"]), "Wu": pairs(x["L1_ffn_Wu"]),
        "Wd": blocks(x["L1_ffn_Wd"].reshape(256, D)), "fcw": x["L1_ffn_conv_w"].reshape(DC, D).T,
        "fcb": x["L1_ffn_conv_b"][:, None],
    })
    eye = np.eye(128, dtype=np.float32)
    keep = np.ones((128, B, T), np.float32)
    keep[:, :, 0] = 0
    mf = {"ident": eye, "mean": np.full((128, 128), 1.0 / 128, np.float32), "ones": np.ones((128, 128), np.float32),
          "iota8": row128(np.arange(E, dtype=np.float32)), "iotat": row128(np.arange(T, dtype=np.float32)),
          "keep": keep}
    pick32 = np.zeros((96, NS, 128), np.float32)
    for n in range(NS):
        pick32[[n, NS + n, 2 * NS + n], n, :] = 1
    pick8 = np.zeros((3 * E, E, 128), np.float32)
    for e in range(E):
        pick8[[e, E + e, 2 * E + e], e, :] = 1
    pickpair = np.concatenate([pick8[:, e, 0:64] for e in range(4)], axis=1)
    mb = {"identb": eye, "pick32": pick32, "pick8": pick8, "pick46": pick8[:, 4] + pick8[:, 6], "pickpair": pickpair}
    arrays = {
        "pack0": packed(PACK0, W0, m0), "pack1": packed(PACK1, W1, m1), "conf": packed(CONF, WF, mf),
        "conb": packed(CONB, WB, mb).astype(ml_dtypes.bfloat16),
    }
    nc = bacc.Bacc("TRN2", target_bir_lowering=False, num_devices=1)
    args = [nc.dram_tensor(k, v.shape, mybir.dt.from_np(v.dtype), kind="ExternalInput").ap() for k, v in arrays.items()]
    out = nc.dram_tensor("y", (128, N), F32, kind="ExternalOutput").ap()
    build(nc, *args, out)
    r = run_bass_kernel_spmd(nc, [arrays], core_ids=[0])
    y = r.results[0]["y"]
    return np.ascontiguousarray(np.asarray(y).reshape(D, T, B).transpose(2, 1, 0))
```

```python
from contextlib import ExitStack

import concourse.bass as bass
from concourse import mybir

F32 = mybir.dt.float32
BF16 = mybir.dt.bfloat16
F16 = mybir.dt.float16
U32 = mybir.dt.uint32
ALU = mybir.AluOpType
ACT = mybir.ActivationFunctionType
AX_X = mybir.AxisListType.X

B, T, D = 8, 128, 128
N = B * T
HALF = N // 2
HB = B // 2
DI, NS, DC, DR = 256, 32, 4, 8
HS, E = 256, 8
G4 = 4
CH = 8
NCH = T // CH
CHB = CH * B
LEAD, PAIRS = 3, 13
LIFT = 2.0 ** 14
FAR = 1.0e24


def columns(parts):
    at, place = 0, {}
    for name, width in parts:
        place[name] = (at, at + width)
        at += width
    return place, at


MAMBA = [("WinT", 2 * DI), ("WxdT", 2 * DR), ("WxB", 2 * 96), ("WxC", 2 * 96), ("WdtT", DI),
         ("WoutT", 2 * D), ("Alog", 2 * NS), ("convw", 2 * DC), ("convb", 2), ("bdt", 2), ("Dp", 2),
         ("ln_g", 1), ("ln_b", 1)]
PACK0, W0 = columns([("xT", N), ("condT", B), ("RWx", E), ("RWt", E), ("rbias", E), ("w1", HS), ("w3", HS),
                     ("w2", HS), ("W1e", E * 128), ("W2e", E * 128)])
PACK1, W1 = columns([(f"{n}_{d}", w) for d in "fb" for n, w in MAMBA]
                    + [("WfT", 2 * D), ("bfuse", 1), ("WxR", D), ("WhR", D), ("bR", 1), ("WqT", D),
                       ("WxL", 4 * D), ("WhL", 4 * D), ("bL", D), ("WrT", D), ("WkT", D), ("WvT", D),
                       ("WoT", D), ("decay", 1), ("ln_w", 1), ("C1T", D), ("C2T", D), ("cb1", 1), ("cb2", 1),
                       ("fWr", E), ("frb", E), ("Wg", 256), ("Wu", 256), ("Wd", 256), ("fcw", DC), ("fcb", 1)])
CONF, WF = columns([("ident", 128), ("mean", 128), ("ones", 128), ("iota8", E), ("iotat", T), ("keep", N),
                     ("gate_lift", 1), ("gate_rows", G4 * CHB)])
CONB, WB = columns([("identb", 128), ("pick32", NS * 128), ("pick8", E * 128), ("pick46", 128),
                    ("pickpair", 256)])


def build(nc, pack0, pack1, conf, conb, out):
    ctx = ExitStack()
    with ctx:
        scopes = [ctx]

        def sb(name, shape, dt=F32):
            return scopes[-1].enter_context(nc.sbuf_tensor(name, shape, dt))

        def sem(name):
            return ctx.enter_context(nc.semaphore(name))

        p0 = sb("p0", [128, W0])
        p1 = sb("p1", [128, W1])
        cf = sb("cf", [128, WF])
        cb = sb("cb", [128, WB], BF16)
        PS = ctx.enter_context(nc.psum_tensor("PS", [128, 8, 512], F32))

        def w(name):
            for src, place in ((p0, PACK0), (p1, PACK1), (cf, CONF), (cb, CONB)):
                if name in place:
                    a, b = place[name]
                    return src[:, a:b]
            raise KeyError(name)

        xT = w("xT")
        condT = w("condT")
        ident = w("ident")
        meanw = w("mean")
        pick32 = w("pick32")

        uin = [sb("uin_f", [128, N]), sb("uin_r", [128, N])]
        lnout = [sb("ln_fwd", [128, HALF]), sb("ln_bwd", [128, HALF])]
        x1 = sb("x1", [128, N])
        Aneg = sb("Aneg", [128, 2, 2 * NS])
        diagD = sb("diagD", [128, 2, 2, 128])
        wq = sb("wq", [128, D])
        g1 = sb("g1", [128, B])
        WxLs = sb("WxLs", [128, 4 * D])
        WhLs = sb("WhLs", [128, 4 * D])
        bLs = sb("bLs", [128, D])
        Wh3 = sb("Wh3", [128, 3, 4 * D], BF16)
        wrest = sb("wrest", [128, 4 * D])
        H0 = sb("H0", [128, B])
        dscale = sb("dscale", [128, T])
        dinv = sb("dinv", [128, T])
        up = sb("up", [128, 2, HB, DC - 1 + T])

        class Router:

            def __init__(self, name, guarded):
                self.guarded = guarded
                self.s = sb(name + "_s", [128, 8, E])
                self.sel = sb(name + "_sel", [128, 8, E])
                self.top = sb(name + "_top", [128, 8, 8])
                self.idx = sb(name + "_idx", [128, 8, 8], U32)
                self.idf = sb(name + "_idf", [128, 8, 2])
                self.hot = sb(name + "_hot", [128, 8, 2, E])
                self.mask = sb(name + "_mask", [128, 8, E])
                self.ss = sb(name + "_ss", [128, 8, E])
                self.den = sb(name + "_den", [128, 8])
                self.rec = sb(name + "_rec", [128, 8])
                self.flag = sb(name + "_flag", [128, 8])
                self.comb = sb(name + "_comb", [128, 8, E])
                self.rest = sb(name + "_rest", [128, 8, E])
                self.parts = sb(name + "_parts", [128, 8, 3 * E], BF16)
                self.gT = sb(name + "_gT", [3 * E, N], BF16)
                self.logits = sem(name + "_logits")
                self.scored = sem(name + "_scored")
                self.step = sem(name + "_step")
                self.turned = sem(name + "_turned")
                self.gates = sem(name + "_gates")

            def act(self, eng, bank):
                eng.wait_ge(self.logits, 1)
                eng.activation(self.s[:, :, :], PS[:, bank, 0:8 * E].rearrange("p (t e) -> p t e", e=E),
                               ACT.Sigmoid).then_inc(self.scored, 1)

            def dve(self, eng, bias, bank):
                done = [0]

                def after(ins):
                    done[0] += 1
                    ins.then_inc(self.step, 1)
                    eng.wait_ge(self.step, done[0])

                eng.wait_ge(self.scored, 1)
                after(eng.tensor_tensor(self.sel[:, :, :], self.s[:, :, :],
                                        bias.unsqueeze(1).to_broadcast([128, 8, E]), ALU.add))
                for t in range(8):
                    done[0] += 1
                    eng.max(self.top[:, t, :], self.sel[:, t, :]).then_inc(self.step, 1)
                eng.wait_ge(self.step, done[0])
                for t in range(8):
                    done[0] += 1
                    eng.max_index(self.idx[:, t, :], self.top[:, t, :], self.sel[:, t, :]).then_inc(self.step, 1)
                eng.wait_ge(self.step, done[0])
                after(eng.tensor_copy(self.idf[:, :, :], self.idx[:, :, 0:2]))
                iota = w("iota8").unsqueeze(1).unsqueeze(1).to_broadcast([128, 8, 2, E])
                after(eng.tensor_tensor(self.hot[:, :, :, :], iota,
                                        self.idf[:, :, :].unsqueeze(3).to_broadcast([128, 8, 2, E]), ALU.is_equal))
                after(eng.tensor_tensor(self.mask[:, :, :], self.hot[:, :, 0, :], self.hot[:, :, 1, :], ALU.add))
                after(eng.tensor_tensor(self.ss[:, :, :], self.s[:, :, :], self.mask[:, :, :], ALU.mult))
                after(eng.tensor_reduce(self.den[:, :], self.ss[:, :, :], AX_X, ALU.add))
                after(eng.tensor_scalar(self.rec[:, :], self.den[:, :], 1e-9, None, ALU.add))
                after(eng.reciprocal(self.rec[:, :], self.rec[:, :]))
                if self.guarded:
                    after(eng.tensor_scalar(self.flag[:, :], self.den[:, :], 1e-9, None, ALU.is_gt))
                    after(eng.tensor_tensor(self.rec[:, :], self.rec[:, :], self.flag[:, :], ALU.mult))
                    after(eng.tensor_scalar(self.flag[:, :], self.flag[:, :], -0.5, 0.5, ALU.mult, ALU.add))
                after(eng.tensor_tensor(self.comb[:, :, :], self.ss[:, :, :],
                                        self.rec[:, :].unsqueeze(2).to_broadcast([128, 8, E]), ALU.mult))
                if self.guarded:
                    after(eng.tensor_tensor(self.mask[:, :, :], self.mask[:, :, :],
                                            self.flag[:, :].unsqueeze(2).to_broadcast([128, 8, E]), ALU.mult))
                    after(eng.tensor_tensor(self.comb[:, :, :], self.comb[:, :, :], self.mask[:, :, :], ALU.add))
                after(eng.tensor_copy(self.parts[:, :, 0:E], self.comb[:, :, :]))
                after(eng.tensor_tensor(self.rest[:, :, :], self.comb[:, :, :], self.parts[:, :, 0:E], ALU.subtract))
                after(eng.tensor_copy(self.parts[:, :, E:2 * E], self.rest[:, :, :]))
                after(eng.tensor_tensor(self.parts[:, :, 2 * E:3 * E], self.rest[:, :, :],
                                        self.parts[:, :, E:2 * E], ALU.subtract))
                self.n_steps = done[0]
                eng.wait_ge(self.turned, 1)
                eng.tensor_copy(self.gT[:, :], PS[0:3 * E, bank, :].bitcast(BF16)).then_inc(self.gates, 1)

            def pe_turn(self, eng, bank):
                n = 1 + 8 + 8 + 7 + (5 if self.guarded else 0) + 1 + 4
                eng.wait_ge(self.step, n)
                turned = PS[0:3 * E, bank, :].bitcast(BF16)
                for t in range(8):
                    mm = eng.transpose(turned[:, t * 128:(t + 1) * 128], self.parts[:, t, :], w("identb"))
                mm.then_inc(self.turned, 1)

        loaded = [sem(f"loaded{i}") for i in range(4)]
        prep_act = sem("prep_act")
        prep_dve = sem("prep_dve")
        prep_pe = sem("prep_pe")
        pads = sem("pads")
        absw = sb("absw", [128, D])
        asum = sb("asum", [128, 1])
        qscale = sb("qscale", [128, 1])
        qthr = sb("qthr", [128, 2])
        qneg = sb("qneg", [128, D])
        sgd = sb("sgd", [128, 1])
        ldec = sb("ldec", [128, 1])
        c2h = sb("c2h", [128, B])
        gate = sb("gate", [128, B])
        eps = sb("eps", [128, 3])

        with nc.Block() as block:
            @block.sync
            def _(eng):
                eng.dma_start(p0[:, 0:1024 + 32], pack0[:, 0:1024 + 32]).then_inc(loaded[0], 16)
                eng.dma_start(cb[:, :], conb).then_inc(loaded[3], 16)
                eng.dma_start(cf[:, :], conf).then_inc(loaded[2], 16)
                eng.dma_start(p0[:, 1024 + 32:], pack0[:, 1024 + 32:]).then_inc(loaded[0], 16)
                eng.dma_start(p1[:, :], pack1).then_inc(loaded[1], 16)
                for s, n in zip(loaded, (32, 16, 16, 16)):
                    eng.wait_ge(s, n)

            @block.gpsimd
            def _(eng):
                eng.memset(up[:, :, :, :], 0.0).then_inc(pads, 1)
                eng.memset(eps[:, 0:1], 1e-5).then_inc(pads, 1)
                eng.memset(eps[:, 1:2], 1e-6).then_inc(pads, 1)
                eng.memset(eps[:, 2:3], 1.0).then_inc(pads, 1)

            @block.scalar
            def _(eng):
                eng.wait_ge(loaded[1], 16)
                eng.wait_ge(loaded[2], 16)
                eng.wait_ge(pads, 4)
                eng.activation(absw[:, :], w("WqT"), ACT.Abs).then_inc(prep_act, 1)
                for d, tag in enumerate("fb"):
                    eng.activation(Aneg[:, d, :], w("Alog_" + tag), ACT.Exp).then_inc(prep_act, 1)
                eng.activation(sgd[:, :], w("decay"), ACT.Sigmoid).then_inc(prep_act, 1)
                eng.wait_ge(prep_dve, 1)
                eng.activation(ldec[:, :], sgd[:, :], ACT.Ln).then_inc(prep_act, 1)
                eng.wait_ge(prep_act, 5)
                eng.activation(dscale[:, :], w("iotat"), ACT.Exp, scale=ldec[:, 0:1]).then_inc(prep_act, 1)
                eng.wait_ge(prep_pe, 1)
                eng.activation(c2h[:, :], PS[:, 0, 0:B], ACT.Silu, bias=w("cb1")).then_inc(prep_act, 1)
                eng.wait_ge(prep_pe, 2)
                eng.activation(gate[:, :], PS[:, 1, 0:B], ACT.Sigmoid, bias=w("cb2")).then_inc(prep_act, 1)

            @block.tensor
            def _(eng):
                eng.wait_ge(loaded[1], 16)
                eng.wait_ge(loaded[2], 16)
                eng.wait_ge(loaded[0], 32)
                eng.matmul(PS[:, 0, 0:B], w("C1T"), condT, start=True, stop=True).then_inc(prep_pe, 1)
                eng.wait_ge(prep_act, 7)
                eng.matmul(PS[:, 1, 0:B], w("C2T"), c2h[:, :], start=True, stop=True).then_inc(prep_pe, 1)
                eng.wait_ge(prep_dve, 2)
                eng.matmul(PS[:, 2, 0:1], w("ones"), asum[:, :], start=True, stop=True).then_inc(prep_pe, 1)

            @block.vector
            def _(eng):
                eng.wait_ge(loaded[1], 16)
                eng.wait_ge(loaded[2], 16)
                eng.wait_ge(loaded[0], 32)
                eng.wait_ge(prep_act, 4)
                eng.tensor_scalar(sgd[:, :], sgd[:, :], 1e-7, None, ALU.max).then_inc(prep_dve, 1)
                eng.tensor_reduce(asum[:, :], absw[:, :], AX_X, ALU.add).then_inc(prep_dve, 1)
                eng.tensor_scalar(Aneg[:, :, :], Aneg[:, :, :], -1.0, None, ALU.mult).then_inc(prep_dve, 1)
                n = 3
                for d, tag in enumerate("fb"):
                    for h in range(2):
                        a = PACK1["Dp_" + tag][0] + h
                        eng.tensor_scalar(diagD[:, d, h, :], ident, p1[:, a:a + 1], None, ALU.mult)\
                           .then_inc(prep_dve, 1)
                        n += 1
                L = 3 * D
                eng.tensor_scalar(WxLs[:, 0:L], w("WxL")[:, 0:L], LIFT / 2, None, ALU.mult).then_inc(prep_dve, 1)
                eng.tensor_scalar(WxLs[:, L:], w("WxL")[:, L:], LIFT, None, ALU.mult).then_inc(prep_dve, 1)
                eng.tensor_scalar(WhLs[:, 0:L], w("WhL")[:, 0:L], 0.5, None, ALU.mult).then_inc(prep_dve, 1)
                eng.tensor_copy(WhLs[:, L:], w("WhL")[:, L:]).then_inc(prep_dve, 1)
                eng.tensor_scalar(bLs[0:G4, :], w("bL")[0:G4, :], w("gate_lift")[0:G4, :], None, ALU.mult)\
                   .then_inc(prep_dve, 1)
                eng.tensor_scalar(H0[:, :], condT, LIFT, None, ALU.mult).then_inc(prep_dve, 1)
                n += 6
                for i in range(3):
                    eng.wait_ge(prep_dve, n)
                    left = WhLs if i == 0 else wrest
                    eng.tensor_copy(Wh3[:, i, :], left[:, :]).then_inc(prep_dve, 1)
                    n += 1
                    if i < 2:
                        eng.wait_ge(prep_dve, n)
                        eng.tensor_tensor(wrest[:, :], left[:, :], Wh3[:, i, :], ALU.subtract).then_inc(prep_dve, 1)
                        n += 1
                eng.wait_ge(prep_act, 6)
                eng.tensor_scalar(dinv[:, :], dscale[:, :], 1e-10, None, ALU.max).then_inc(prep_dve, 1)
                n += 1
                eng.wait_ge(prep_dve, n)
                eng.reciprocal(dinv[:, :], dinv[:, :]).then_inc(prep_dve, 1)
                n += 1
                eng.wait_ge(prep_pe, 3)
                eng.tensor_scalar(qscale[:, :], PS[:, 2, 0:1], 1.0 / (D * D), 1e-5, ALU.mult, ALU.max)\
                   .then_inc(prep_dve, 1)
                n += 1
                eng.wait_ge(prep_dve, n)
                eng.tensor_scalar(qthr[:, 0:1], qscale[:, :], 0.5, None, ALU.mult).then_inc(prep_dve, 1)
                eng.tensor_scalar(qthr[:, 1:2], qscale[:, :], -0.5, None, ALU.mult).then_inc(prep_dve, 1)
                n += 2
                eng.wait_ge(prep_dve, n)
                eng.tensor_scalar(wq[:, :], w("WqT"), qthr[:, 0:1], qscale[:, 0:1], ALU.is_gt, ALU.mult)\
                   .then_inc(prep_dve, 1)
                eng.tensor_scalar(qneg[:, :], w("WqT"), qthr[:, 1:2], qscale[:, 0:1], ALU.is_lt, ALU.mult)\
                   .then_inc(prep_dve, 1)
                n += 2
                eng.wait_ge(prep_dve, n)
                eng.tensor_tensor(wq[:, :], wq[:, :], qneg[:, :], ALU.subtract).then_inc(prep_dve, 1)
                eng.wait_ge(prep_act, 8)
                eng.tensor_scalar(g1[:, :], gate[:, :], 1.0, None, ALU.add).then_inc(prep_dve, 1)

        units = [(th, "shared", m) for th in range(2) for m in range(2)]
        units += [(th, "expert", e) for th in range(2) for e in range(E)]
        scopes.append(ExitStack())
        r0 = Router("r0", guarded=True)
        m_a, m_b, m_act, m_mul, m_acc, m_in, m_rev = (sem("moe_" + n)
                                                  for n in ("a", "b", "act", "mul", "acc", "in", "rev"))
        mG = sb("mG", [128, 2, 512])
        mS = sb("mS", [128, 2, 512])
        first = {th: min(j for j, u in enumerate(units) if u[0] == th) for th in range(2)}
        last = {th: max(j for j, u in enumerate(units) if u[0] == th) for th in range(2)}

        with nc.Block() as block:
            @block.tensor
            def _(eng):
                for t in range(8):
                    eng.matmul(PS[:, 0, t * E:(t + 1) * E], xT[:, t * 128:(t + 1) * 128], w("RWx"),
                               start=(t == 0), stop=False, skip_group_check=True)
                    mm = eng.matmul(PS[:, 0, t * E:(t + 1) * E], condT[:, t:t + 1].to_broadcast([128, 128]),
                                    w("RWt"), start=False, stop=True, skip_group_check=True)
                mm.then_inc(r0.logits, 1)

                def accumulate(j):
                    th, kind, i = units[j]
                    wt = w("w2" if kind == "shared" else "W2e")[:, i * 128:(i + 1) * 128]
                    eng.wait_ge(m_mul, j + 1)
                    eng.matmul(PS[:, 6 + th, :], wt, mS[:, j % 2, :], start=(j == first[th]),
                               stop=(j == last[th]), skip_group_check=True).then_inc(m_acc, 1)

                for j, (th, kind, i) in enumerate(units):
                    cols = xT[:, th * HALF:(th + 1) * HALF]
                    if j >= 2:
                        eng.wait_ge(m_act, j - 1)
                    wt = w("w1" if kind == "shared" else "W1e")[:, i * 128:(i + 1) * 128]
                    eng.matmul(PS[:, 2 + j % 2, :], wt, cols, start=True, stop=True).then_inc(m_a, 1)
                    if (kind, th, i) == ("expert", 0, 0):
                        r0.pe_turn(eng, 1)
                        eng.wait_ge(r0.gates, 1)
                    if j >= 2:
                        eng.wait_ge(m_mul, j - 1)
                    if kind == "shared":
                        eng.matmul(PS[:, 4 + j % 2, :], w("w3")[:, i * 128:(i + 1) * 128], cols,
                                   start=True, stop=True).then_inc(m_b, 1)
                    else:
                        eng.matmul(PS[:, 4 + j % 2, :], w("pick8")[0:3 * E, i * 128:(i + 1) * 128],
                                   r0.gT[:, th * HALF:(th + 1) * HALF], start=True, stop=True).then_inc(m_b, 1)
                    if j:
                        accumulate(j - 1)
                accumulate(len(units) - 1)

            @block.scalar
            def _(eng):
                r0.act(eng, 0)
                for j, (th, kind, i) in enumerate(units):
                    eng.wait_ge(m_a, j + 1)
                    if j >= 2:
                        eng.wait_ge(m_mul, j - 1)
                    eng.activation(mG[:, j % 2, :], PS[:, 2 + j % 2, :],
                                   ACT.Silu if kind == "shared" else ACT.Gelu).then_inc(m_act, 1)
                for th in range(2):
                    eng.wait_ge(m_in, th + 1)
                    a, b = th * HALF, (th + 1) * HALF
                    eng.activation(uin[1][:, a:b].rearrange("p (b t) -> p b t", t=T),
                                   uin[0][:, a:b].rearrange("p (b t) -> p b t", t=T)[:, :, ::-1], ACT.Copy)\
                       .then_inc(m_rev, 1)

            @block.vector
            def _(eng):
                def multiply(j):
                    eng.wait_ge(m_act, j + 1)
                    eng.wait_ge(m_b, j + 1)
                    if j >= 2:
                        eng.wait_ge(m_acc, j - 1)
                    eng.tensor_tensor(mS[:, j % 2, :], mG[:, j % 2, :], PS[:, 4 + j % 2, :], ALU.mult)\
                       .then_inc(m_mul, 1)

                for j in range(3):
                    multiply(j)
                r0.dve(eng, w("rbias"), 1)
                for j in range(3, len(units)):
                    multiply(j)
                for th in range(2):
                    eng.wait_ge(m_acc, last[th] + 1)
                    eng.tensor_scalar(uin[0][:, th * HALF:(th + 1) * HALF], PS[:, 6 + th, :], 1.0 / 3.0, None,
                                      ALU.mult).then_inc(m_in, 1)

        uc = sb("uc", [128, 2, HALF])
        cv = sb("cv", [128, 2, HALF])
        sz = sb("sz", [128, 2, HALF])
        dtr = sb("dtr", [DR, HALF])
        dt_ = sb("dt", [128, 2, HALF])
        dtu = sb("dtu", [128, 2, HALF])
        spv = sb("spv", [128, 2, HALF])
        spe = sb("spe", [128, 2, HALF])
        spl = sb("spl", [128, 2, HALF])
        spq = sb("spq", [128, 2, HALF])
        bc3 = [sb("b3", [96, HALF], BF16), sb("c3", [96, HALF], BF16)]
        rest = sb("rest", [96, HALF])
        mid = sb("mid", [96, HALF], BF16)
        Bsb = sb("Bsb", [128, 2, HALF])
        dBu = sb("dBu", [128, 4, HALF])
        hst = sb("hst", [128, 4, HALF])
        hC = sb("hC", [128, 4, HALF])
        yz = sb("yz", [128, 2, HALF])
        fo = sb("fo", [128, HALF])
        cen = sb("cen", [128, HALF])
        sq = sb("sq", [128, HALF])
        sd = sb("sd", [128, HALF])

        f_xz, f_u, f_z, f_conv, f_uc, f_dbl, f_dtr, f_dtp, f_sp, f_hi, f_v = (
            sem("front_" + n) for n in ("xz", "u", "z", "conv", "uc", "dbl", "dtr", "dtp", "sp", "hi", "v"))
        s_b, s_c, s_bc, s_da, s_dbu, s_h, s_hc, s_y = (
            sem("scan_" + n) for n in ("b", "c", "bcopy", "dA", "dBu", "h", "hC", "y"))
        k_yz, k_o, k_fo, k_mean, k_cen, k_sq, k_var, k_sd, k_n, k_fuse, k_x1 = (
            sem("back_" + n) for n in ("yz", "o", "fo", "mean", "cen", "sq", "var", "sd", "n", "fuse", "x1"))
        YB, CB, BB, AB = (0, 1), (2, 3), (4, 7), (5, 6)

        for c, (th, d) in enumerate((th, d) for th in range(2) for d in range(2)):
            tag = "fb"[d]
            cols = uin[d][:, th * HALF:(th + 1) * HALF]

            def col(name, i, tag=tag):
                a = PACK1[name + "_" + tag][0] + i
                return p1[:, a:a + 1]

            with nc.Block() as block:
                @block.tensor
                def _(eng):
                    for q in range(4):
                        eng.matmul(PS[:, q, :], w("WinT_" + tag)[:, q * 128:(q + 1) * 128], cols,
                                   start=True, stop=True).then_inc(f_xz, 1)
                    eng.wait_ge(f_uc, 2 * c + 2)
                    for bank, name, m in ((4, "WxdT_", DR), (5, "WxB_", 96), (6, "WxC_", 96)):
                        for h in range(2):
                            mm = eng.matmul(PS[0:m, bank, :], w(name + tag)[:, h * m:(h + 1) * m], uc[:, h, :],
                                            start=(h == 0), stop=(h == 1))
                        mm.then_inc(f_dbl, 1)
                    eng.wait_ge(f_dtr, c + 1)
                    eng.wait_ge(f_u, 2 * c + 2)
                    for h in range(2):
                        eng.matmul(PS[:, h, :], w("WdtT_" + tag)[0:DR, h * 128:(h + 1) * 128], dtr[:, :],
                                   start=True, stop=True).then_inc(f_dtp, 1)

                @block.scalar
                def _(eng):
                    for h in range(2):
                        eng.wait_ge(f_xz, 4 * c + h + 1)
                        eng.activation(up[:, h, :, DC - 1:], PS[:, h, :].rearrange("p (b t) -> p b t", t=T),
                                       ACT.Copy).then_inc(f_u, 1)
                    for h in range(2):
                        eng.wait_ge(f_xz, 4 * c + h + 3)
                        eng.activation(sz[:, h, :], PS[:, 2 + h, :], ACT.Silu).then_inc(f_z, 1)
                    for h in range(2):
                        eng.wait_ge(f_conv, 8 * c + 4 * h + 4)
                        eng.activation(uc[:, h, :], cv[:, h, :], ACT.Silu).then_inc(f_uc, 1)
                    eng.wait_ge(f_dbl, 3 * c + 1)
                    eng.activation(dtr[:, :], PS[0:DR, 4, :], ACT.Copy).then_inc(f_dtr, 1)
                    for i in range(2):
                        eng.wait_ge(f_dbl, 3 * c + 2 + i)
                        eng.activation(bc3[i][:, :], PS[0:96, 5 + i, :], ACT.Copy).then_inc(f_hi, 1)
                    for h in range(2):
                        eng.wait_ge(f_dtp, 2 * c + h + 1)
                        eng.activation(spv[:, h, :], PS[:, h, :], ACT.Identity, bias=col("bdt", h)).then_inc(f_sp, 1)
                    eng.wait_ge(f_sp, 5 * c + 2)
                    eng.activation(spl[:, :, :], spv[:, :, :], ACT.Abs).then_inc(f_sp, 1)
                    eng.wait_ge(f_sp, 5 * c + 3)
                    eng.activation(spe[:, :, :], spl[:, :, :], ACT.Exp, scale=-1.0).then_inc(f_sp, 1)
                    eng.wait_ge(f_sp, 5 * c + 4)
                    eng.activation(spl[:, :, :], spe[:, :, :], ACT.Ln, bias=eps[:, 2:3]).then_inc(f_sp, 1)

                @block.vector
                def _(eng):
                    n = 8 * c
                    for h in range(2):
                        eng.wait_ge(f_u, 2 * c + h + 1)
                        acc = cv[:, h, :].rearrange("p (b t) -> p b t", t=T)
                        eng.tensor_scalar(acc, up[:, h, :, 0:T], col("convw", h * DC), col("convb", h),
                                          ALU.mult, ALU.add).then_inc(f_conv, 1)
                        n += 1
                        for k in range(1, DC):
                            eng.wait_ge(f_conv, n)
                            eng.scalar_tensor_tensor(acc, up[:, h, :, k:k + T], col("convw", h * DC + k), acc,
                                                     ALU.mult, ALU.add).then_inc(f_conv, 1)
                            n += 1
                    n = 16 * c

                    def after(ins):
                        nonlocal n
                        n += 1
                        ins.then_inc(f_v, 1)
                        eng.wait_ge(f_v, n)

                    for i in range(2):
                        eng.wait_ge(f_hi, 2 * c + i + 1)
                        after(eng.tensor_tensor(rest[:, :], PS[0:96, 5 + i, :], bc3[i][:, :], ALU.subtract))
                        after(eng.tensor_copy(mid[:, :], rest[:, :]))
                        after(eng.tensor_copy(bc3[i][32:64, :], mid[32:64, :]))
                        after(eng.tensor_tensor(bc3[i][64:96, :], rest[64:96, :], mid[64:96, :], ALU.subtract))
                    eng.wait_ge(f_sp, 5 * c + 5)
                    after(eng.tensor_scalar(spq[:, :, :], spe[:, :, :], 1.0, None, ALU.add))
                    after(eng.scalar_tensor_tensor(spq[:, :, :], spq[:, :, :], 1.0, spe[:, :, :],
                                                   ALU.subtract, ALU.subtract))
                    after(eng.scalar_tensor_tensor(spl[:, :, :], spv[:, :, :], 0.0, spl[:, :, :], ALU.max, ALU.add))
                    after(eng.tensor_tensor(dt_[:, :, :], spl[:, :, :], spq[:, :, :], ALU.subtract))
                    after(eng.tensor_tensor(dtu[:, :, :], dt_[:, :, :], uc[:, :, :], ALU.mult))
                    for h in range(2):
                        after(eng.memset(dt_[:, h, :].rearrange("p (b t) -> p b t", t=T)[:, :, 0:1], FAR))
                    after(eng.tensor_copy(cen[:, 0:1], dt_[:, 0, 0:1]))

            def schedule(eng, step, last):
                for n in range(0, LEAD):
                    step(n, n % 2)
                with eng.Fori(0, PAIRS) as i:
                    step(i * 2 + LEAD, LEAD % 2)
                    step(i * 2 + (LEAD + 1), (LEAD + 1) % 2)
                for n in range(LEAD + 2 * PAIRS, last + 1):
                    step(n, n % 2)

            def at_least(eng, s, base, rel):
                if not isinstance(rel, int):
                    eng.wait_ge(s, rel + base)
                elif base + rel > 0:
                    eng.wait_ge(s, base + rel)

            nb, kb = c * NS, c * 2 * NS

            with nc.Block() as block:
                @block.tensor
                def _(eng):
                    def spread_b(n, slot):
                        at_least(eng, s_bc, nb, n - 1)
                        eng.matmul(PS[:, BB[slot], :], pick32[0:96, bass.ds(n * 128, 128)], bc3[0][:, :],
                                   start=True, stop=True).then_inc(s_b, 1)

                    def spread_c(n, slot):
                        at_least(eng, s_hc, kb, n * 2 - 2)
                        eng.matmul(PS[:, CB[slot], :], pick32[0:96, bass.ds(n * 128, 128)], bc3[1][:, :],
                                   start=True, stop=True).then_inc(s_c, 1)

                    def step(n, slot):
                        static = isinstance(n, int)
                        if not (static and n + 2 >= NS):
                            spread_b(n + 2, slot)
                        if not (static and n == 0):
                            for h in range(2):
                                at_least(eng, s_hc, kb, n * 2 - 1 + h)
                                eng.matmul(PS[:, YB[h], :], ident, hC[:, 2 * (1 - slot) + h, :], start=False,
                                           stop=(static and n == NS), skip_group_check=True).then_inc(s_y, 1)
                        if not (static and n + 1 >= NS):
                            spread_c(n + 1, 1 - slot)

                    for n in range(2):
                        spread_b(n, n)
                    spread_c(0, 0)
                    for h in range(2):
                        eng.matmul(PS[:, YB[h], :], diagD[:, d, h, :], uc[:, h, :], start=True, stop=False,
                                   skip_group_check=True)
                    schedule(eng, step, NS)

                @block.scalar
                def _(eng):
                    def copy_b(n, slot):
                        at_least(eng, s_b, nb, n + 1)
                        at_least(eng, s_dbu, kb, n * 2 - 2)
                        eng.activation(Bsb[:, slot, :], PS[:, BB[slot], :], ACT.Copy).then_inc(s_bc, 1)

                    def decay(n, h):
                        at_least(eng, s_h, kb, n * 2 - 1 + h)
                        eng.activation(PS[:, AB[h], :], dt_[:, h, :], ACT.Exp,
                                       scale=Aneg[:, d, bass.ds(n + h * NS, 1)]).then_inc(s_da, 1)

                    def step(n, slot):
                        static = isinstance(n, int)
                        decay(n + 1, 0)
                        if not (static and n + 2 >= NS):
                            copy_b(n + 2, slot)
                        decay(n + 1, 1)

                    copy_b(0, 0)
                    decay(0, 0)
                    copy_b(1, 1)
                    decay(0, 1)
                    schedule(eng, step, NS - 2)

                @block.gpsimd
                def _(eng):
                    def step(n, slot):
                        at_least(eng, s_bc, nb, n + 1)
                        for h in range(2):
                            at_least(eng, s_h, kb, n * 2 - 3 + h)
                            eng.tensor_tensor(dBu[:, 2 * slot + h, :], dtu[:, h, :], Bsb[:, slot, :], ALU.mult)\
                               .then_inc(s_dbu, 1)

                    schedule(eng, step, NS - 1)

                @block.vector
                def _(eng):
                    def product(n, slot, h):
                        at_least(eng, s_h, kb, n * 2 + 1 + h)
                        at_least(eng, s_c, nb, n + 1)
                        at_least(eng, s_y, kb, n * 2 - 3 + h)
                        eng.tensor_tensor(hC[:, 2 * slot + h, :], hst[:, 2 * slot + h, :], PS[:, CB[slot], :],
                                          ALU.mult).then_inc(s_hc, 1)

                    def scan(n, slot, h):
                        at_least(eng, s_da, kb, n * 2 + 1 + h)
                        at_least(eng, s_dbu, kb, n * 2 + 1 + h)
                        at_least(eng, s_hc, kb, n * 2 - 3 + h)
                        eng.tensor_tensor_scan(hst[:, 2 * slot + h, :], PS[:, AB[h], :], dBu[:, 2 * slot + h, :],
                                               0.0, ALU.mult, ALU.add).then_inc(s_h, 1)

                    def step(n, slot):
                        static = isinstance(n, int)
                        if not (static and n == NS):
                            scan(n, slot, 0)
                        if not (static and n == 0):
                            product(n - 1, 1 - slot, 1)
                        if not (static and n == NS):
                            scan(n, slot, 1)
                            product(n, slot, 0)

                    schedule(eng, step, NS)

            with nc.Block() as block:
                @block.tensor
                def _(eng):
                    eng.wait_ge(k_yz, 2 * c + 2)
                    for h in range(2):
                        mm = eng.matmul(PS[:, 2, :], w("WoutT_" + tag)[:, h * 128:(h + 1) * 128], yz[:, h, :],
                                        start=(h == 0), stop=(h == 1))
                    mm.then_inc(k_o, 1)
                    eng.wait_ge(k_fo, c + 1)
                    eng.matmul(PS[:, 3, :], meanw, fo[:, :], start=True, stop=True).then_inc(k_mean, 1)
                    eng.wait_ge(k_sq, c + 1)
                    eng.matmul(PS[:, 4, :], meanw, sq[:, :], start=True, stop=True).then_inc(k_var, 1)
                    if d == 1:
                        eng.wait_ge(k_n, 3 * c + 3)
                        for i in range(2):
                            mm = eng.matmul(PS[:, 5, :], w("WfT")[:, i * 128:(i + 1) * 128], lnout[i][:, :],
                                            start=(i == 0), stop=(i == 1))
                        mm.then_inc(k_fuse, 1)

                @block.scalar
                def _(eng):
                    eng.wait_ge(k_o, c + 1)
                    eng.activation(fo[:, :], PS[:, 2, :], ACT.Copy).then_inc(k_fo, 1)
                    eng.wait_ge(k_cen, c + 1)
                    eng.activation(sq[:, :], cen[:, :], ACT.Square).then_inc(k_sq, 1)
                    eng.wait_ge(k_var, c + 1)
                    eng.activation(sd[:, :], PS[:, 4, :], ACT.Sqrt, bias=eps[:, 0:1]).then_inc(k_sd, 1)

                @block.vector
                def _(eng):
                    for h in range(2):
                        eng.tensor_tensor(yz[:, h, :], sz[:, h, :], PS[:, YB[h], :], ALU.mult).then_inc(k_yz, 1)
                    eng.wait_ge(k_mean, c + 1)
                    eng.tensor_tensor(cen[:, :], fo[:, :], PS[:, 3, :], ALU.subtract).then_inc(k_cen, 1)
                    eng.wait_ge(k_cen, c + 1)
                    eng.wait_ge(k_sd, c + 1)
                    eng.reciprocal(sd[:, :], sd[:, :]).then_inc(k_n, 1)
                    eng.wait_ge(k_n, 3 * c + 1)
                    eng.tensor_tensor(cen[:, :], cen[:, :], sd[:, :], ALU.mult).then_inc(k_n, 1)
                    eng.wait_ge(k_n, 3 * c + 2)
                    dst = lnout[d][:, :].rearrange("p (b t) -> p b t", t=T)
                    eng.tensor_scalar(dst[:, :, ::-1] if d else dst, cen[:, :].rearrange("p (b t) -> p b t", t=T),
                                      col("ln_g", 0), col("ln_b", 0), ALU.mult, ALU.add).then_inc(k_n, 1)
                    if d == 1:
                        eng.wait_ge(k_fuse, th + 1)
                        dst = x1[:, :].rearrange("p (t b) -> p b t", b=B)[:, th * HB:(th + 1) * HB, :]
                        eng.scalar_tensor_tensor(
                            dst, PS[:, 5, :].rearrange("p (b t) -> p b t", t=T), w("bfuse"),
                            xT[:, th * HALF:(th + 1) * HALF].rearrange("p (b t) -> p b t", t=T), ALU.add, ALU.add)\
                           .then_inc(k_x1, 1)

        scopes.pop().close()
        hr = sb("hr", [128, N])
        x2 = sb("x2", [128, N])
        Hs = sb("Hs", [128, N])
        hp = sb("hp", [128, 2, 2, B], F16)
        gt = sb("gt", [128, 2, 5, B])
        vv = sb("vv", [128, 2, B])
        oo = sb("oo", [128, B])
        tc = sb("tc", [128, B])
        r_mm, r_h, r_ffn, r_x2 = (sem("rnn_" + n) for n in ("mm", "h", "ffn", "x2"))
        l_mm, l_g, l_v, l_c, l_o, l_t, l_h, l_hi, l_lo = (
            sem("lstm_" + n) for n in ("mm", "g", "v", "c", "o", "t", "h", "hi", "lo"))
        RB, LB, FB = (0, 1), (2, 3), 4
        LAG = 2

        with nc.Block() as block:
            @block.tensor
            def _(eng):
                def preload_rnn(c):
                    if c >= 2:
                        eng.wait_ge(r_h, (c - 1) * CH)
                    eng.matmul(PS[:, RB[c % 2], 0:CHB], w("WxR"), x1[:, c * CHB:(c + 1) * CHB], start=True,
                               stop=False, skip_group_check=True)

                def rnn_step(t):
                    c, s = divmod(t, CH)
                    if t:
                        eng.wait_ge(r_h, t)
                    eng.matmul(PS[:, RB[c % 2], s * B:(s + 1) * B], w("WhR"),
                               hr[:, (t - 1) * B:t * B] if t else condT, start=False, stop=True,
                               skip_group_check=True).then_inc(r_mm, 1)

                def ternary(c):
                    eng.wait_ge(r_h, (c + 1) * CH)
                    if c:
                        eng.wait_ge(r_x2, c)
                    eng.matmul(PS[:, FB, 0:CHB], wq[:, :], hr[:, c * CHB:(c + 1) * CHB], start=True, stop=True)\
                       .then_inc(r_ffn, 1)

                def gates(c):
                    return PS[:, LB[c % 2], 0:G4 * CHB]

                def preload_bias(c):
                    if c >= 2:
                        eng.wait_ge(l_g, (c - 1) * CH)
                    eng.matmul(gates(c), bLs[0:G4, :], w("gate_rows")[0:G4, :], start=True, stop=False,
                               skip_group_check=True)

                def preload_gate(c, g):
                    eng.wait_ge(r_x2, c + 1)
                    eng.matmul(gates(c).rearrange("p (s g b) -> p s g b", g=G4, b=B)[:, :, g, :],
                               WxLs[:, g * 128:(g + 1) * 128],
                               x2[:, c * CHB:(c + 1) * CHB].rearrange("p (s b) -> p s b", b=B), start=False,
                               stop=False, skip_group_check=True)

                def lstm_step(t):
                    c, s = divmod(t, CH)

                    def into(g):
                        return gates(c)[:, (s * G4 + g) * B:(s * G4 + g + 1) * B]

                    if t == 0:
                        for g in range(G4):
                            mm = eng.matmul(into(g), WhLs[:, g * 128:(g + 1) * 128], H0[:, :], start=False,
                                            stop=True, skip_group_check=True)
                    else:
                        for part, ready, weights in ((0, l_hi, (0, 1, 2)), (1, l_lo, (0, 1))):
                            eng.wait_ge(ready, t)
                            for i in weights:
                                for g in range(G4):
                                    mm = eng.matmul(into(g), Wh3[:, i, g * 128:(g + 1) * 128],
                                                    hp[:, (t - 1) % 2, part, :], start=False, stop=True,
                                                    skip_group_check=True)
                    mm.then_inc(l_mm, 1)

                preload_rnn(0)
                for c in range(NCH + LAG):
                    for s in range(CH):
                        if c >= LAG:
                            lstm_step((c - LAG) * CH + s)
                        if c < NCH:
                            rnn_step(c * CH + s)
                        if 1 <= c <= NCH:
                            if s == 0:
                                ternary(c - 1)
                                preload_bias(c - 1)
                            elif s <= G4:
                                preload_gate(c - 1, s - 1)
                        if s == CH - 2 and c + 1 < NCH:
                            preload_rnn(c + 1)

            @block.scalar
            def _(eng):
                for c in range(NCH + LAG):
                    for s in range(CH):
                        if c >= LAG:
                            t = (c - LAG) * CH + s
                            eng.wait_ge(l_mm, t + 1)
                            if t >= 2:
                                eng.wait_ge(l_h, t - 1)
                            eng.activation(gt[:, t % 2, 0:G4, :],
                                           PS[:, LB[c % 2], s * G4 * B:(s + 1) * G4 * B]
                                           .rearrange("p (g b) -> p g b", b=B), ACT.Tanh, scale=1.0 / LIFT)\
                               .then_inc(l_g, 1)
                        if c < NCH:
                            t = c * CH + s
                            eng.wait_ge(r_mm, t + 1)
                            eng.activation(hr[:, t * B:(t + 1) * B], PS[:, RB[c % 2], s * B:(s + 1) * B], ACT.Tanh,
                                           bias=w("bR")).then_inc(r_h, 1)
                        if c >= LAG:
                            t = (c - LAG) * CH + s
                            eng.wait_ge(l_c, t + 2)
                            eng.activation(tc[:, :], gt[:, (t + 1) % 2, 4, :], ACT.Tanh, scale=0.5).then_inc(l_t, 1)

            @block.vector
            def _(eng):
                eng.memset(gt[:, 0, 4, :], 0.0).then_inc(l_c, 1)
                for c in range(NCH + LAG):
                    for s in range(CH):
                        if c >= LAG:
                            t = (c - LAG) * CH + s
                            cur, nxt = gt[:, t % 2, :, :], gt[:, (t + 1) % 2, :, :]
                            eng.wait_ge(l_g, t + 1)
                            eng.wait_ge(l_c, t + 1)
                            eng.scalar_tensor_tensor(vv[:, :, :], cur[:, 0:2, :], 1.0, cur[:, 3:5, :],
                                                     ALU.add, ALU.mult).then_inc(l_v, 1)
                            eng.wait_ge(l_v, t + 1)
                            eng.scalar_tensor_tensor(nxt[:, 4, :], vv[:, 1, :], 0.5, vv[:, 0, :],
                                                     ALU.mult, ALU.add).then_inc(l_c, 1)
                            eng.tensor_scalar(oo[:, :], cur[:, 2, :], 1.0, LIFT / 2, ALU.add, ALU.mult)\
                               .then_inc(l_o, 1)
                            eng.wait_ge(l_o, t + 1)
                            eng.wait_ge(l_t, t + 1)
                            eng.tensor_tensor(hp[:, t % 2, 0, :], oo[:, :], tc[:, :], ALU.mult).then_inc(l_hi, 1)
                            eng.tensor_tensor(Hs[:, t * B:(t + 1) * B], oo[:, :], tc[:, :], ALU.mult)\
                               .then_inc(l_h, 1)
                            eng.wait_ge(l_hi, t + 1)
                            eng.wait_ge(l_h, t + 1)
                            eng.tensor_tensor(hp[:, t % 2, 1, :], Hs[:, t * B:(t + 1) * B], hp[:, t % 2, 0, :],
                                              ALU.subtract).then_inc(l_lo, 1)
                        if s == 0 and 1 <= c <= NCH:
                            span = slice((c - 1) * CHB, c * CHB)
                            eng.wait_ge(r_ffn, c)
                            eng.tensor_tensor(x2[:, span], x1[:, span], PS[:, FB, 0:CHB], ALU.add).then_inc(r_x2, 1)

        rr = sb("rr", [128, N])
        kvs = sb("kvs", [128, N])
        cum = sb("cum", [128, N])
        yy = sb("yy", [128, N])
        x3 = sb("x3", [128, N])
        PAD = (DC - 1) * B
        vp = sb("vp", [128, PAD + N])
        res = sb("res", [128, N])
        tG = sb("tG", [128, 2, 512])
        tM = sb("tM", [128, 2, 512])
        tS = sb("tS", [128, 2, 512])
        r1 = Router("r1", guarded=False)
        a_mm, a_act, a_dve, a_cum, a_ms, a_sd, a_y, a_o = (
            sem("attn_" + n) for n in ("mm", "act", "dve", "cum", "ms", "sd", "y", "o"))
        e_a, e_b, e_g, e_act, e_mul, e_acc, e_x, e_res = (
            sem("ffn_" + n) for n in ("a", "b", "g", "act", "mul", "acc", "x", "res"))
        v_pad = sem("v_pad")
        v_in = sem("v_in")
        stored = sem("stored")

        def bt(ap):
            return ap.rearrange("p (b t) -> p b t", t=T)

        def tb(ap):
            return ap.rearrange("p (t b) -> p b t", b=B)

        def half(ap, h):
            return ap[:, h * 512:(h + 1) * 512]

        with nc.Block() as block:
            @block.tensor
            def _(eng):
                for h in range(2):
                    if h:
                        eng.wait_ge(a_act, 2 * h)
                        eng.wait_ge(a_dve, 2 * h - 1)
                    for bank, name in ((0, "WrT"), (1, "WkT"), (2, "WvT")):
                        eng.matmul(PS[:, bank, :], w(name), half(Hs, h), start=True, stop=True).then_inc(a_mm, 1)
                for h in range(2):
                    eng.wait_ge(a_ms, h + 1)
                    eng.matmul(PS[:, 3 + h, :], meanw, half(kvs, h), start=True, stop=True).then_inc(a_mm, 1)
                for h in range(2):
                    eng.wait_ge(a_y, 3 * h + 3)
                    eng.matmul(PS[:, 5 + h, :], w("WoT"), half(yy, h), start=True, stop=True).then_inc(a_o, 1)
                eng.wait_ge(v_in, 2)
                for t in range(8):
                    mm = eng.matmul(PS[:, 0, t * E:(t + 1) * E], vp[:, PAD + t * 128:PAD + (t + 1) * 128], w("fWr"),
                                    start=(t == 0), stop=True, skip_group_check=True)
                mm.then_inc(r1.logits, 1)

                for j in range(4):
                    h, pair = j // 2, j % 2
                    cols = vp[:, PAD + h * 512:PAD + (h + 1) * 512]
                    if j >= 1:
                        eng.wait_ge(e_act, j)
                        eng.wait_ge(e_mul, 2 * j)
                    eng.matmul(PS[:, 2, :], w("Wg")[:, pair * 128:(pair + 1) * 128], cols, start=True, stop=True)\
                       .then_inc(e_a, 1)
                    eng.matmul(PS[:, 3, :], w("Wu")[:, pair * 128:(pair + 1) * 128], cols, start=True, stop=True)\
                       .then_inc(e_b, 1)
                    if j == 0:
                        r1.pe_turn(eng, 1)
                        eng.wait_ge(r1.gates, 1)
                    eng.matmul(PS[:, 4, :], w("pickpair")[0:3 * E, pair * 128:(pair + 1) * 128],
                               r1.gT[:, h * 512:(h + 1) * 512], start=True, stop=True).then_inc(e_g, 1)
                    eng.wait_ge(e_mul, 2 * j + 2)
                    eng.matmul(PS[:, 5, :] if h == 0 else PS[:, 6, :], w("Wd")[:, pair * 128:(pair + 1) * 128],
                               tS[:, j % 2, :], start=(pair == 0), stop=(pair == 1)).then_inc(e_acc, 1)
                for h in range(2):
                    if h:
                        eng.wait_ge(e_res, 9)
                    eng.matmul(PS[:, 7, :], w("pick46")[0:3 * E, :], r1.gT[:, h * 512:(h + 1) * 512],
                               start=True, stop=True).then_inc(e_x, 1)
                    eng.matmul(PS[:, 0, :], w("pick8")[0:3 * E, 7 * 128:8 * 128], r1.gT[:, h * 512:(h + 1) * 512],
                               start=True, stop=True).then_inc(e_x, 1)

            @block.scalar
            def _(eng):
                for h in range(2):
                    eng.wait_ge(a_mm, 3 * h + 1)
                    eng.activation(half(rr, h), PS[:, 0, :], ACT.Sigmoid, scale=1.0 / LIFT).then_inc(a_act, 1)
                    eng.wait_ge(a_mm, 3 * h + 2)
                    if h:
                        eng.wait_ge(a_dve, 1)
                    eng.activation(half(yy, h), PS[:, 1, :], ACT.Copy, scale=1.0 / (LIFT * LIFT)).then_inc(a_act, 1)
                for h in range(2):
                    eng.wait_ge(a_cum, 3 + h)
                    eng.activation(half(kvs, h), half(yy, h), ACT.Square).then_inc(a_ms, 1)
                for h in range(2):
                    eng.wait_ge(a_mm, 6 + h + 1)
                    eng.activation(half(kvs, h), PS[:, 3 + h, :], ACT.Sqrt, bias=eps[:, 1:2]).then_inc(a_sd, 1)
                r1.act(eng, 0)
                for j in range(4):
                    eng.wait_ge(e_a, j + 1)
                    if j >= 2:
                        eng.wait_ge(e_mul, 2 * j - 3)
                    eng.activation(tG[:, j % 2, :], PS[:, 2, :], ACT.Silu).then_inc(e_act, 1)

            @block.vector
            def _(eng):
                eng.memset(vp[:, 0:PAD], 0.0).then_inc(v_pad, 1)
                for h in range(2):
                    eng.wait_ge(a_act, 2 * h + 2)
                    eng.wait_ge(a_mm, 3 * h + 3)
                    eng.tensor_tensor(half(yy, h), half(yy, h), PS[:, 2, :], ALU.mult).then_inc(a_dve, 1)
                    eng.wait_ge(a_dve, 2 * h + 1)
                    ts = slice(h * 64, (h + 1) * 64)
                    eng.tensor_tensor(bt(kvs[:, :])[:, :, ts], tb(half(yy, h)),
                                      dinv[:, ts].unsqueeze(1).to_broadcast([128, B, 64]), ALU.mult)\
                       .then_inc(a_dve, 1)
                eng.wait_ge(a_dve, 4)
                eng.tensor_tensor_scan(cum[:, :], w("keep"), kvs[:, :], 0.0, ALU.mult, ALU.add).then_inc(a_cum, 1)
                eng.wait_ge(a_cum, 1)
                eng.tensor_tensor(bt(cum[:, :]), bt(cum[:, :]), dscale[:, :].unsqueeze(1).to_broadcast([128, B, T]),
                                  ALU.mult).then_inc(a_cum, 1)
                eng.wait_ge(a_cum, 2)
                for h in range(2):
                    eng.tensor_tensor(tb(half(yy, h)), tb(half(rr, h)), bt(cum[:, :])[:, :, h * 64:(h + 1) * 64],
                                      ALU.mult).then_inc(a_cum, 1)
                for h in range(2):
                    eng.wait_ge(a_sd, h + 1)
                    eng.reciprocal(half(kvs, h), half(kvs, h)).then_inc(a_y, 1)
                    eng.wait_ge(a_y, 3 * h + 1)
                    eng.tensor_scalar(half(yy, h), half(yy, h), w("ln_w"), None, ALU.mult).then_inc(a_y, 1)
                    eng.wait_ge(a_y, 3 * h + 2)
                    eng.tensor_tensor(half(yy, h), half(yy, h), half(kvs, h), ALU.mult).then_inc(a_y, 1)
                for h in range(2):
                    eng.wait_ge(a_o, h + 1)
                    eng.tensor_tensor(half(x3, h), half(x2, h), PS[:, 5 + h, :], ALU.add).then_inc(v_pad, 1)
                    eng.wait_ge(v_pad, h + 2)
                    eng.tensor_tensor(vp[:, PAD + h * 512:PAD + (h + 1) * 512].rearrange("p (t b) -> p t b", b=B),
                                      half(x3, h).rearrange("p (t b) -> p t b", b=B),
                                      g1[:, :].unsqueeze(1).to_broadcast([128, 64, B]), ALU.mult).then_inc(v_in, 1)
                r1.dve(eng, w("frb"), 1)
                for j in range(4):
                    eng.wait_ge(e_act, j + 1)
                    eng.wait_ge(e_b, j + 1)
                    eng.tensor_tensor(tM[:, j % 2, :], tG[:, j % 2, :], PS[:, 3, :], ALU.mult).then_inc(e_mul, 1)
                    eng.wait_ge(e_mul, 2 * j + 1)
                    eng.wait_ge(e_g, j + 1)
                    if j >= 2:
                        eng.wait_ge(e_acc, j - 1)
                    eng.tensor_tensor(tS[:, j % 2, :], tM[:, j % 2, :], PS[:, 4, :], ALU.mult).then_inc(e_mul, 1)
                n = 0

                def after(ins):
                    nonlocal n
                    n += 1
                    ins.then_inc(e_res, 1)
                    eng.wait_ge(e_res, n)

                a0 = PACK1["fcw"][0]
                for h in range(2):
                    o = half(res, h)
                    v = vp[:, PAD + h * 512:PAD + (h + 1) * 512]

                    def tap(k):
                        return vp[:, h * 512 + k * B:(h + 1) * 512 + k * B], p1[:, a0 + k:a0 + k + 1]

                    after(eng.tensor_scalar(o, tap(0)[0], tap(0)[1], w("fcb"), ALU.mult, ALU.add))
                    for k in range(1, DC):
                        after(eng.scalar_tensor_tensor(o, tap(k)[0], tap(k)[1], o, ALU.mult, ALU.add))
                    after(eng.tensor_tensor(o, o, half(x3, h), ALU.add))
                    eng.wait_ge(e_acc, 2 * h + 2)
                    after(eng.tensor_tensor(o, o, PS[:, 5 + h, :], ALU.add))
                    eng.wait_ge(e_x, 2 * h + 2)
                    after(eng.tensor_tensor(tM[:, 0, :], v, PS[:, 7, :], ALU.mult))
                    after(eng.scalar_tensor_tensor(tM[:, 1, :], v, 0.0, PS[:, 0, :], ALU.max, ALU.mult))
                    after(eng.tensor_tensor(o, o, tM[:, 0, :], ALU.add))
                    after(eng.tensor_tensor(o, o, tM[:, 1, :], ALU.add))

            @block.sync
            def _(eng):
                for h in range(2):
                    eng.wait_ge(e_res, 10 * (h + 1))
                    eng.dma_start(half(out, h), half(res, h)).then_inc(stored, 16)
                eng.wait_ge(stored, 32)


def kernel(**inputs):
    import numpy as np
    import ml_dtypes
    import concourse.bacc as bacc
    from concourse.bass_utils import run_bass_kernel_spmd

    x = {k: np.asarray(v) for k, v in inputs.items()}

    def packed(place, width, parts):
        a = np.zeros((128, width), np.float32)
        for name, v in parts.items():
            lo, hi = place[name]
            v = np.asarray(v)
            v = v.reshape(v.shape[0], -1)
            a[:v.shape[0], lo:lo + v.shape[1]] = v
        return a

    def blocks(m, rows=128):
        return m.reshape(-1, rows, m.shape[1]).transpose(1, 0, 2)

    def row128(v):
        return np.broadcast_to(v[None, :], (128, v.shape[0]))

    m0 = {
        "xT": x["x"].reshape(N, D).T, "condT": x["cond_1024"].T,
        "RWx": x["L0_cond_router_W"][0:D], "RWt": x["L0_cond_router_W"][D:], "rbias": row128(x["L0_cond_router_bias"]),
        "w1": x["L0_cond_w1"], "w3": x["L0_cond_w3"], "w2": blocks(x["L0_cond_w2"]),
        "W1e": x["L0_cond_W1e"].transpose(1, 0, 2), "W2e": x["L0_cond_W2e"].transpose(1, 0, 2),
    }
    m1 = {}
    for t in "fb":
        g = {k[len("L0_attn_"):-2]: v for k, v in x.items() if k.startswith("L0_attn_") and k.endswith("_" + t)}
        wx = g["Wx"].T
        three = lambda m: np.concatenate([m, m, m], axis=1)
        m1.update({k + "_" + t: v for k, v in {
            "WinT": g["Win"].T, "WxdT": blocks(wx[:, 0:DR]), "WxB": blocks(three(wx[:, DR:DR + NS])),
            "WxC": blocks(three(wx[:, DR + NS:])), "WdtT": g["Wdt"].T, "WoutT": blocks(g["Wout"].T),
            "Alog": blocks(g["Alog"]), "convw": blocks(g["convw"]), "convb": blocks(g["convb"][:, None]),
            "bdt": blocks(g["bdt"][:, None]), "Dp": blocks(g["Dp"][:, None]),
            "ln_g": g["ln_g"][:, None], "ln_b": g["ln_b"][:, None]}.items()})
    pairs = lambda m: m.transpose(1, 0, 2)
    m1.update({
        "WfT": blocks(x["L0_attn_Wfuse"].T), "bfuse": x["L0_attn_bfuse"][:, None],
        "WxR": x["L0_cond2_Wx"], "WhR": x["L0_cond2_Wh"], "bR": x["L0_cond2_b"][:, None],
        "WqT": x["L0_ffn_weight"].T, "WxL": x["L1_cond_Wx"], "WhL": x["L1_cond_Wh"], "bL": x["L1_cond_b"].reshape(G4, D),
        "WrT": x["L1_attn_Wr"].T, "WkT": x["L1_attn_Wk"].T, "WvT": x["L1_attn_Wv"].T, "WoT": x["L1_attn_Wo"].T,
        "decay": x["L1_attn_decay"][:, None], "ln_w": x["L1_attn_ln_w"][:, None],
        "C1T": x["L1_cond2_W1"].T, "C2T": x["L1_cond2_W2"].T, "cb1": x["L1_cond2_b1"][:, None],
        "cb2": x["L1_cond2_b2"][:, None], "fWr": x["L1_ffn_Wr"], "frb": row128(x["L1_ffn_router_bias"]),
        "Wg": pairs(x["L1_ffn_Wg"]), "Wu": pairs(x["L1_ffn_Wu"]),
        "Wd": blocks(x["L1_ffn_Wd"].reshape(256, D)), "fcw": x["L1_ffn_conv_w"].reshape(DC, D).T,
        "fcb": x["L1_ffn_conv_b"][:, None],
    })
    eye = np.eye(128, dtype=np.float32)
    keep = np.ones((128, B, T), np.float32)
    keep[:, :, 0] = 0
    gate_rows = np.broadcast_to(np.eye(G4, dtype=np.float32)[:, None, :, None], (G4, CH, G4, B))
    mf = {"ident": eye, "mean": np.full((128, 128), 1.0 / 128, np.float32), "ones": np.ones((128, 128), np.float32),
          "iota8": row128(np.arange(E, dtype=np.float32)), "iotat": row128(np.arange(T, dtype=np.float32)),
          "keep": keep, "gate_lift": np.array([[LIFT / 2]] * 3 + [[LIFT]], np.float32), "gate_rows": gate_rows}
    pick32 = np.zeros((96, NS, 128), np.float32)
    for n in range(NS):
        pick32[[n, NS + n, 2 * NS + n], n, :] = 1
    pick8 = np.zeros((3 * E, E, 128), np.float32)
    for e in range(E):
        pick8[[e, E + e, 2 * E + e], e, :] = 1
    pickpair = np.concatenate([pick8[:, e, 0:64] for e in range(4)], axis=1)
    mb = {"identb": eye, "pick32": pick32, "pick8": pick8, "pick46": pick8[:, 4] + pick8[:, 6], "pickpair": pickpair}
    arrays = {
        "pack0": packed(PACK0, W0, m0), "pack1": packed(PACK1, W1, m1), "conf": packed(CONF, WF, mf),
        "conb": packed(CONB, WB, mb).astype(ml_dtypes.bfloat16),
    }
    nc = bacc.Bacc("TRN2", target_bir_lowering=False, num_devices=1)
    args = [nc.dram_tensor(k, v.shape, mybir.dt.from_np(v.dtype), kind="ExternalInput").ap() for k, v in arrays.items()]
    out = nc.dram_tensor("y", (128, N), F32, kind="ExternalOutput").ap()
    build(nc, *args, out)
    r = run_bass_kernel_spmd(nc, [arrays], core_ids=[0])
    y = r.results[0]["y"]
    return np.ascontiguousarray(np.asarray(y).reshape(D, T, B).transpose(2, 1, 0))
```

```python
from contextlib import ExitStack

import concourse.bass as bass
from concourse import mybir

F32 = mybir.dt.float32
BF16 = mybir.dt.bfloat16
F16 = mybir.dt.float16
U32 = mybir.dt.uint32
ALU = mybir.AluOpType
ACT = mybir.ActivationFunctionType
AX_X = mybir.AxisListType.X

B, T, D = 8, 128, 128
N = B * T
HALF = N // 2
HB = B // 2
DI, NS, DC, DR = 256, 32, 4, 8
HS, E = 256, 8
G4 = 4
CH = 8
NCH = T // CH
CHB = CH * B
PT = 16
PW, PIECES = PT * B, T // PT
QUIET, TURNS = 2, 10
BD = 3 * NS + DR
SLOTS = 32
LIFT = 2.0 ** 14
LN2 = 0.6931471805599453
FAR = 1.0e24


def columns(parts):
    at, place = 0, {}
    for name, width in parts:
        place[name] = (at, at + width)
        at += width
    return place, at


MAMBA = [("WinuT", DI), ("WinzT", DI), ("taps", DC * DI), ("WxBD", 2 * BD), ("WxC", 2 * 3 * NS), ("WdtP", DI),
         ("WoutT", 2 * D), ("Alog", 2 * NS), ("convb", 2), ("bdt", 2), ("Dp", 2), ("ln_g", 1), ("ln_b", 1)]
PACK0, W0 = columns([("xT", N), ("condT", B), ("RWx", E), ("RWt", E), ("rbias", E), ("decay", 1),
                     ("w1", HS), ("w3", HS), ("w2", HS), ("W1e", E * 128), ("W2e", E * 128)])
PACK1, W1 = columns([(f"{n}_{d}", w) for d in "fb" for n, w in MAMBA]
                    + [("WfT", 2 * D), ("bfuse", 1), ("WxR", D), ("WhR", D), ("bR", 1), ("WqT", D),
                       ("WxL", 4 * D), ("WhL", 4 * D), ("bL", D), ("WrT", D), ("WkT", D), ("WvT", D),
                       ("WoT", D), ("ln_w", 1), ("C1T", D), ("C2T", D), ("cb1", 1), ("cb2", 1),
                       ("fWr", E), ("frb", E), ("Wg", 256), ("Wu", 256), ("Wd", 256), ("fcw", DC), ("fcb", 1)])
CONF, WF = columns([("iota8", E), ("ident", 128), ("mean", 128), ("iotat", T), ("gate_lift", 1)])
CONB, WB = columns([("identb", 128), ("pick8", E * 128), ("less_mid", 3 * NS), ("less_lo", 3 * NS), ("pick46", 128),
                    ("gate_rows", G4 * CHB), ("pickpair", 256), ("pick32", NS * 128)])


def build(nc, pack0, pack1, conf, conb, out):
    ctx = ExitStack()
    with ctx:
        scopes = [ctx]

        def sb(name, shape, dt=F32):
            return scopes[-1].enter_context(nc.sbuf_tensor(name, shape, dt))

        def sem(name):
            return ctx.enter_context(nc.semaphore(name))

        p0 = sb("p0", [128, W0])
        p1 = sb("p1", [128, W1])
        cf = sb("cf", [128, WF])
        cb = sb("cb", [128, WB], BF16)
        PS = ctx.enter_context(nc.psum_tensor("PS", [128, 8, 512], F32))

        def w(name):
            for src, place in ((p0, PACK0), (p1, PACK1), (cf, CONF), (cb, CONB)):
                if name in place:
                    a, b = place[name]
                    return src[:, a:b]
            raise KeyError(name)

        xT = w("xT")
        condT = w("condT")
        ident = w("ident")
        meanw = w("mean")
        pick32 = w("pick32")

        PADT = DC - 1 + T
        uin = [sb("uin_f", [128, B, PADT]), sb("uin_r", [128, B, PADT])]
        lnout = [sb("ln_fwd", [128, HALF]), sb("ln_bwd", [128, HALF])]
        x1 = sb("x1", [128, N])
        Aneg = sb("Aneg", [128, 2, 2 * NS])
        diagD = sb("diagD", [128, 2, 2, 128])
        wq = sb("wq", [128, D])
        g1 = sb("g1", [128, B])
        WxLs = sb("WxLs", [128, 4 * D])
        WhLs = sb("WhLs", [128, 4 * D])
        bLs = sb("bLs", [96, D])
        brest = sb("brest", [96, D])
        bmid = sb("bmid", [96, D], BF16)
        bL3 = sb("bL3", [96, D], BF16)
        Wh3 = sb("Wh3", [128, 3, 4 * D], BF16)
        wrest = sb("wrest", [128, 4 * D])
        H0 = sb("H0", [128, B])
        dscale = sb("dscale", [128, T])
        dinv = sb("dinv", [128, T])
        keep = sb("keep", [128, PW])
        bias2 = sb("bias2", [128, E])
        cbh = sb("cbh", [128, 2, 2])
        mwo = sb("mwo", [128, 2, 2])
        WoC = sb("WoC", [128, 2, 2, D])
        WfG = sb("WfG", [128, 2, D])
        bF = sb("bF", [128, 1])

        class Router:

            def __init__(self, name):
                self.s = sb(name + "_s", [128, 8, E])
                self.sel = sb(name + "_sel", [128, 8, E])
                self.top = sb(name + "_top", [128, 8, 8])
                self.idx = sb(name + "_idx", [128, 8, 8], U32)
                self.idf = sb(name + "_idf", [128, 8, 2])
                self.hot = sb(name + "_hot", [128, 8, 2, E])
                self.mask = sb(name + "_mask", [128, 8, E])
                self.ss = sb(name + "_ss", [128, 8, E])
                self.den = sb(name + "_den", [128, 8])
                self.rec = sb(name + "_rec", [128, 8])
                self.flag = sb(name + "_flag", [128, 8])
                self.comb = sb(name + "_comb", [128, 8, E])
                self.rest = sb(name + "_rest", [128, 8, E])
                self.parts = sb(name + "_parts", [128, 8, 3 * E], BF16)
                self.gT = sb(name + "_gT", [3 * E, N], BF16)
                self.logits = sem(name + "_logits")
                self.scored = sem(name + "_scored")
                self.step = sem(name + "_step")
                self.turned = sem(name + "_turned")
                self.gates = sem(name + "_gates")

            def act(self, eng, bank):
                eng.wait_ge(self.logits, 1)
                eng.activation(self.s[:, :, :], PS[:, bank, 0:8 * E].rearrange("p (t e) -> p t e", e=E),
                               ACT.Sigmoid).then_inc(self.scored, 1)

            def dve(self, eng, bias, bank, multiply, consts):
                done = [0]

                def after(ins):
                    done[0] += 1
                    ins.then_inc(self.step, 1)
                    eng.wait_ge(self.step, done[0])

                eng.wait_ge(self.scored, 1)
                after(eng.tensor_tensor(self.sel[:, :, :], self.s[:, :, :],
                                        bias.unsqueeze(1).to_broadcast([128, 8, E]), ALU.add))
                for t in range(8):
                    done[0] += 1
                    eng.max(self.top[:, t, :], self.sel[:, t, :]).then_inc(self.step, 1)
                eng.wait_ge(self.step, done[0])
                for t in range(8):
                    done[0] += 1
                    eng.max_index(self.idx[:, t, :], self.top[:, t, :], self.sel[:, t, :]).then_inc(self.step, 1)
                eng.wait_ge(self.step, done[0])
                after(eng.tensor_copy(self.idf[:, :, :], self.idx[:, :, 0:2]))
                eng.wait_ge(consts, 16)
                iota = w("iota8").unsqueeze(1).unsqueeze(1).to_broadcast([128, 8, 2, E])
                after(eng.tensor_tensor(self.hot[:, :, :, :], iota,
                                        self.idf[:, :, :].unsqueeze(3).to_broadcast([128, 8, 2, E]), ALU.is_equal))
                after(eng.tensor_tensor(self.mask[:, :, :], self.hot[:, :, 0, :], self.hot[:, :, 1, :], ALU.add))
                after(eng.tensor_tensor(self.ss[:, :, :], self.s[:, :, :], self.mask[:, :, :], ALU.mult))
                after(eng.tensor_reduce(self.den[:, :], self.ss[:, :, :], AX_X, ALU.add))
                after(eng.tensor_scalar(self.rec[:, :], self.den[:, :], 1e-9, None, ALU.add))
                after(eng.reciprocal(self.rec[:, :], self.rec[:, :]))
                after(eng.tensor_scalar(self.flag[:, :], self.den[:, :], 1e-9, None, ALU.is_gt))
                after(eng.tensor_tensor(self.rec[:, :], self.rec[:, :], self.flag[:, :], ALU.mult))
                after(eng.tensor_scalar(self.flag[:, :], self.flag[:, :], -0.5, 0.5, ALU.mult, ALU.add))
                after(eng.tensor_tensor(self.comb[:, :, :], self.ss[:, :, :],
                                        self.rec[:, :].unsqueeze(2).to_broadcast([128, 8, E]), ALU.mult))
                after(eng.tensor_tensor(self.mask[:, :, :], self.mask[:, :, :],
                                        self.flag[:, :].unsqueeze(2).to_broadcast([128, 8, E]), ALU.mult))
                after(eng.tensor_tensor(self.comb[:, :, :], self.comb[:, :, :], self.mask[:, :, :], ALU.add))
                multiply(0)
                after(eng.tensor_copy(self.parts[:, :, 0:E], self.comb[:, :, :]))
                after(eng.tensor_tensor(self.rest[:, :, :], self.comb[:, :, :], self.parts[:, :, 0:E], ALU.subtract))
                after(eng.tensor_copy(self.parts[:, :, E:2 * E], self.rest[:, :, :]))
                after(eng.tensor_tensor(self.parts[:, :, 2 * E:3 * E], self.rest[:, :, :],
                                        self.parts[:, :, E:2 * E], ALU.subtract))
                multiply(1)
                multiply(2)
                eng.wait_ge(self.turned, 1)
                eng.tensor_copy(self.gT[:, :], PS[0:3 * E, bank, :].bitcast(BF16)).then_inc(self.gates, 1)

            def pe_turn(self, eng, bank):
                n = 1 + 8 + 8 + 7 + 5 + 1 + 4
                eng.wait_ge(self.step, n)
                turned = PS[0:3 * E, bank, :].bitcast(BF16)
                for t in range(8):
                    mm = eng.transpose(turned[:, t * 128:(t + 1) * 128], self.parts[:, t, :], w("identb"))
                mm.then_inc(self.turned, 1)

        loads = ("tokens", "routing", "shared", "experts", "consts", "weights", "picks")
        loaded = {name: sem("loaded_" + name) for name in loads}
        prep_act = sem("prep_act")
        prep_dve = sem("prep_dve")
        prep_pe = sem("prep_pe")
        prep_pool = sem("prep_pool")
        f_mwo = sem("prep_wout_sums")
        pads = sem("pads")
        absw = sb("absw", [128, D])
        asum = sb("asum", [128, 1])
        qscale = sb("qscale", [128, 1])
        qthr = sb("qthr", [128, 2])
        qneg = sb("qneg", [128, D])
        sgd = sb("sgd", [128, 1])
        ldec = sb("ldec", [128, 1])
        c2h = sb("c2h", [128, B])
        gate = sb("gate", [128, B])
        c2t = sb("c2t", [128, B])
        c2v = sb("c2v", [128, B])
        cb12 = sb("cb12", [128, 2])
        prep_c2h = sem("prep_c2h")
        ones = sb("ones_", [128, 128])
        cw = sb("cond_weights", [128, B, E])
        f_cond = sem("cond_weighted")
        eps = sb("eps", [128, 3])

        scopes.append(ExitStack())
        uc = sb("uc", [128, 2, 2, HALF])
        sz = sb("sz", [128, 2, 2, HALF])
        dt_ = sb("dt", [128, 2, 2, HALF])
        dtu = sb("dtu", [128, 2, 2, HALF])
        bc3 = sb("bc3", [96, 2, 2, HALF], BF16)
        th_ = sb("th", [128, 2, HALF])
        vu = sb("vu", [128, 2, HALF])
        dtr = sb("dtr", [BD, HALF])
        spv = sb("spv", [128, 2, HALF])
        spe = sb("spe", [128, 2, HALF])
        spl = sb("spl", [128, 2, HALF])
        spq = sb("spq", [128, 2, HALF])
        yz = sb("yz", [128, 2, HALF])
        cen = vu[:, 0, :]
        sq = th_[:, 0, :]
        sd = vu[:, 1, :]
        YB, CB, BB, AB, XB = (0, 1), (2, 3), 4, (5, 6), 7

        f_u, f_th, f_v, f_uc, f_zp, f_tz, f_z, f_bc, f_dtr, f_part, f_sub, f_dtp, f_spv, f_abs, f_e, f_ln, f_q, \
            f_dt, f_dtu, f_far = (sem("front_" + n) for n in (
                "u", "th", "v", "uc", "zp", "tz", "z", "bc", "dtr", "part", "sub", "dtp", "spv", "abs", "e", "ln", "q",
                "dt", "dtu", "far"))
        k_yz, k_o, k_sq, k_cen, k_var, k_rstd, k_n, k_fuse, k_x1 = (
            sem("back_" + n) for n in ("yz", "o", "sq", "cen", "var", "rstd", "n", "fuse", "x1"))

        def seqs(ap):
            return ap.rearrange("p (b t) -> p b t", t=T)

        def col(name, d, i):
            a = PACK1[name + "_" + "fb"[d]][0] + i
            return p1[:, a:a + 1]

        def pos(eng, s, v):
            if v > 0:
                eng.wait_ge(s, v)

        def turn_bank(cf, m):
            if cf != 0:
                return PS[:, XB, :]
            return PS[:, 1 if 4 <= m < 8 or m in (13, 15) or m >= 19 else 0, :]

        def side_pe(eng, m, cb, cf):
            X = turn_bank(cf, m)
            if cf is not None:
                th, d = divmod(cf, 2)
                tag = "fb"[d]
                if m < 2 * DC:
                    h, k = divmod(m, DC)
                    if m == 0 and cf == 0:
                        eng.wait_ge(m_in, 1)
                        eng.wait_ge(r0.scored, 1)
                        eng.wait_ge(prep_pool, POOL_FRONT)
                    elif m == 0:
                        eng.wait_ge(f_part, 6 * cf)
                        pos(eng, k_rstd, 2 * (cf - 2))
                        pos(eng, k_x1, (cf - 2) // 2)
                        eng.wait_ge(m_rev if d else m_in, th + 1)
                        eng.wait_ge(m_in, 2)
                    elif k == 0 and cf == 0:
                        eng.wait_ge(prep_act, PREP_ACTS)
                    elif k == 0:
                        eng.wait_ge(f_v, 2 * cf + 1)
                    mm = eng.matmul(X, w("taps_" + tag)[:, k * DI + h * 128:k * DI + (h + 1) * 128],
                                    uin[d][:, th * HB:(th + 1) * HB, k:k + T], start=(k == 0), stop=(k == DC - 1))
                    if k == DC - 1:
                        mm.then_inc(f_u, 1)
                elif m in (15, 17):
                    h = (m - 15) // 2
                    if cf == 0:
                        eng.wait_ge(f_spv, h + 1)
                    elif h:
                        eng.wait_ge(f_z, 2 * cf + 1)
                    else:
                        eng.wait_ge(f_spv, 2 * cf + 2)
                    eng.matmul(X, w("WinzT_" + tag)[:, h * 128:(h + 1) * 128],
                               uin[d][:, th * HB:(th + 1) * HB, DC - 1:], start=True, stop=True).then_inc(f_zp, 1)
                elif m in (9, 10, 19, 20):
                    which, h = (0, m - 9) if m < 11 else (1, m - 19)
                    name, width = (("WxBD_", BD), ("WxC_", 3 * NS))[which]
                    if m == 9:
                        eng.wait_ge(f_uc, 2 * cf + 2)
                    elif m == 19:
                        eng.wait_ge(f_z, 2 * cf + (2 if cf else 1))
                    mm = eng.matmul(X[0:width, :], w(name + tag)[:, h * width:(h + 1) * width], uc[:, cf % 2, h, :],
                                    start=(h == 0), stop=(h == 1), skip_group_check=True)
                    if h:
                        mm.then_inc(f_bc, 1)
                elif m in (11, 12, 21, 22):
                    which, i = (0, m - 11) if m < 13 else (1, m - 21)
                    eng.wait_ge(f_part, 6 * cf + 3 * which + i + 1)
                    if m == 11:
                        eng.wait_ge(f_dtr, cf + 1)
                    eng.matmul(X[0:96, :], w(("less_mid", "less_lo")[i])[0:96, :], bc3[:, cf % 2, which, :],
                               start=False, stop=True, skip_group_check=True).then_inc(f_sub, 1)
                elif m in (13, 14):
                    h = m - 13
                    if h == 0:
                        eng.wait_ge(f_dtr, cf + 1)
                    if h == 0 or cf == 0:
                        eng.wait_ge(f_part, 6 * cf + 3)
                    else:
                        eng.wait_ge(f_spv, 2 * cf + 1)
                    eng.matmul(X, w("WdtP_" + tag)[0:BD, h * 128:(h + 1) * 128], dtr[:, :], start=True,
                               stop=True).then_inc(f_dtp, 1)
            if cb is not None:
                if m in (23, 24):
                    h = m - 23
                    if h == 0:
                        eng.wait_ge(k_yz, 2 * cb + 2)
                        eng.wait_ge(prep_pool, POOL_BACK)
                        if cf is not None:
                            eng.wait_ge(f_part, 6 * cf + 6)
                        else:
                            eng.wait_ge(f_part, 24)
                            eng.wait_ge(k_rstd, 2 * cb)
                            eng.wait_ge(k_x1, cb // 2)
                    mm = eng.matmul(X, WoC[:, cb % 2, h, :], yz[:, h, :], start=(h == 0), stop=(h == 1))
                    if h:
                        mm.then_inc(k_o, 1)
                elif m == 25:
                    eng.wait_ge(k_sq, cb + 1)
                    eng.wait_ge(k_cen, cb + 1)
                    eng.matmul(X, meanw, sq[:, :], start=True, stop=True).then_inc(k_var, 1)
                elif m in (29, 30) and cb % 2 == 1:
                    i = m - 29
                    if i == 0:
                        eng.wait_ge(k_rstd, 2 * cb + 1)
                    eng.wait_ge(k_n, cb + i)
                    mm = eng.matmul(X, WfG[:, i, :], lnout[i][:, :], start=(i == 0), stop=(i == 1))
                    if i:
                        mm.then_inc(k_fuse, 1)

        def side_act(eng, m, cb, cf):
            X = turn_bank(cf, m)
            if cf is not None:
                d, par = cf % 2, cf % 2
                if m == 1 and cf:
                    eng.preload_act_table_set("exp_and_others")
                elif m in (3, 7):
                    h = (m - 3) // 4
                    eng.wait_ge(f_u, 2 * cf + h + 1)
                    pos(eng, f_z, 2 * cf - 1 + h)
                    eng.activation(th_[:, h, :], X, ACT.Tanh, scale=0.5, bias=cbh[:, d, h:h + 1]).then_inc(f_th, 1)
                    eng.activation(vu[:, h, :], X, ACT.Identity, bias=col("convb", d, h)).then_inc(f_v, 1)
                elif m in (15, 17):
                    h = (m - 15) // 2
                    eng.wait_ge(f_zp, 2 * cf + h + 1)
                    eng.wait_ge(f_uc, 2 * cf + h + 1)
                    eng.activation(th_[:, h, :], X, ACT.Tanh, scale=0.5).then_inc(f_tz, 1)
                    if cf == 0 and h:
                        eng.preload_act_table_set("natural_log_exp_and_others")
                elif m in (10, 20):
                    which = (m - 10) // 10
                    eng.wait_ge(f_bc, 2 * cf + which + 1)
                    if which == 0:
                        pos(eng, f_dtp, 2 * cf)
                        eng.activation(dtr[:, :], X[0:BD, :], ACT.Copy).then_inc(f_dtr, 1)
                    eng.activation(bc3[:, par, which, :], X[0:96, :], ACT.Copy).then_inc(f_part, 1)
                elif m in (11, 12, 21, 22):
                    which, i = (0, m - 11) if m < 13 else (1, m - 21)
                    eng.wait_ge(f_sub, 4 * cf + 2 * which + i + 1)
                    eng.activation(bc3[:, par, which, :], X[0:96, :], ACT.Copy).then_inc(f_part, 1)
                elif m in (13, 14):
                    h = m - 13
                    eng.wait_ge(f_dtp, 2 * cf + h + 1)
                    pos(eng, f_dt, 2 * cf)
                    eng.activation(spv[:, h, :], X, ACT.Identity, bias=col("bdt", d, h)).then_inc(f_spv, 1)
                elif m == 16:
                    eng.wait_ge(f_spv, 2 * cf + 2)
                    for h in range(2):
                        eng.activation(spl[:, h, :], spv[:, h, :], ACT.Abs).then_inc(f_abs, 1)
                if m in (17, 18):
                    h = m - 17
                    eng.wait_ge(f_abs, 2 * cf + h + 1)
                    eng.activation(spe[:, h, :], spl[:, h, :], ACT.Exp, scale=-1.0).then_inc(f_e, 1)
            if cf != 0 and m == (24 if cf is None else 18):
                eng.preload_act_table_set("natural_log_exp_and_others")
            if cf is not None and m in (20, 21):
                h = m - 20
                eng.wait_ge(f_e, 2 * cf + 2)
                eng.activation(spl[:, h, :], spe[:, h, :], ACT.Ln, bias=eps[:, 2:3]).then_inc(f_ln, 1)
            if cb is not None:
                if m == 24:
                    eng.wait_ge(k_o, cb + 1)
                    pos(eng, k_n, cb)
                    eng.activation(sq[:, :], X, ACT.Square).then_inc(k_sq, 1)
                    eng.activation(cen[:, :], X, ACT.Copy).then_inc(k_cen, 1)
                elif m == 25:
                    eng.wait_ge(k_var, cb + 1)
                    eng.activation(sd[:, :], X, ACT.Ln, bias=eps[:, 0:1]).then_inc(k_rstd, 1)
                elif m == 26:
                    eng.wait_ge(k_rstd, 2 * cb + 1)
                    eng.activation(sd[:, :], sd[:, :], ACT.Exp, scale=-0.5).then_inc(k_rstd, 1)

        def side_dve(eng, m, cb, cf):
            if cf is not None:
                par = cf % 2
                if m in (4, 8):
                    h = (m - 4) // 4
                    eng.wait_ge(f_th, 2 * cf + h + 1)
                    eng.wait_ge(f_v, 2 * cf + h + 1)
                    eng.scalar_tensor_tensor(uc[:, par, h, :], th_[:, h, :], 1.0, vu[:, h, :], ALU.add, ALU.mult)\
                       .then_inc(f_uc, 1)
                elif m in (16, 18):
                    h = (m - 16) // 2
                    eng.wait_ge(f_tz, 2 * cf + h + 1)
                    eng.scalar_tensor_tensor(sz[:, par, h, :], th_[:, h, :], 1.0, turn_bank(cf, m - 1), ALU.add,
                                             ALU.mult).then_inc(f_z, 1)
                elif m in (19, 20):
                    h = m - 19
                    eng.wait_ge(f_e, 2 * cf + h + 1)
                    eng.tensor_scalar(spq[:, h, :], spe[:, h, :], 1.0, None, ALU.add).then_inc(f_q, 1)
                    eng.wait_ge(f_q, 6 * cf + 2 * h + 1)
                    eng.scalar_tensor_tensor(spq[:, h, :], spq[:, h, :], 1.0, spe[:, h, :], ALU.subtract,
                                             ALU.subtract).then_inc(f_q, 1)
                elif 21 <= m < 27:
                    h, i = divmod(m - 21, 3)
                    if i == 0:
                        eng.wait_ge(f_ln, 2 * cf + h + 1)
                        eng.scalar_tensor_tensor(spl[:, h, :], spv[:, h, :], 0.0, spl[:, h, :], ALU.max, ALU.add)\
                           .then_inc(f_q, 1)
                    elif i == 1:
                        eng.wait_ge(f_q, 6 * cf + 5 + h)
                        eng.tensor_tensor(dt_[:, par, h, :], spl[:, h, :], spq[:, h, :], ALU.subtract)\
                           .then_inc(f_dt, 1)
                    else:
                        eng.wait_ge(f_dt, 2 * cf + h + 1)
                        eng.scalar_tensor_tensor(dtu[:, par, h, :], uc[:, par, h, :], 0.5, dt_[:, par, h, :],
                                                 ALU.mult, ALU.mult).then_inc(f_dtu, 1)
                        eng.wait_ge(f_dtu, 2 * cf + h + 1)
                        eng.memset(seqs(dt_[:, par, h, :])[:, :, 0:1], FAR).then_inc(f_far, 1)
            if cb is not None:
                d, th = cb % 2, cb // 2
                if m == 28:
                    eng.wait_ge(k_rstd, 2 * cb + 2)
                    dst = seqs(lnout[d][:, :])
                    eng.tensor_tensor(dst[:, :, ::-1] if d else dst, seqs(cen[:, :]), seqs(sd[:, :]), ALU.mult)\
                       .then_inc(k_n, 1)
                elif m == 31 and d == 1:
                    eng.wait_ge(k_fuse, th + 1)
                    dst = x1[:, :].rearrange("p (t b) -> p b t", b=B)[:, th * HB:(th + 1) * HB, :]
                    eng.scalar_tensor_tensor(dst, seqs(PS[:, XB, :]), bF[:, 0:1],
                                             seqs(xT[:, th * HALF:(th + 1) * HALF]), ALU.add, ALU.add)\
                       .then_inc(k_x1, 1)

        units = [(th, "shared", m) for th in range(2) for m in range(2)]
        units += [(th, "expert", e) for th in range(2) for e in range(E)]
        PREP = 6
        POOL_FRONT = 2 * 7 + 2
        POOL_BACK = POOL_FRONT + 2 * 3
        PREP_ACTS = 11
        scopes.append(ExitStack())
        r0 = Router("r0")
        m_a, m_b, m_act, m_mul, m_acc, m_in, m_rev = (sem("moe_" + n)
                                                      for n in ("a", "b", "act", "mul", "acc", "in", "rev"))
        mG = sb("mG", [128, 2, 512])
        mS = sb("mS", [128, 2, 512])
        first = {th: min(j for j, u in enumerate(units) if u[0] == th) for th in range(2)}
        last = {th: max(j for j, u in enumerate(units) if u[0] == th) for th in range(2)}
        SIDE_FROM = last[0] + 2
        PER_UNIT, EARLY = 3, 16

        def moe_side(side, eng, j):
            if j >= SIDE_FROM:
                lo = min((j - SIDE_FROM) * PER_UNIT, EARLY)
                for m in range(lo, min(lo + PER_UNIT, EARLY) if j < len(units) - 1 else SLOTS):
                    side(eng, m, None, 0)

        def load_inputs(eng):
            def load(dst, src, place, a, b, name):
                lo, hi = place[a][0], place[b][1]
                eng.dma_start(dst[:, lo:hi], src[:, lo:hi]).then_inc(loaded[name], 16)

            load(p0, pack0, PACK0, "xT", "decay", "tokens")
            load(cb, conb, CONB, "identb", "less_lo", "routing")
            load(p0, pack0, PACK0, "w1", "w2", "shared")
            load(cf, conf, CONF, "iota8", "gate_lift", "consts")
            load(p0, pack0, PACK0, "W1e", "W2e", "experts")
            load(p1, pack1, PACK1, "WinuT_f", "fcb", "weights")
            load(cb, conb, CONB, "pick46", "pick32", "picks")
            for name in loads:
                eng.wait_ge(loaded[name], 16)

        def moe_pool(eng):
            eng.memset(ones[:, :], 1.0).then_inc(pads, 1)
            eng.memset(eps[:, 0:1], 1e-5).then_inc(pads, 1)
            eng.memset(eps[:, 1:2], 63.5 * LN2).then_inc(pads, 1)
            eng.memset(eps[:, 2:3], 1.0).then_inc(pads, 1)
            for d in range(2):
                eng.memset(uin[d][:, :, 0:DC - 1], 0.0).then_inc(pads, 1)
            eng.memset(keep[:, :], 1.0).then_inc(pads, 1)
            eng.wait_ge(pads, 7)
            eng.memset(keep[:, :].rearrange("p (b t) -> p b t", t=PT)[:, :, 0:1], 0.0).then_inc(pads, 1)
            n = 0

            def did(ins):
                nonlocal n
                n += 1
                ins.then_inc(prep_pool, 1)

            def after(ins):
                did(ins)
                eng.wait_ge(prep_pool, n)

            eng.wait_ge(loaded["weights"], 16)
            eng.wait_ge(loaded["consts"], 16)
            for d, tag in enumerate("fb"):
                taps = w("taps_" + tag).rearrange("p (k i) -> p k i", i=DI)
                did(eng.tensor_tensor(taps, taps, w("WinuT_" + tag).unsqueeze(1).to_broadcast([128, DC, DI]),
                                      ALU.mult))
                for name in ("WxBD_", "WxC_"):
                    did(eng.tensor_scalar(w(name + tag), w(name + tag), 0.5, None, ALU.mult))
                for h in range(2):
                    did(eng.tensor_scalar(diagD[:, d, h, :], ident, col("Dp", d, h), 0.5, ALU.mult, ALU.mult))
                    did(eng.tensor_scalar(cbh[:, d, h:h + 1], col("convb", d, h), 0.5, None, ALU.mult))
            for q, name in enumerate(("cb1", "cb2")):
                did(eng.tensor_scalar(cb12[:, q:q + 1], w(name), 0.5, None, ALU.mult))
            for d, tag in enumerate("fb"):
                did(eng.tensor_scalar(WfG[:, d, :], w("WfT")[:, d * 128:(d + 1) * 128], col("ln_g", d, 0), None,
                                      ALU.mult))
                for h in range(2):
                    eng.wait_ge(prep_dve, 3)
                    did(eng.tensor_scalar(WoC[:, d, h, :], w("WoutT_" + tag)[:, h * 128:(h + 1) * 128], 0.5,
                                          mwo[:, d, h:h + 1], ALU.mult, ALU.add))
            for th in range(2):
                if th:
                    L = 3 * D
                    did(eng.tensor_scalar(WxLs[:, 0:L], w("WxL")[:, 0:L], LIFT / 2, None, ALU.mult))
                    did(eng.tensor_scalar(WxLs[:, L:], w("WxL")[:, L:], LIFT, None, ALU.mult))
                    did(eng.tensor_scalar(WhLs[:, 0:L], w("WhL")[:, 0:L], 0.5, None, ALU.mult))
                    after(eng.tensor_copy(WhLs[:, L:], w("WhL")[:, L:]))
                    after(eng.tensor_scalar(bLs[:, :], w("bL")[0:96, :], w("gate_lift")[0:96, :], None, ALU.mult))
                    after(eng.tensor_copy(bL3[:, :], bLs[:, :]))
                    after(eng.tensor_tensor(brest[:, :], bLs[:, :], bL3[:, :], ALU.subtract))
                    after(eng.tensor_copy(bmid[:, :], brest[:, :]))
                    after(eng.tensor_copy(bL3[32:64, :], bmid[32:64, :]))
                    after(eng.tensor_tensor(bL3[64:96, :], brest[64:96, :], bmid[64:96, :], ALU.subtract))
                    did(eng.tensor_scalar(H0[:, :], condT, LIFT, None, ALU.mult))
                    did(eng.tensor_scalar(w("WoT"), w("WoT"), w("ln_w"), None, ALU.mult))
                    did(eng.tensor_scalar(w("Wd"), w("Wd"), 0.5, None, ALU.mult))
                    did(eng.tensor_scalar(bias2[:, :], w("frb"), 2.0, None, ALU.mult))
                    for i in range(3):
                        left = WhLs if i == 0 else wrest
                        after(eng.tensor_copy(Wh3[:, i, :], left[:, :]))
                        if i < 2:
                            after(eng.tensor_tensor(wrest[:, :], left[:, :], Wh3[:, i, :], ALU.subtract))
                eng.wait_ge(m_in, th + 1)
                eng.tensor_copy(uin[1][:, th * HB:(th + 1) * HB, DC - 1:],
                                uin[0][:, th * HB:(th + 1) * HB, :DC - 2:-1]).then_inc(m_rev, 1)

        def moe_pe(eng):
            eng.wait_ge(pads, 1)
            eng.wait_ge(f_cond, 1)
            eng.matmul(PS[:, 0, 0:8 * E], ones[:, :], cw[:, :, :], start=True, stop=False,
                       skip_group_check=True)
            for t in range(8):
                mm = eng.matmul(PS[:, 0, t * E:(t + 1) * E], xT[:, t * 128:(t + 1) * 128], w("RWx"),
                                start=False, stop=True, skip_group_check=True)
            mm.then_inc(r0.logits, 1)

            def accumulate(j):
                th, kind, i = units[j]
                wt = w("w2" if kind == "shared" else "W2e")[:, i * 128:(i + 1) * 128]
                eng.wait_ge(m_mul, j + 1)
                eng.matmul(PS[:, 6 + th, :], wt, mS[:, j % 2, :], start=(j == first[th]),
                           stop=(j == last[th]), skip_group_check=True).then_inc(m_acc, 1)

            def prepare(j):
                if j == PREP:
                    eng.wait_ge(loaded["weights"], 16)
                    eng.wait_ge(loaded["consts"], 16)
                    eng.wait_ge(r0.gates, 1)
                    eng.matmul(PS[:, 1, 0:B], w("C1T"), condT, start=True, stop=True, skip_group_check=True)
                    for i in range(2):
                        mm = eng.matmul(PS[:, 1, 16:17], w("WfT")[:, i * 128:(i + 1) * 128], col("ln_b", i, 0),
                                        start=(i == 0), stop=(i == 1), skip_group_check=True)
                    mm.then_inc(prep_pe, 1)
                elif j == PREP + 2:
                    eng.wait_ge(prep_dve, 2)
                    eng.wait_ge(prep_act, 8)
                    eng.matmul(PS[:, 1, 24:25], ones[:, :], asum[:, :], start=True, stop=True,
                               skip_group_check=True)
                    eng.wait_ge(prep_c2h, 1)
                    eng.matmul(PS[:, 1, 8:8 + B], w("C2T"), c2h[:, :], start=True, stop=True,
                               skip_group_check=True).then_inc(prep_pe, 1)

            eng.wait_ge(loaded["shared"], 16)
            for j, (th, kind, i) in enumerate(units):
                cols = xT[:, th * HALF:(th + 1) * HALF]
                if (kind, th, i) == ("expert", 0, 0):
                    eng.wait_ge(loaded["experts"], 16)
                if j >= 2:
                    eng.wait_ge(m_act, j - 1)
                wt = w("w1" if kind == "shared" else "W1e")[:, i * 128:(i + 1) * 128]
                eng.matmul(PS[:, 2 + j % 2, :], wt, cols, start=True, stop=True).then_inc(m_a, 1)
                if (kind, th, i) == ("expert", 0, 0):
                    eng.wait_ge(loaded["routing"], 16)
                    r0.pe_turn(eng, 1)
                    eng.wait_ge(r0.gates, 1)
                if j >= 2:
                    eng.wait_ge(m_mul, j - 1)
                if kind == "shared":
                    eng.matmul(PS[:, 4 + j % 2, :], w("w3")[:, i * 128:(i + 1) * 128], cols,
                               start=True, stop=True).then_inc(m_b, 1)
                else:
                    eng.matmul(PS[:, 4 + j % 2, :], w("pick8")[0:3 * E, i * 128:(i + 1) * 128],
                               r0.gT[:, th * HALF:(th + 1) * HALF], start=True, stop=True).then_inc(m_b, 1)
                if j:
                    accumulate(j - 1)
                prepare(j)
                if j == len(units) - 1:
                    accumulate(j)
                moe_side(side_pe, eng, j)

        def moe_act(eng):
            def prepare(j):
                if j == PREP:
                    eng.wait_ge(loaded["weights"], 16)
                    eng.wait_ge(loaded["consts"], 16)
                    eng.activation(absw[:, :], w("WqT"), ACT.Abs).then_inc(prep_act, 1)
                    eng.preload_act_table_set("natural_log_exp_and_others")
                    for d, tag in enumerate("fb"):
                        eng.activation(Aneg[:, d, :], w("Alog_" + tag), ACT.Exp).then_inc(prep_act, 1)
                    eng.wait_ge(prep_dve, 1)
                    eng.activation(ldec[:, :], sgd[:, :], ACT.Ln).then_inc(prep_act, 1)
                    eng.wait_ge(prep_act, 5)
                    eng.activation(dscale[:, :], w("iotat"), ACT.Exp, scale=ldec[:, 0:1])\
                       .then_inc(prep_act, 1)
                elif j == PREP + 1:
                    eng.wait_ge(prep_pe, 1)
                    eng.wait_ge(prep_pool, POOL_FRONT)
                    eng.activation(c2t[:, :], PS[:, 1, 0:B], ACT.Tanh, scale=0.5, bias=cb12[:, 0:1])\
                       .then_inc(prep_act, 1)
                    eng.activation(c2v[:, :], PS[:, 1, 0:B], ACT.Identity, bias=w("cb1"))\
                       .then_inc(prep_act, 1)
                elif j == PREP + 3:
                    eng.wait_ge(prep_pe, 2)
                    eng.activation(gate[:, :], PS[:, 1, 8:8 + B], ACT.Tanh, scale=0.25, bias=cb12[:, 1:2])\
                       .then_inc(prep_act, 1)
                    eng.activation(bF[:, :], PS[:, 1, 16:17], ACT.Identity, bias=w("bfuse")).then_inc(prep_act, 1)
                    eng.activation(qscale[:, :], PS[:, 1, 24:25], ACT.Copy, scale=1.0 / (D * D))\
                       .then_inc(prep_act, 1)

            r0.act(eng, 0)
            eng.activation(sgd[:, :], w("decay"), ACT.Sigmoid).then_inc(prep_act, 1)
            eng.wait_ge(pads, 8)
            for j, (th, kind, i) in enumerate(units):
                eng.wait_ge(m_a, j + 1)
                if j >= 2:
                    eng.wait_ge(m_mul, j - 1)
                eng.activation(mG[:, j % 2, :], PS[:, 2 + j % 2, :],
                               ACT.Silu if kind == "shared" else ACT.Gelu).then_inc(m_act, 1)
                prepare(j)
                moe_side(side_act, eng, j)

        def moe_dve(eng):
            def multiply(j):
                eng.wait_ge(m_act, j + 1)
                eng.wait_ge(m_b, j + 1)
                if j >= 2:
                    eng.wait_ge(m_acc, j - 1)
                eng.tensor_tensor(mS[:, j % 2, :], mG[:, j % 2, :], PS[:, 4 + j % 2, :], ALU.mult)\
                   .then_inc(m_mul, 1)

            n = 0

            def did(ins):
                nonlocal n
                n += 1
                ins.then_inc(prep_dve, 1)

            def after(ins):
                did(ins)
                eng.wait_ge(prep_dve, n)

            def prepare():
                eng.wait_ge(prep_act, 2)
                did(eng.tensor_scalar(sgd[:, :], sgd[:, :], 1e-7, None, ALU.max))
                did(eng.tensor_reduce(asum[:, :], absw[:, :], AX_X, ALU.add))
                for d, tag in enumerate("fb"):
                    eng.tensor_reduce(mwo[:, d, :], w("WoutT_" + tag).rearrange("p (h e) -> p h e", e=D), AX_X,
                                      ALU.add).then_inc(f_mwo, 1)
                eng.wait_ge(f_mwo, 2)
                did(eng.tensor_scalar(mwo[:, :, :], mwo[:, :, :], -0.5 / D, None, ALU.mult))
                eng.wait_ge(prep_act, 4)
                did(eng.tensor_scalar(Aneg[:, :, :], Aneg[:, :, :], -1.0, None, ALU.mult))
                eng.wait_ge(prep_act, 6)
                after(eng.tensor_scalar(dinv[:, :], dscale[:, :], 1e-10, None, ALU.max))
                did(eng.reciprocal(dinv[:, :], dinv[:, :]))

            def prepare_gate():
                eng.wait_ge(prep_act, 8)
                eng.scalar_tensor_tensor(c2h[:, :], c2t[:, :], 1.0, c2v[:, :], ALU.add, ALU.mult)\
                   .then_inc(prep_c2h, 1)

            def prepare_rest():
                eng.wait_ge(prep_act, 11)
                did(eng.tensor_scalar(g1[:, :], gate[:, :], 0.5, 1.5, ALU.mult, ALU.add))
                after(eng.tensor_scalar(qscale[:, :], qscale[:, :], 1e-5, None, ALU.max))
                did(eng.tensor_scalar(qthr[:, 0:1], qscale[:, :], 0.5, None, ALU.mult))
                after(eng.tensor_scalar(qthr[:, 1:2], qscale[:, :], -0.5, None, ALU.mult))
                did(eng.tensor_scalar(wq[:, :], w("WqT"), qthr[:, 0:1], qscale[:, 0:1], ALU.is_gt, ALU.mult))
                after(eng.tensor_scalar(qneg[:, :], w("WqT"), qthr[:, 1:2], qscale[:, 0:1], ALU.is_lt, ALU.mult))
                did(eng.tensor_tensor(wq[:, :], wq[:, :], qneg[:, :], ALU.subtract))

            def done(th):
                eng.wait_ge(m_acc, last[th] + 1)
                eng.tensor_scalar(uin[0][:, th * HB:(th + 1) * HB, DC - 1:], seqs(PS[:, 6 + th, :]), 1.0 / 3.0,
                                  None, ALU.mult).then_inc(m_in, 1)

            eng.wait_ge(loaded["tokens"], 16)
            eng.tensor_tensor(cw[:, :, :], condT.unsqueeze(2).to_broadcast([128, B, E]),
                              w("RWt").unsqueeze(1).to_broadcast([128, B, E]), ALU.mult).then_inc(f_cond, 1)
            r0.dve(eng, w("rbias"), 1, multiply, loaded["consts"])
            for j in range(3, len(units)):
                multiply(j)
                if j == PREP:
                    eng.wait_ge(loaded["weights"], 16)
                    prepare()
                if j == PREP + 1:
                    prepare_gate()
                if j == PREP + 3:
                    prepare_rest()
                if j == last[0] + 1:
                    done(0)
                if j == last[1]:
                    done(1)
                moe_side(side_dve, eng, j)

        Bsb = sb("Bsb", [128, 2, HALF])
        dBu = sb("dBu", [128, 4, HALF])
        hst = sb("hst", [128, 4, HALF])
        hC = sb("hC", [128, 4, HALF])
        s_b, s_c, s_bc, s_da, s_dbu, s_h, s_hc, s_y = (
            sem("scan_" + n) for n in ("b", "c", "bcopy", "dA", "dBu", "h", "hC", "y"))
        PASSES, ALL = 4, 4 * NS

        def schedule(eng, step):
            for c in range(PASSES):
                for n in range(NS):
                    if c < PASSES - 1 or not QUIET <= n < QUIET + 2 * TURNS:
                        step(c, n, n % 2)
                    elif n == QUIET:
                        with eng.Fori(0, TURNS) as i:
                            step(c, i * 2 + QUIET, QUIET % 2)
                            step(c, i * 2 + (QUIET + 1), (QUIET + 1) % 2)

        def at_least(eng, s, base, rel):
            if not isinstance(rel, int):
                eng.wait_ge(s, rel + base)
            else:
                pos(eng, s, base + rel)

        def locate(c, n):
            if not isinstance(n, int):
                return c, n
            g = c * NS + n
            return (g // NS, g % NS) if g < ALL else None

        def neighbours(c):
            return (c - 1 if c else None), (c + 1 if c + 1 < PASSES else None)

        with nc.Block() as block:
            @block.sync
            def _(eng):
                load_inputs(eng)

            @block.tensor
            def _(eng):
                moe_pe(eng)

                def spread_b(c, n):
                    if locate(c, n) is None:
                        return
                    cc, nn = locate(c, n)
                    if isinstance(nn, int) and nn == 0:
                        eng.wait_ge(f_part, 6 * cc + 3)
                    at_least(eng, s_bc, c * NS, n)
                    eng.matmul(PS[:, BB, :], pick32[0:96, bass.ds(nn * 128, 128)], bc3[:, cc % 2, 0, :],
                               start=True, stop=True).then_inc(s_b, 1)

                def spread_c(c, n, slot):
                    if locate(c, n) is None:
                        return
                    cc, nn = locate(c, n)
                    if isinstance(nn, int) and nn == 0:
                        eng.wait_ge(f_part, 6 * cc + 6)
                    at_least(eng, s_hc, c * 2 * NS, n * 2 - 2)
                    eng.matmul(PS[:, CB[slot], :], pick32[0:96, bass.ds(nn * 128, 128)], bc3[:, cc % 2, 1, :],
                               start=True, stop=True).then_inc(s_c, 1)

                def add_y(c, n, slot):
                    for h in range(2):
                        at_least(eng, s_hc, c * 2 * NS, n * 2 + 1 + h)
                        eng.matmul(PS[:, YB[h], :], ident, hC[:, 2 * slot + h, :], start=False,
                                   stop=(isinstance(n, int) and n % NS == NS - 1),
                                   skip_group_check=True).then_inc(s_y, 1)

                def step(c, n, slot):
                    static = isinstance(n, int)
                    spread_b(c, n + 2)
                    if static:
                        side_pe(eng, n, *neighbours(c))
                    if static and n == 1:
                        pos(eng, k_yz, 2 * c)
                        for h in range(2):
                            eng.matmul(PS[:, YB[h], :], diagD[:, c % 2, h, :], uc[:, c % 2, h, :], start=True,
                                       stop=False, skip_group_check=True)
                    if not (static and c == 0 and n == 0):
                        add_y(c, n - 1, 1 - slot)
                    spread_c(c, n + 1, 1 - slot)

                eng.wait_ge(loaded["picks"], 16)
                spread_b(0, 0)
                spread_b(0, 1)
                spread_c(0, 0, 0)
                schedule(eng, step)
                add_y(PASSES - 1, NS - 1, 1)
                for m in range(SLOTS):
                    side_pe(eng, m, PASSES - 1, None)

            @block.scalar
            def _(eng):
                moe_act(eng)

                def copy_b(c, n, slot):
                    if locate(c, n) is None:
                        return
                    at_least(eng, s_b, c * NS, n + 1)
                    at_least(eng, s_dbu, c * 2 * NS, n * 2 - 2)
                    eng.activation(Bsb[:, slot, :], PS[:, BB, :], ACT.Copy).then_inc(s_bc, 1)

                def decay(c, n, h):
                    if locate(c, n) is None:
                        return
                    cc, nn = locate(c, n)
                    if isinstance(nn, int) and nn == 0:
                        eng.wait_ge(f_far, 2 * cc + h + 1)
                    at_least(eng, s_h, c * 2 * NS, n * 2 - 1 + h)
                    eng.activation(PS[:, AB[h], :], dt_[:, cc % 2, h, :], ACT.Exp,
                                   scale=Aneg[:, cc % 2, bass.ds(nn + h * NS, 1)]).then_inc(s_da, 1)

                def step(c, n, slot):
                    decay(c, n + 1, 0)
                    copy_b(c, n + 2, slot)
                    decay(c, n + 1, 1)
                    if isinstance(n, int):
                        side_act(eng, n, *neighbours(c))

                eng.wait_ge(prep_dve, 4)
                copy_b(0, 0, 0)
                decay(0, 0, 0)
                copy_b(0, 1, 1)
                decay(0, 0, 1)
                schedule(eng, step)
                for m in range(SLOTS):
                    side_act(eng, m, PASSES - 1, None)
                eng.preload_act_table_set("exp_and_others")

            @block.gpsimd
            def _(eng):
                moe_pool(eng)

                def step(c, n, slot):
                    at_least(eng, s_bc, c * NS, n + 1)
                    for h in range(2):
                        if isinstance(n, int) and n == 0:
                            eng.wait_ge(f_dtu, 2 * c + h + 1)
                        at_least(eng, s_h, c * 2 * NS, n * 2 - 3 + h)
                        eng.tensor_tensor(dBu[:, 2 * slot + h, :], dtu[:, c % 2, h, :], Bsb[:, slot, :], ALU.mult)\
                           .then_inc(s_dbu, 1)

                schedule(eng, step)

            @block.vector
            def _(eng):
                moe_dve(eng)

                def product(c, n, slot, h):
                    at_least(eng, s_h, c * 2 * NS, n * 2 + 1 + h)
                    at_least(eng, s_c, c * NS, n + 1)
                    at_least(eng, s_y, c * 2 * NS, n * 2 - 3 + h)
                    eng.tensor_tensor(hC[:, 2 * slot + h, :], hst[:, 2 * slot + h, :], PS[:, CB[slot], :],
                                      ALU.mult).then_inc(s_hc, 1)

                def scan(c, n, slot, h):
                    at_least(eng, s_da, c * 2 * NS, n * 2 + 1 + h)
                    at_least(eng, s_dbu, c * 2 * NS, n * 2 + 1 + h)
                    at_least(eng, s_hc, c * 2 * NS, n * 2 - 3 + h)
                    eng.tensor_tensor_scan(hst[:, 2 * slot + h, :], PS[:, AB[h], :], dBu[:, 2 * slot + h, :],
                                           0.0, ALU.mult, ALU.add).then_inc(s_h, 1)

                def gated(c):
                    eng.wait_ge(s_y, (c + 1) * 2 * NS)
                    for h in range(2):
                        eng.tensor_tensor(yz[:, h, :], sz[:, c % 2, h, :], PS[:, YB[h], :], ALU.mult)\
                           .then_inc(k_yz, 1)

                def step(c, n, slot):
                    static = isinstance(n, int)
                    scan(c, n, slot, 0)
                    if not (static and c == 0 and n == 0):
                        product(c, n - 1, 1 - slot, 1)
                    scan(c, n, slot, 1)
                    product(c, n, slot, 0)
                    if static and n == 0 and c:
                        gated(c - 1)
                    if static:
                        side_dve(eng, n, *neighbours(c))

                schedule(eng, step)
                product(PASSES - 1, NS - 1, 1, 1)
                gated(PASSES - 1)
                for m in range(SLOTS):
                    side_dve(eng, m, PASSES - 1, None)
        scopes.pop().close()

        scopes.pop().close()
        hr = sb("hr", [128, N])
        x2 = sb("x2", [128, N])
        Hs = sb("Hs", [128, N])
        hp = sb("hp", [128, 2, 2, B], F16)
        gt = sb("gt", [128, 2, 5, B])
        vv = sb("vv", [128, 2, B])
        oo = sb("oo", [128, B])
        tc = sb("tc", [128, B])
        r_mm, r_h, r_ffn, r_x2 = (sem("rnn_" + n) for n in ("mm", "h", "ffn", "x2"))
        l_mm, l_g, l_v, l_c, l_o, l_t, l_h, l_hi, l_lo = (
            sem("lstm_" + n) for n in ("mm", "g", "v", "c", "o", "t", "h", "hi", "lo"))
        RB, LB, FB = (0, 1), (2, 3), 4
        BR = 64 + G4
        LAG = 2
        l_cp = sem("lstm_cell_psum")

        def cell(c):
            return PS[:, LB[c % 2], G4 * CHB:G4 * CHB + B]


        TAIL, AFTER = 33, 33
        PAD = (DC - 1) * B
        x3 = sb("x3", [128, N])
        vp = sb("vp", [128, PAD + N])
        res = sb("res", [128, N])

        def pair(name, shape, dt=F32):
            return [sb(f"{name}{i}", shape, dt) for i in range(2)]

        rr, kk, kv, kvs, cum, st, yy, sq2, rb, at, cva, cvb, m46, m7 = (
            pair("tail_" + n, [128, PW]) for n in (
                "r", "k", "kv", "kvs", "cum", "state", "y", "sq", "rstd", "attn", "conv", "tap", "pass", "relu"))
        var, lf, rs, nt, nu = (pair("tail_" + n, [128, 1]) for n in ("var", "lf", "rs", "nt", "nu"))
        tl, s2, sel2, top8, ha, hb, hs, cb2_, rest2 = (
            pair("tail_" + n, [128, E]) for n in ("tl", "s2", "sel", "top", "ha", "hb", "hs", "comb", "rest"))
        idx8 = pair("tail_idx", [128, 8], U32)
        idf2, den2 = pair("tail_idf", [128, 2]), pair("tail_den", [128, 1])
        parts2 = pair("tail_parts", [128, 3 * E], BF16)
        gT2 = pair("tail_gT", [3 * E, PW], BF16)
        tg, m1_, m3_ = (pair("tail_" + n, [128, 2 * PW]) for n in ("tg", "gu", "gated"))
        t_kv, t_r, t_k, t_v, t_kvs, t_car, t_cum, t_st, t_yy, t_sq, t_ms, t_n, t_y0, t_o, t_rb, t_at, t_x3, t_vv = (
            sem("tail_" + n) for n in ("kv_mm", "r", "k", "kv", "kvs", "carry", "cum", "state", "y", "sq", "ms",
                                       "newton", "guess", "wo", "rb", "attn", "x3", "v"))
        t_lg, t_tl, t_rt, t_tr, t_gT, t_gu, t_tg, t_m1, t_m2, t_pick, t_m3, t_acc, t_cv, t_pass, t_sum, t_res = (
            sem("tail_" + n) for n in ("logits", "tl", "route", "turned", "gT", "gu", "tg", "m1", "m2", "pick", "m3",
                                       "acc", "conv", "pass", "sum", "res"))
        t_dn, t_pass46, v_pad = sem("tail_den"), sem("tail_pass46"), sem("v_pad")
        stored = sem("stored")
        AB4, AB5, AB6, AB7 = (PS[:, i, :] for i in (4, 5, 6, 7))
        NEWTON, ROUTE = 11, 13

        def tail_at(part, eng, t):
            for p in range(PIECES):
                k = t - PT * (p + 1)
                if 0 <= k < TAIL:
                    part(eng, p, k)

        def bt(ap):
            return ap.rearrange("p (b t) -> p b t", t=PT)

        def tb(ap):
            return ap.rearrange("p (t b) -> p b t", b=B)

        def tail_pe(eng, p, k):
            i, S = p % 2, slice(p * PW, (p + 1) * PW)
            V = slice(PAD + p * PW, PAD + (p + 1) * PW)
            if k in (0, 1, 2):
                if k == 0:
                    eng.wait_ge(l_h, (p + 1) * PT)
                    pos(eng, t_at, p)
                elif k == 1:
                    eng.wait_ge(t_r, p + 1)
                else:
                    eng.wait_ge(t_k, p + 1)
                eng.matmul(AB5[:, k * PW:(k + 1) * PW], w(("WrT", "WkT", "WvT")[k]), Hs[:, S], start=True, stop=True,
                           skip_group_check=True).then_inc(t_kv, 1)
            elif k == 9:
                eng.wait_ge(t_sq, p + 1)
                pos(eng, t_gT, p)
                eng.matmul(AB4[:, 128:129], sq2[i][:, :], meanw[:, 0:1], start=True, stop=True,
                           skip_group_check=True).then_inc(t_ms, 1)
            elif k == 13:
                eng.wait_ge(t_v, p + 1)
                eng.matmul(AB5[:, 0:PW], w("WoT"), yy[i][:, :], start=True, stop=True, skip_group_check=True)
            elif k == 14:
                eng.wait_ge(t_n, NEWTON * (p + 1))
                eng.matmul(AB5[:, PW:2 * PW], rs[i][:, :].to_broadcast([128, 128]), ident, start=True, stop=True,
                           skip_group_check=True).then_inc(t_o, 1)
            elif k == 17:
                eng.wait_ge(t_vv, p + 1)
                eng.matmul(AB4[:, 136:136 + E], vp[:, V], w("fWr"), start=True, stop=True, skip_group_check=True)\
                   .then_inc(t_lg, 1)
            elif 19 <= k < 23:
                q = k - 19
                pos(eng, t_res, p)
                wt = w("Wg" if q < 2 else "Wu")[:, q % 2 * 128:(q % 2 + 1) * 128]
                mm = eng.matmul(AB7[:, q * PW:(q + 1) * PW], wt, vp[:, V], start=True, stop=True, skip_group_check=True)
                if q == 3:
                    mm.then_inc(t_gu, 1)
            elif k == 25:
                eng.wait_ge(t_rt, ROUTE * (p + 1))
                eng.transpose(PS[0:3 * E, 4, 192:256].bitcast(BF16), parts2[i][:, :], w("identb")).then_inc(t_tr, 1)
            elif k == 26:
                eng.wait_ge(t_gT, p + 1)
                pos(eng, t_pass, p)
                for q, sel in enumerate((w("pickpair")[0:3 * E, 0:128], w("pickpair")[0:3 * E, 128:256],
                                         w("pick46")[0:3 * E, :], w("pick8")[0:3 * E, 7 * 128:8 * 128])):
                    mm = eng.matmul(AB6[:, q * PW:(q + 1) * PW], sel, gT2[i][:, :], start=True, stop=True,
                                    skip_group_check=True)
                mm.then_inc(t_pick, 1)
            elif k == 31:
                eng.wait_ge(t_m3, p + 1)
                for q in range(2):
                    mm = eng.matmul(AB7[:, 0:PW], w("Wd")[:, q * 128:(q + 1) * 128], m3_[i][:, q * PW:(q + 1) * PW],
                                    start=(q == 0), stop=(q == 1), skip_group_check=True)
                mm.then_inc(t_acc, 1)

        def tail_act(eng, p, k):
            i = p % 2
            if k == 0:
                eng.wait_ge(t_kv, 3 * p + 1)
                eng.activation(rr[i][:, :], AB5[:, 0:PW], ACT.Tanh, scale=0.5 / LIFT).then_inc(t_r, 1)
            elif k == 1:
                eng.wait_ge(t_kv, 3 * p + 2)
                eng.activation(kk[i][:, :], AB5[:, PW:2 * PW], ACT.Copy, scale=1.0 / (LIFT * LIFT)).then_inc(t_k, 1)
            elif k == 8:
                eng.wait_ge(t_yy, p + 1)
                eng.activation(sq2[i][:, :], yy[i][:, :], ACT.Square).then_inc(t_sq, 1)
            elif k == 11:
                eng.wait_ge(t_n, NEWTON * p + 2)
                eng.activation(rs[i][:, :], lf[i][:, :], ACT.Exp, scale=-0.5 * LN2 / 2 ** 23, bias=eps[:, 1:2])\
                   .then_inc(t_y0, 1)
            elif k == 14:
                eng.wait_ge(t_o, p + 1)
                eng.activation(rb[i][:, :], AB5[:, PW:2 * PW], ACT.Copy).then_inc(t_rb, 1)
            elif k == 17:
                eng.wait_ge(t_lg, p + 1)
                eng.activation(tl[i][:, :], AB4[:, 136:136 + E], ACT.Tanh, scale=0.5).then_inc(t_tl, 1)
            elif k == 22:
                eng.wait_ge(t_gu, p + 1)
                eng.activation(tg[i][:, :], AB7[:, 0:2 * PW], ACT.Tanh, scale=0.5).then_inc(t_tg, 1)
            elif k == 25:
                eng.wait_ge(t_tr, p + 1)
                eng.activation(gT2[i][:, :], PS[0:3 * E, 4, 192:256].bitcast(BF16), ACT.Copy).then_inc(t_gT, 1)

        def tail_dve(eng, p, k):
            tail_dve_slot(eng, p, k)
            if p == PIECES - 1:
                tail_chain(eng, p, k)

        def tail_dve_slot(eng, p, k):
            i = p % 2
            V = slice(PAD + p * PW, PAD + (p + 1) * PW)

            def newton(n, ins):
                ins.then_inc(t_n, 1)
                eng.wait_ge(t_n, NEWTON * p + n)

            def route(n, ins):
                ins.then_inc(t_rt, 1)
                eng.wait_ge(t_rt, ROUTE * p + n)

            if k == 2:
                eng.wait_ge(t_kv, 3 * p + 3)
                eng.wait_ge(t_k, p + 1)
                eng.tensor_tensor(kv[i][:, :], kk[i][:, :], AB5[:, 2 * PW:3 * PW], ALU.mult).then_inc(t_v, 1)
            elif k == 4:
                eng.wait_ge(t_kvs, p + 1)
                if p:
                    eng.tensor_tensor(bt(kvs[i][:, :])[:, :, 0:1], bt(kvs[i][:, :])[:, :, 0:1],
                                      bt(cum[1 - i][:, :])[:, :, PT - 1:PT], ALU.add).then_inc(t_car, 1)
            elif k == 5:
                pos(eng, t_car, p)
                eng.tensor_tensor_scan(cum[i][:, :], keep[:, :], kvs[i][:, :], 0.0, ALU.mult, ALU.add)\
                   .then_inc(t_cum, 1)
            elif k == 7:
                eng.wait_ge(t_st, p + 1)
                eng.scalar_tensor_tensor(tb(yy[i][:, :]), tb(rr[i][:, :]), 1.0, bt(st[i][:, :]), ALU.add, ALU.mult)\
                   .then_inc(t_yy, 1)
            elif k == 10:
                eng.wait_ge(t_ms, p + 1)
                newton(1, eng.tensor_scalar(var[i][:, :], AB4[:, 128:129], 4e-6, None, ALU.add))
                newton(2, eng.tensor_copy(lf[i][:, :], var[i][:, :].bitcast(U32)))
            elif k in (11, 12, 13):
                n = 3 * (k - 11) + 2
                eng.wait_ge(t_y0, p + 1)
                newton(n + 1, eng.scalar_tensor_tensor(nt[i][:, :], rs[i][:, :], var[i][:, 0:1], rs[i][:, :],
                                                       ALU.mult, ALU.mult))
                newton(n + 2, eng.tensor_scalar(nu[i][:, :], nt[i][:, :], -0.5, 1.5, ALU.mult, ALU.add))
                newton(n + 3, eng.tensor_tensor(rs[i][:, :], rs[i][:, :], nu[i][:, :], ALU.mult))
            elif k == 14:
                eng.wait_ge(t_rb, p + 1)
                eng.tensor_tensor(at[i][:, :], rb[i][:, :], AB5[:, 0:PW], ALU.mult).then_inc(t_at, 1)
            elif k == 17:
                eng.wait_ge(t_tl, p + 1)
                route(1, eng.tensor_scalar(s2[i][:, :], tl[i][:, :], 1.0, None, ALU.add))
                route(2, eng.tensor_tensor(sel2[i][:, :], s2[i][:, :], bias2[:, :], ALU.add))
            elif k == 18:
                route(3, eng.max(top8[i][:, :], sel2[i][:, :]))
                route(4, eng.max_index(idx8[i][:, :], top8[i][:, :], sel2[i][:, :]))
            elif k == 19:
                route(5, eng.tensor_copy(idf2[i][:, :], idx8[i][:, 0:2]))
                for h, dst in enumerate((ha[i], hb[i])):
                    route(6 + h, eng.scalar_tensor_tensor(dst[:, :], w("iota8"), idf2[i][:, h:h + 1], s2[i][:, :],
                                                          ALU.is_equal, ALU.mult))
            elif k == 20:
                route(8, eng.tensor_tensor(hs[i][:, :], ha[i][:, :], hb[i][:, :], ALU.add))
                route(9, eng.tensor_reduce(den2[i][:, :], hs[i][:, :], AX_X, ALU.add))
                eng.tensor_scalar(den2[i][:, :], den2[i][:, :], 2e-9, None, ALU.add).then_inc(t_dn, 1)
            elif k == 21:
                eng.wait_ge(t_dn, 3 * p + 1)
                eng.reciprocal(den2[i][:, :], den2[i][:, :]).then_inc(t_dn, 1)
                eng.wait_ge(t_dn, 3 * p + 2)
                eng.tensor_scalar(cb2_[i][:, :], hs[i][:, :], den2[i][:, 0:1], None, ALU.mult).then_inc(t_dn, 1)
                eng.wait_ge(t_dn, 3 * p + 3)
                route(10, eng.tensor_copy(parts2[i][:, 0:E], cb2_[i][:, :]))
            elif k == 22:
                route(11, eng.tensor_tensor(rest2[i][:, :], cb2_[i][:, :], parts2[i][:, 0:E], ALU.subtract))
                route(12, eng.tensor_copy(parts2[i][:, E:2 * E], rest2[i][:, :]))
                route(13, eng.tensor_tensor(parts2[i][:, 2 * E:], rest2[i][:, :], parts2[i][:, E:2 * E],
                                            ALU.subtract))
            elif k == 24:
                eng.wait_ge(t_tg, p + 1)
                eng.scalar_tensor_tensor(m1_[i][:, :], tg[i][:, :], 1.0, AB7[:, 0:2 * PW], ALU.add, ALU.mult)\
                   .then_inc(t_m1, 1)
            elif k == 27:
                eng.wait_ge(t_m1, p + 1)
                eng.tensor_tensor(m1_[i][:, :], m1_[i][:, :], AB7[:, 2 * PW:], ALU.mult).then_inc(t_m2, 1)
            elif k == 30:
                eng.wait_ge(t_m2, p + 1)
                eng.wait_ge(t_pick, p + 1)
                eng.tensor_tensor(m3_[i][:, :], m1_[i][:, :], AB6[:, 0:2 * PW], ALU.mult).then_inc(t_m3, 1)
            elif k == 31:
                eng.tensor_tensor(m46[i][:, :], vp[:, V], AB6[:, 2 * PW:3 * PW], ALU.mult).then_inc(t_pass46, 1)
                eng.scalar_tensor_tensor(m7[i][:, :], vp[:, V], 0.0, AB6[:, 3 * PW:], ALU.max, ALU.mult)\
                   .then_inc(t_pass, 1)
            elif k == 32:
                eng.wait_ge(t_sum, 2 * p + 2)
                eng.wait_ge(t_acc, p + 1)
                eng.tensor_tensor(res[:, p * PW:(p + 1) * PW], cva[i][:, :], AB7[:, 0:PW], ALU.add).then_inc(t_res, 1)

        def tail_chain(eng, p, k):
            i, S = p % 2, slice(p * PW, (p + 1) * PW)
            V = slice(PAD + p * PW, PAD + (p + 1) * PW)
            ts = slice(p * PT, (p + 1) * PT)
            if k == 3:
                eng.wait_ge(t_v, p + 1)
                eng.tensor_tensor(bt(kvs[i][:, :]), tb(kv[i][:, :]),
                                  dinv[:, ts].unsqueeze(1).to_broadcast([128, B, PT]), ALU.mult).then_inc(t_kvs, 1)
            elif k == 6:
                eng.wait_ge(t_cum, p + 1)
                eng.tensor_tensor(bt(st[i][:, :]), bt(cum[i][:, :]),
                                  dscale[:, ts].unsqueeze(1).to_broadcast([128, B, PT]), ALU.mult).then_inc(t_st, 1)
            elif k == 15:
                eng.wait_ge(t_at, p + 1)
                eng.tensor_tensor(x3[:, S], x2[:, S], at[i][:, :], ALU.add).then_inc(t_x3, 1)
                eng.wait_ge(t_x3, p + 1)
                eng.tensor_tensor(vp[:, V].rearrange("p (t b) -> p t b", b=B),
                                  x3[:, S].rearrange("p (t b) -> p t b", b=B),
                                  g1[:, :].unsqueeze(1).to_broadcast([128, PT, B]), ALU.mult).then_inc(t_vv, 1)
            elif k == 31:
                eng.wait_ge(t_cv, 2 * DC * (p + 1))
                eng.wait_ge(t_pass46, p + 1)
                eng.tensor_tensor(cva[i][:, :], cva[i][:, :], m46[i][:, :], ALU.add).then_inc(t_sum, 1)
                eng.wait_ge(t_pass, p + 1)
                eng.wait_ge(t_sum, 2 * p + 1)
                eng.tensor_tensor(cva[i][:, :], cva[i][:, :], m7[i][:, :], ALU.add).then_inc(t_sum, 1)

        def tail_pool(eng, p, k):
            i, S = p % 2, slice(p * PW, (p + 1) * PW)
            a0 = PACK1["fcw"][0]
            if p == 0 and k == 1:
                eng.memset(vp[:, 0:PAD], 0.0).then_inc(v_pad, 1)
            if p < PIECES - 1:
                tail_chain(eng, p, k)
            if k == 17:
                n = 8 * p

                def did(ins):
                    nonlocal n
                    n += 1
                    ins.then_inc(t_cv, 1)
                    eng.wait_ge(t_cv, n)

                def tap(dst, q, second):
                    src, by = vp[:, p * PW + q * B:(p + 1) * PW + q * B], p1[:, a0 + q:a0 + q + 1]
                    if second is None:
                        return eng.tensor_scalar(dst[i][:, :], src, by, None, ALU.mult)
                    return eng.tensor_scalar(dst[i][:, :], src, by, second, ALU.mult, ALU.add)

                eng.wait_ge(v_pad, 1)
                eng.wait_ge(t_vv, p + 1)
                did(tap(cva, 0, w("fcb")))
                for q in range(1, DC):
                    did(tap(cvb, q, None))
                    did(eng.tensor_tensor(cva[i][:, :], cva[i][:, :], cvb[i][:, :], ALU.add))
                did(eng.tensor_tensor(cva[i][:, :], cva[i][:, :], x3[:, S], ALU.add))

        with nc.Block() as block:
            @block.tensor
            def _(eng):
                def preload_rnn(c):
                    if c >= 2:
                        eng.wait_ge(r_h, (c - 1) * CH)
                    eng.matmul(PS[:, RB[c % 2], 0:CHB], w("WxR"), x1[:, c * CHB:(c + 1) * CHB], start=True,
                               stop=False, skip_group_check=True)

                def rnn_step(t):
                    c, s = divmod(t, CH)
                    if t:
                        eng.wait_ge(r_h, t)
                    eng.matmul(PS[:, RB[c % 2], s * B:(s + 1) * B], w("WhR"),
                               hr[:, (t - 1) * B:t * B] if t else condT, start=False, stop=True,
                               skip_group_check=True).then_inc(r_mm, 1)

                def ternary(c):
                    eng.wait_ge(r_h, (c + 1) * CH)
                    if c:
                        eng.wait_ge(r_x2, c)
                    eng.matmul(PS[:, FB, 0:CHB], wq[:, :], hr[:, c * CHB:(c + 1) * CHB], start=True, stop=True)\
                       .then_inc(r_ffn, 1)

                def gates(c):
                    return PS[:, LB[c % 2], 0:G4 * CHB]

                def preload_bias(c):
                    eng.wait_ge(r_x2, c + 1)
                    if c >= 2:
                        eng.wait_ge(l_g, (c - 1) * CH)
                    eng.matmul(gates(c), bL3[0:BR, :], w("gate_rows")[0:BR, :], start=True, stop=False,
                               skip_group_check=True)

                def preload_gate(c, g):
                    eng.matmul(gates(c).rearrange("p (s g b) -> p s g b", g=G4, b=B)[:, :, g, :],
                               WxLs[:, g * 128:(g + 1) * 128],
                               x2[:, c * CHB:(c + 1) * CHB].rearrange("p (s b) -> p s b", b=B), start=False,
                               stop=False, skip_group_check=True)

                def lstm_step(t):
                    c, s = divmod(t, CH)

                    def into(g):
                        return gates(c)[:, (s * G4 + g) * B:(s * G4 + g + 1) * B]

                    if t == 0:
                        for g in range(G4):
                            mm = eng.matmul(into(g), WhLs[:, g * 128:(g + 1) * 128], H0[:, :], start=False,
                                            stop=True, skip_group_check=True)
                    else:
                        for part, ready, weights in ((0, l_hi, (0, 1, 2)), (1, l_lo, (0, 1))):
                            eng.wait_ge(ready, t)
                            for i in weights:
                                for g in range(G4):
                                    mm = eng.matmul(into(g), Wh3[:, i, g * 128:(g + 1) * 128],
                                                    hp[:, (t - 1) % 2, part, :], start=False, stop=True,
                                                    skip_group_check=True)
                    mm.then_inc(l_mm, 1)

                preload_rnn(0)
                for c in range(NCH + LAG):
                    for s in range(CH):
                        if c >= LAG:
                            lstm_step((c - LAG) * CH + s)
                        if c < NCH:
                            rnn_step(c * CH + s)
                        if 1 <= c <= NCH:
                            if s == 0:
                                ternary(c - 1)
                            elif s == 1:
                                preload_bias(c - 1)
                            elif s <= G4 + 1:
                                preload_gate(c - 1, s - 2)
                        if s == CH - 2 and c + 1 < NCH:
                            preload_rnn(c + 1)
                        if c >= LAG:
                            tail_at(tail_pe, eng, (c - LAG) * CH + s)
                for t in range(T, T + AFTER):
                    tail_at(tail_pe, eng, t)

            @block.scalar
            def _(eng):
                for c in range(NCH + LAG):
                    for s in range(CH):
                        if c >= LAG:
                            t = (c - LAG) * CH + s
                            eng.wait_ge(l_mm, t + 1)
                            if t >= 2:
                                eng.wait_ge(l_h, t - 1)
                            eng.activation(gt[:, t % 2, 0:G4, :],
                                           PS[:, LB[c % 2], s * G4 * B:(s + 1) * G4 * B]
                                           .rearrange("p (g b) -> p g b", b=B), ACT.Tanh, scale=1.0 / LIFT)\
                               .then_inc(l_g, 1)
                        if c < NCH:
                            t = c * CH + s
                            eng.wait_ge(r_mm, t + 1)
                            eng.activation(hr[:, t * B:(t + 1) * B], PS[:, RB[c % 2], s * B:(s + 1) * B], ACT.Tanh,
                                           bias=w("bR")).then_inc(r_h, 1)
                        if c >= LAG:
                            t = (c - LAG) * CH + s
                            eng.wait_ge(l_cp, t + 1)
                            eng.activation(tc[:, :], cell(c), ACT.Tanh, scale=0.5).then_inc(l_t, 1)
                            tail_at(tail_act, eng, t)
                for t in range(T, T + AFTER):
                    tail_at(tail_act, eng, t)

            @block.vector
            def _(eng):
                eng.memset(gt[:, 0, 4, :], 0.0).then_inc(l_c, 1)
                for c in range(NCH + LAG):
                    for s in range(CH):
                        if c >= LAG:
                            t = (c - LAG) * CH + s
                            cur, nxt = gt[:, t % 2, :, :], gt[:, (t + 1) % 2, :, :]
                            eng.wait_ge(l_g, t + 1)
                            eng.wait_ge(l_c, t + 1)
                            eng.scalar_tensor_tensor(vv[:, :, :], cur[:, 0:2, :], 1.0, cur[:, 3:5, :],
                                                     ALU.add, ALU.mult).then_inc(l_v, 1)
                            eng.wait_ge(l_v, t + 1)
                            eng.scalar_tensor_tensor(cell(c), vv[:, 1, :], 0.5, vv[:, 0, :],
                                                     ALU.mult, ALU.add).then_inc(l_cp, 1)
                            eng.scalar_tensor_tensor(nxt[:, 4, :], vv[:, 1, :], 0.5, vv[:, 0, :],
                                                     ALU.mult, ALU.add).then_inc(l_c, 1)
                            eng.tensor_scalar(oo[:, :], cur[:, 2, :], 1.0, LIFT / 2, ALU.add, ALU.mult)\
                               .then_inc(l_o, 1)
                            eng.wait_ge(l_o, t + 1)
                            eng.wait_ge(l_t, t + 1)
                            eng.tensor_tensor(hp[:, t % 2, 0, :], oo[:, :], tc[:, :], ALU.mult).then_inc(l_hi, 1)
                            eng.tensor_tensor(Hs[:, t * B:(t + 1) * B], oo[:, :], tc[:, :], ALU.mult)\
                               .then_inc(l_h, 1)
                            eng.wait_ge(l_hi, t + 1)
                            eng.wait_ge(l_h, t + 1)
                            eng.tensor_tensor(hp[:, t % 2, 1, :], Hs[:, t * B:(t + 1) * B], hp[:, t % 2, 0, :],
                                              ALU.subtract).then_inc(l_lo, 1)
                        if s == 0 and 1 <= c <= NCH:
                            span = slice((c - 1) * CHB, c * CHB)
                            eng.wait_ge(r_ffn, c)
                            eng.tensor_tensor(x2[:, span], x1[:, span], PS[:, FB, 0:CHB], ALU.add).then_inc(r_x2, 1)
                        if c >= LAG:
                            tail_at(tail_dve, eng, (c - LAG) * CH + s)
                for t in range(T, T + AFTER):
                    tail_at(tail_dve, eng, t)

            @block.gpsimd
            def _(eng):
                for t in range(T + AFTER):
                    tail_at(tail_pool, eng, t)

            @block.sync
            def _(eng):
                for p in range(PIECES):
                    eng.wait_ge(t_res, p + 1)
                    eng.dma_start(out[:, p * PW:(p + 1) * PW], res[:, p * PW:(p + 1) * PW]).then_inc(stored, 16)
                eng.wait_ge(stored, 16 * PIECES)


def kernel(**inputs):
    import numpy as np
    import ml_dtypes
    import concourse.bacc as bacc
    from concourse.bass_utils import run_bass_kernel_spmd

    x = {k: np.asarray(v) for k, v in inputs.items()}

    def packed(place, width, parts):
        a = np.zeros((128, width), np.float32)
        for name, v in parts.items():
            lo, hi = place[name]
            v = np.asarray(v)
            v = v.reshape(v.shape[0], -1)
            a[:v.shape[0], lo:lo + v.shape[1]] = v
        return a

    def blocks(m, rows=128):
        return m.reshape(-1, rows, m.shape[1]).transpose(1, 0, 2)

    def spaced(m):
        a = np.zeros((96, m.shape[1]), np.float32)
        for i in range(0, 96, 32):
            a[i:i + G4] = m
        return a

    def row128(v):
        return np.broadcast_to(v[None, :], (128, v.shape[0]))

    m0 = {
        "xT": x["x"].reshape(N, D).T, "condT": x["cond_1024"].T,
        "RWx": x["L0_cond_router_W"][0:D], "RWt": x["L0_cond_router_W"][D:], "rbias": row128(x["L0_cond_router_bias"]),
        "decay": x["L1_attn_decay"][:, None],
        "w1": x["L0_cond_w1"], "w3": x["L0_cond_w3"], "w2": blocks(x["L0_cond_w2"]),
        "W1e": x["L0_cond_W1e"].transpose(1, 0, 2), "W2e": x["L0_cond_W2e"].transpose(1, 0, 2),
    }
    m1 = {}
    for t in "fb":
        g = {k[len("L0_attn_"):-2]: v for k, v in x.items() if k.startswith("L0_attn_") and k.endswith("_" + t)}
        wx = g["Wx"].T
        three = lambda m: np.concatenate([m, m, m], axis=1)
        m1.update({k + "_" + t: v for k, v in {
            "WinuT": g["Win"][0:DI].T, "WinzT": g["Win"][DI:].T, "taps": row128(g["convw"].T.reshape(-1)),
            "WxBD": blocks(np.concatenate([three(wx[:, DR:DR + NS]), wx[:, 0:DR]], axis=1)),
            "WxC": blocks(three(wx[:, DR + NS:])),
            "WdtP": np.concatenate([np.zeros((3 * NS, DI), np.float32), g["Wdt"].T]), "WoutT": blocks(g["Wout"].T),
            "Alog": blocks(g["Alog"]), "convb": blocks(g["convb"][:, None]),
            "bdt": blocks(g["bdt"][:, None]), "Dp": blocks(g["Dp"][:, None]),
            "ln_g": g["ln_g"][:, None], "ln_b": g["ln_b"][:, None]}.items()})
    pairs = lambda m: m.transpose(1, 0, 2)
    m1.update({
        "WfT": blocks(x["L0_attn_Wfuse"].T), "bfuse": x["L0_attn_bfuse"][:, None],
        "WxR": x["L0_cond2_Wx"], "WhR": x["L0_cond2_Wh"], "bR": x["L0_cond2_b"][:, None],
        "WqT": x["L0_ffn_weight"].T, "WxL": x["L1_cond_Wx"], "WhL": x["L1_cond_Wh"],
        "bL": spaced(x["L1_cond_b"].reshape(G4, D)),
        "WrT": x["L1_attn_Wr"].T, "WkT": x["L1_attn_Wk"].T, "WvT": x["L1_attn_Wv"].T, "WoT": x["L1_attn_Wo"].T,
        "ln_w": x["L1_attn_ln_w"][:, None],
        "C1T": x["L1_cond2_W1"].T, "C2T": x["L1_cond2_W2"].T, "cb1": x["L1_cond2_b1"][:, None],
        "cb2": x["L1_cond2_b2"][:, None], "fWr": x["L1_ffn_Wr"], "frb": row128(x["L1_ffn_router_bias"]),
        "Wg": pairs(x["L1_ffn_Wg"]), "Wu": pairs(x["L1_ffn_Wu"]),
        "Wd": blocks(x["L1_ffn_Wd"].reshape(256, D)), "fcw": x["L1_ffn_conv_w"].reshape(DC, D).T,
        "fcb": x["L1_ffn_conv_b"][:, None],
    })
    eye = np.eye(128, dtype=np.float32)
    gate_rows = np.broadcast_to(np.eye(G4, dtype=np.float32)[:, None, :, None], (G4, CH, G4, B))
    mf = {"ident": eye, "mean": np.full((128, 128), 1.0 / 128, np.float32), 
          "iota8": row128(np.arange(E, dtype=np.float32)), "iotat": row128(np.arange(T, dtype=np.float32)),
          "gate_lift": spaced(np.array([[LIFT / 2]] * 3 + [[LIFT]], np.float32))}
    pick32 = np.zeros((96, NS, 128), np.float32)
    for n in range(NS):
        pick32[[n, NS + n, 2 * NS + n], n, :] = 1
    less = [-np.eye(3 * NS, dtype=np.float32) * (np.arange(3 * NS) >= i * NS) for i in (1, 2)]
    pick8 = np.zeros((3 * E, E, 128), np.float32)
    for e in range(E):
        pick8[[e, E + e, 2 * E + e], e, :] = 1
    pickpair = np.concatenate([pick8[:, e, 0:64] for e in range(4)], axis=1)
    mb = {"identb": eye, "pick32": pick32, "pick8": pick8, "pick46": pick8[:, 4] + pick8[:, 6], "pickpair": pickpair,
          "less_mid": less[0], "less_lo": less[1], "gate_rows": spaced(gate_rows.reshape(G4, -1))}
    arrays = {
        "pack0": packed(PACK0, W0, m0), "pack1": packed(PACK1, W1, m1), "conf": packed(CONF, WF, mf),
        "conb": packed(CONB, WB, mb).astype(ml_dtypes.bfloat16),
    }
    nc = bacc.Bacc("TRN2", target_bir_lowering=False, num_devices=1)
    args = [nc.dram_tensor(k, v.shape, mybir.dt.from_np(v.dtype), kind="ExternalInput").ap() for k, v in arrays.items()]
    out = nc.dram_tensor("y", (128, N), F32, kind="ExternalOutput").ap()
    build(nc, *args, out)
    r = run_bass_kernel_spmd(nc, [arrays], core_ids=[0])
    y = r.results[0]["y"]
    return np.ascontiguousarray(np.asarray(y).reshape(D, T, B).transpose(2, 1, 0))
```
